# Optimizing a Trainium2 kernel written in Bass

```python
import numpy as np
import jax
import jax.numpy as jnp

def _softmax(x, axis=-1):
    return jax.nn.softmax(x, axis=axis)

def _gelu(x):
    return jax.nn.gelu(x, approximate=True)

def _silu(x):
    return jax.nn.silu(x)

def _sigmoid(x):
    return jax.nn.sigmoid(x)

def _layernorm(x, axis=-1, eps=1e-05):
    m = jnp.mean(x, axis=axis, keepdims=True)
    v = jnp.var(x, axis=axis, keepdims=True)
    return (x - m) / jnp.sqrt(v + eps)

def _scatter_add(tgt, idx, src, axis=0):
    return tgt.at[idx].add(src)

def _segment_sum(src, seg, n):
    return jax.ops.segment_sum(src, seg, n)
kernel_name = 'mk_flamingo_gated_d4_seqx_r4_ec3ebc'

def setup_inputs(seed: int=0):
    np.random.seed(seed)
    _w = jnp.asarray

    def _rec_inputs():
        import jax
        import jax.numpy as jnp
        _rk = jax.random.key(seed)
        x = -0.0003929 + 0.9999 * jax.random.normal(jax.random.fold_in(_rk, 1), (2, 1024, 256), jnp.float32)
        _lenS = 1024 - jax.random.randint(jax.random.fold_in(_rk, 7), (2,), 0, max(1, 1024 // 4) + 1, jnp.int32)
        _lenS2 = 154 - jax.random.randint(jax.random.fold_in(_rk, 8), (2,), 0, max(1, 154 // 4) + 1, jnp.int32)
        _ctx_768P = jax.random.normal(jax.random.fold_in(_rk, 11), (2, 16, 192), jnp.float32)
        _ctx_768c = jax.random.dirichlet(jax.random.fold_in(_rk, 511), 0.3 * jnp.ones((16,), jnp.float32), (2, 154))
        _ctx_768t = jnp.einsum('bsk,bkd->bsd', _ctx_768c, _ctx_768P)
        _ctx_768t = _ctx_768t * jax.lax.rsqrt(jnp.mean(jnp.square(_ctx_768t)) + 1e-12) * 0.953939
        ctx_768 = 0.00095986 + 0.999812 * (_ctx_768t + 0.3 * jax.random.normal(jax.random.fold_in(_rk, 611), (2, 154, 192), jnp.float32))
        _validS = jnp.arange(1024)[None, :] < _lenS[:, None]
        _validS2 = jnp.arange(154)[None, :] < _lenS2[:, None]
        _causal = jnp.tril(jnp.ones((1024, 1024), dtype=bool))
        mask_BxS2_bf1 = jnp.ones((2, 154), dtype=bool)
        _g = jax.random.normal(jax.random.fold_in(_rk, 9001), (2, 4), jnp.float32)
        _g = jnp.sign(_g) * jnp.maximum(jnp.abs(_g), 1.0) + (_g == 0) * 1.0
        g_xattn = _g[0]
        g_ffn = _g[1]
        return (x, ctx_768, mask_BxS2_bf1, g_xattn, g_ffn)
    x, ctx_768, mask_BxS2_bf1, g_xattn, g_ffn = _rec_inputs()

    def _L0_xattn_setup():
        import jax, jax.numpy as jnp
        import numpy as np
        DIM = 256
        CTX_DIM = 192
        HEADS = 16
        key = jax.random.key(seed)
        ks = jax.random.split(key, 7)
        B, N, M = (4, 1024, 64)
        x = jax.random.normal(ks[0], (B, N, DIM), dtype=jnp.float32)
        context = jax.random.normal(ks[1], (B, M, CTX_DIM), dtype=jnp.float32)
        context_mask = jnp.ones((B, M), dtype=bool)
        s_d = 1.0 / np.sqrt(DIM)
        s_c = 1.0 / np.sqrt(CTX_DIM)
        Wq = jax.random.normal(ks[2], (DIM, DIM), dtype=jnp.float32) * s_d
        Wk = jax.random.normal(ks[3], (CTX_DIM, DIM), dtype=jnp.float32) * s_c
        Wv = jax.random.normal(ks[4], (CTX_DIM, DIM), dtype=jnp.float32) * s_c
        Wo = jax.random.normal(ks[5], (DIM, DIM), dtype=jnp.float32) * s_d
        return {'x': x, 'context': context, 'context_mask': context_mask, 'Wq': Wq, 'Wk': Wk, 'Wv': Wv, 'Wo': Wo}
    _L0_xattn_all = _L0_xattn_setup()
    _L0_xattn_in = {k: v for k, v in _L0_xattn_all.items() if k in ('Wq', 'Wk', 'Wv', 'Wo')}
    del _L0_xattn_all

    def _L0_ffn_setup():
        import jax, jax.numpy as jnp
        import numpy as np
        B, S, DIM = (4, 1024, 256)
        BASE_COUPLING = 0.1
        NUM_CYCLES = 3

        def _gelu(x):
            return jax.nn.gelu(x, approximate=False)

        def _coupling_net(h, w1, b1, w2, b2, w3, b3, w4, b4):
            h = _gelu(h @ w1 + b1)
            h = _gelu(h @ w2 + b2)
            h = _gelu(h @ w3 + b3)
            return jax.nn.sigmoid(h @ w4 + b4)

        def _global_net(h, w1, b1, w2, b2, w3, b3):
            h = _gelu(h @ w1 + b1)
            h = _gelu(h @ w2 + b2)
            return jax.nn.sigmoid(h @ w3 + b3)

        def _twist(x):
            o_r, o_i, p_r, p_i = jnp.split(x, 4, axis=-1)
            return jnp.concatenate([p_r, -p_i, -o_r, o_i], axis=-1)
        key = jax.random.key(seed)
        ks = jax.random.split(key, 9)
        d = DIM

        def w(k, fan_in, fan_out):
            return jax.random.normal(k, (fan_in, fan_out), dtype=jnp.float32) / np.sqrt(fan_in).astype(np.float32)
        inp = {'x': jax.random.normal(ks[0], (B, S, d), dtype=jnp.float32)}
        cn_dims = [(d, d), (d, d // 2), (d // 2, d // 4), (d // 4, 1)]
        for i, (a, b) in enumerate(cn_dims):
            inp[f'cn_w{i + 1}'] = w(ks[1 + i], a, b)
            inp[f'cn_b{i + 1}'] = jnp.zeros((b,), dtype=jnp.float32)
        gc_dims = [(d, d // 2), (d // 2, d // 4), (d // 4, 1)]
        for i, (a, b) in enumerate(gc_dims):
            inp[f'gc_w{i + 1}'] = w(ks[5 + i], a, b)
            inp[f'gc_b{i + 1}'] = jnp.zeros((b,), dtype=jnp.float32)
        inp['adaptive_range'] = jnp.full((1,), 0.2, dtype=jnp.float32)
        return inp
    _L0_ffn_all = _L0_ffn_setup()
    _L0_ffn_in = {k: v for k, v in _L0_ffn_all.items() if k in ('cn_w1', 'cn_b1', 'cn_w2', 'cn_b2', 'cn_w3', 'cn_b3', 'cn_w4', 'cn_b4', 'gc_w1', 'gc_b1', 'gc_w2', 'gc_b2', 'gc_w3', 'gc_b3', 'adaptive_range')}
    del _L0_ffn_all

    def _L1_xattn_setup():
        import jax, jax.numpy as jnp
        import numpy as np
        HEADS = 8
        DIM_HEAD = 64
        SCALE = DIM_HEAD ** (-0.5)
        key = jax.random.key(seed)
        ks = jax.random.split(key, 7)
        b, n, m = (4, 512, 256)
        qd, cd, inner = (256, 192, HEADS * DIM_HEAD)
        s = lambda fan_in: 1.0 / np.sqrt(fan_in)
        return {'x': jax.random.normal(ks[0], (b, n, qd), jnp.float32), 'context': jax.random.normal(ks[1], (b, m, cd), jnp.float32), 'Wq': jax.random.normal(ks[2], (qd, inner), jnp.float32) * s(qd), 'Wk': jax.random.normal(ks[3], (cd, inner), jnp.float32) * s(cd), 'Wv': jax.random.normal(ks[4], (cd, inner), jnp.float32) * s(cd), 'Wout': jax.random.normal(ks[5], (inner, qd), jnp.float32) * s(inner), 'bout': jax.random.normal(ks[6], (qd,), jnp.float32) * 0.01}
    _L1_xattn_all = _L1_xattn_setup()
    _L1_xattn_in = {k: v for k, v in _L1_xattn_all.items() if k in ('Wq', 'Wk', 'Wv', 'Wout', 'bout')}
    del _L1_xattn_all

    def _L1_ffn_setup():
        import jax, jax.numpy as jnp
        import numpy as np
        EPS = 1e-08

        def _ste(x, q):
            return x + jax.lax.stop_gradient(q - x)

        def quant_act_uint8(x):
            s = jax.lax.stop_gradient(jnp.maximum(jnp.max(x), EPS)) / 255.0
            q = jnp.clip(jnp.round(x / s), 0.0, 255.0) * s
            return (_ste(x, q), s)

        def quant_weight_int8_perchannel(w):
            s = jax.lax.stop_gradient(jnp.maximum(jnp.max(jnp.abs(w), axis=1, keepdims=True), EPS)) / 127.0
            q = jnp.clip(jnp.round(w / s), -128.0, 127.0) * s
            return (_ste(w, q), s[:, 0])

        def quant_bias_int32(b, s_in, s_w):
            s = jax.lax.stop_gradient(s_in * s_w)
            q = jnp.round(b / s) * s
            return _ste(b, q)

        def quant_linear(x, w, b):
            xq, s_in = quant_act_uint8(x)
            wq, s_w = quant_weight_int8_perchannel(w)
            bq = quant_bias_int32(b, s_in, s_w)
            return jnp.einsum('btd,fd->btf', xq, wq) + bq
        key = jax.random.key(seed)
        k1, k2, k3, k4, k5 = jax.random.split(key, 5)
        B, S, D, F = (4, 512, 256, 1024)
        return {'x': jax.random.normal(k1, (B, S, D), dtype=jnp.float32), 'w1': jax.random.normal(k2, (F, D), dtype=jnp.float32) * (1.0 / np.sqrt(D)), 'b1': jax.random.normal(k3, (F,), dtype=jnp.float32) * 0.01, 'w2': jax.random.normal(k4, (D, F), dtype=jnp.float32) * (1.0 / np.sqrt(F)), 'b2': jax.random.normal(k5, (D,), dtype=jnp.float32) * 0.01}
    _L1_ffn_all = _L1_ffn_setup()
    _L1_ffn_in = {k: v for k, v in _L1_ffn_all.items() if k in ('w1', 'b1', 'w2', 'b2')}
    del _L1_ffn_all

    def _L2_xattn_setup():
        import jax, jax.numpy as jnp
        import numpy as np
        N_HEADS = 16
        DIM_EMBED = 256
        DIM_CROSS = 192
        DIM_HEAD = DIM_EMBED // N_HEADS
        key = jax.random.key(seed)
        ks = jax.random.split(key, 10)
        B, Sq, Sk = (8, 1024, 77)
        s_e = 1.0 / np.sqrt(DIM_EMBED)
        s_c = 1.0 / np.sqrt(DIM_CROSS)
        return {'x': jax.random.normal(ks[0], (B, Sq, DIM_EMBED), jnp.float32), 'y': jax.random.normal(ks[1], (B, Sk, DIM_CROSS), jnp.float32), 'wq': jax.random.normal(ks[2], (DIM_EMBED, DIM_EMBED), jnp.float32) * s_e, 'bq': jax.random.normal(ks[3], (DIM_EMBED,), jnp.float32) * 0.01, 'wk': jax.random.normal(ks[4], (DIM_CROSS, DIM_EMBED), jnp.float32) * s_c, 'bk': jax.random.normal(ks[5], (DIM_EMBED,), jnp.float32) * 0.01, 'wv': jax.random.normal(ks[6], (DIM_CROSS, DIM_EMBED), jnp.float32) * s_c, 'bv': jax.random.normal(ks[7], (DIM_EMBED,), jnp.float32) * 0.01, 'wo': jax.random.normal(ks[8], (DIM_EMBED, DIM_EMBED), jnp.float32) * s_e, 'bo': jax.random.normal(ks[9], (DIM_EMBED,), jnp.float32) * 0.01}
    _L2_xattn_all = _L2_xattn_setup()
    _L2_xattn_in = {k: v for k, v in _L2_xattn_all.items() if k in ('wq', 'bq', 'wk', 'bk', 'wv', 'bv', 'wo', 'bo')}
    del _L2_xattn_all

    def _L2_ffn_setup():
        import jax, jax.numpy as jnp
        import numpy as np
        B, T, D, E, K = (2, 512, 256, 8, 2)
        H = 2 * D
        key = jax.random.key(seed)
        ks = jax.random.split(key, 5)
        s = 0.02
        return {'x': jax.random.normal(ks[0], (B, T, D), jnp.float32), 'Wr': jax.random.normal(ks[1], (D, E), jnp.float32) * s, 'br': jnp.zeros((E,), jnp.float32), 'W1': jax.random.normal(ks[2], (E, D, H), jnp.float32) * s, 'b1': jnp.zeros((E, H), jnp.float32), 'W2': jax.random.normal(ks[3], (E, H, D), jnp.float32) * s, 'b2': jnp.zeros((E, D), jnp.float32)}
    _L2_ffn_all = _L2_ffn_setup()
    _L2_ffn_in = {k: v for k, v in _L2_ffn_all.items() if k in ('Wr', 'br', 'W1', 'b1', 'W2', 'b2')}
    del _L2_ffn_all

    def _L3_xattn_setup():
        import jax, jax.numpy as jnp
        import numpy as np
        QUERY_DIM, KV_DIM, EMBED_DIM, NUM_HEADS = (256, 192, 256, 16)
        HEAD_DIM = EMBED_DIM // NUM_HEADS
        SCALE = HEAD_DIM ** (-0.5)
        LN_EPS = 1e-05

        def _l2norm(x, eps=1e-12):
            n = jnp.sqrt(jnp.sum(x * x, axis=-1, keepdims=True))
            return x / jnp.maximum(n, eps)
        key = jax.random.key(seed)
        ks = jax.random.split(key, 12)
        B, Nq, Nk = (2, 512, 512)
        s = lambda d: 1.0 / np.sqrt(d)
        return {'query': jax.random.normal(ks[0], (B, Nq, QUERY_DIM), jnp.float32), 'key': jax.random.normal(ks[1], (B, Nk, KV_DIM), jnp.float32), 'value': jax.random.normal(ks[2], (B, Nk, KV_DIM), jnp.float32), 'Wq': jax.random.normal(ks[3], (QUERY_DIM, EMBED_DIM), jnp.float32) * s(QUERY_DIM), 'bq': jnp.zeros((EMBED_DIM,), jnp.float32), 'Wk': jax.random.normal(ks[4], (KV_DIM, EMBED_DIM), jnp.float32) * s(KV_DIM), 'bk': jnp.zeros((EMBED_DIM,), jnp.float32), 'Wv': jax.random.normal(ks[5], (KV_DIM, EMBED_DIM), jnp.float32) * s(KV_DIM), 'bv': jnp.zeros((EMBED_DIM,), jnp.float32), 'Wo': jax.random.normal(ks[6], (EMBED_DIM, EMBED_DIM), jnp.float32) * s(EMBED_DIM), 'bo': jnp.zeros((EMBED_DIM,), jnp.float32), 'ln_gamma': jnp.ones((EMBED_DIM,), jnp.float32), 'ln_beta': jnp.zeros((EMBED_DIM,), jnp.float32)}
    _L3_xattn_all = _L3_xattn_setup()
    _L3_xattn_in = {k: v for k, v in _L3_xattn_all.items() if k in ('Wq', 'bq', 'Wk', 'bk', 'Wv', 'bv', 'Wo', 'bo', 'ln_gamma', 'ln_beta')}
    del _L3_xattn_all

    def _L3_ffn_setup():
        import jax, jax.numpy as jnp
        import numpy as np
        B, S, D = (1, 512, 256)
        F = 352
        E = 16
        K = 2
        CAP_FACTOR = 1.25

        def _mlp(h, wg, wu, wd):
            return jax.nn.silu(h @ wg) * (h @ wu) @ wd
        key = jax.random.key(seed)
        ks = jax.random.split(key, 10)
        sd = 0.02
        return {'x': jax.random.normal(ks[0], (B, S, D), jnp.float32), 'router_w': jax.random.normal(ks[1], (D, E), jnp.float32) * sd, 'router_b': jnp.zeros((E,), jnp.float32), 'w_gate': jax.random.normal(ks[2], (E, D, F), jnp.float32) * sd, 'w_up': jax.random.normal(ks[3], (E, D, F), jnp.float32) * sd, 'w_down': jax.random.normal(ks[4], (E, F, D), jnp.float32) * sd, 'sw_gate': jax.random.normal(ks[5], (D, F), jnp.float32) * sd, 'sw_up': jax.random.normal(ks[6], (D, F), jnp.float32) * sd, 'sw_down': jax.random.normal(ks[7], (F, D), jnp.float32) * sd}
    _L3_ffn_all = _L3_ffn_setup()
    _L3_ffn_in = {k: v for k, v in _L3_ffn_all.items() if k in ('router_w', 'router_b', 'w_gate', 'w_up', 'w_down', 'sw_gate', 'sw_up', 'sw_down')}
    del _L3_ffn_all
    return {'x': x, 'ctx_768': ctx_768, 'mask_BxS2_bf1': mask_BxS2_bf1, 'g_xattn': g_xattn, 'g_ffn': g_ffn, 'L0_xattn_Wq': _L0_xattn_in['Wq'], 'L0_xattn_Wk': _L0_xattn_in['Wk'], 'L0_xattn_Wv': _L0_xattn_in['Wv'], 'L0_xattn_Wo': _L0_xattn_in['Wo'], 'L0_ffn_cn_w1': _L0_ffn_in['cn_w1'], 'L0_ffn_cn_b1': _L0_ffn_in['cn_b1'], 'L0_ffn_cn_w2': _L0_ffn_in['cn_w2'], 'L0_ffn_cn_b2': _L0_ffn_in['cn_b2'], 'L0_ffn_cn_w3': _L0_ffn_in['cn_w3'], 'L0_ffn_cn_b3': _L0_ffn_in['cn_b3'], 'L0_ffn_cn_w4': _L0_ffn_in['cn_w4'], 'L0_ffn_cn_b4': _L0_ffn_in['cn_b4'], 'L0_ffn_gc_w1': _L0_ffn_in['gc_w1'], 'L0_ffn_gc_b1': _L0_ffn_in['gc_b1'], 'L0_ffn_gc_w2': _L0_ffn_in['gc_w2'], 'L0_ffn_gc_b2': _L0_ffn_in['gc_b2'], 'L0_ffn_gc_w3': _L0_ffn_in['gc_w3'], 'L0_ffn_gc_b3': _L0_ffn_in['gc_b3'], 'L0_ffn_adaptive_range': _L0_ffn_in['adaptive_range'], 'L1_xattn_Wq': _L1_xattn_in['Wq'], 'L1_xattn_Wk': _L1_xattn_in['Wk'], 'L1_xattn_Wv': _L1_xattn_in['Wv'], 'L1_xattn_Wout': _L1_xattn_in['Wout'], 'L1_xattn_bout': _L1_xattn_in['bout'], 'L1_ffn_w1': _L1_ffn_in['w1'], 'L1_ffn_b1': _L1_ffn_in['b1'], 'L1_ffn_w2': _L1_ffn_in['w2'], 'L1_ffn_b2': _L1_ffn_in['b2'], 'L2_xattn_wq': _L2_xattn_in['wq'], 'L2_xattn_bq': _L2_xattn_in['bq'], 'L2_xattn_wk': _L2_xattn_in['wk'], 'L2_xattn_bk': _L2_xattn_in['bk'], 'L2_xattn_wv': _L2_xattn_in['wv'], 'L2_xattn_bv': _L2_xattn_in['bv'], 'L2_xattn_wo': _L2_xattn_in['wo'], 'L2_xattn_bo': _L2_xattn_in['bo'], 'L2_ffn_Wr': _L2_ffn_in['Wr'], 'L2_ffn_br': _L2_ffn_in['br'], 'L2_ffn_W1': _L2_ffn_in['W1'], 'L2_ffn_b1': _L2_ffn_in['b1'], 'L2_ffn_W2': _L2_ffn_in['W2'], 'L2_ffn_b2': _L2_ffn_in['b2'], 'L3_xattn_Wq': _L3_xattn_in['Wq'], 'L3_xattn_bq': _L3_xattn_in['bq'], 'L3_xattn_Wk': _L3_xattn_in['Wk'], 'L3_xattn_bk': _L3_xattn_in['bk'], 'L3_xattn_Wv': _L3_xattn_in['Wv'], 'L3_xattn_bv': _L3_xattn_in['bv'], 'L3_xattn_Wo': _L3_xattn_in['Wo'], 'L3_xattn_bo': _L3_xattn_in['bo'], 'L3_xattn_ln_gamma': _L3_xattn_in['ln_gamma'], 'L3_xattn_ln_beta': _L3_xattn_in['ln_beta'], 'L3_ffn_router_w': _L3_ffn_in['router_w'], 'L3_ffn_router_b': _L3_ffn_in['router_b'], 'L3_ffn_w_gate': _L3_ffn_in['w_gate'], 'L3_ffn_w_up': _L3_ffn_in['w_up'], 'L3_ffn_w_down': _L3_ffn_in['w_down'], 'L3_ffn_sw_gate': _L3_ffn_in['sw_gate'], 'L3_ffn_sw_up': _L3_ffn_in['sw_up'], 'L3_ffn_sw_down': _L3_ffn_in['sw_down']}

def reference(x, ctx_768, mask_BxS2_bf1, g_xattn, g_ffn, L0_xattn_Wq, L0_xattn_Wk, L0_xattn_Wv, L0_xattn_Wo, L0_ffn_cn_w1, L0_ffn_cn_b1, L0_ffn_cn_w2, L0_ffn_cn_b2, L0_ffn_cn_w3, L0_ffn_cn_b3, L0_ffn_cn_w4, L0_ffn_cn_b4, L0_ffn_gc_w1, L0_ffn_gc_b1, L0_ffn_gc_w2, L0_ffn_gc_b2, L0_ffn_gc_w3, L0_ffn_gc_b3, L0_ffn_adaptive_range, L1_xattn_Wq, L1_xattn_Wk, L1_xattn_Wv, L1_xattn_Wout, L1_xattn_bout, L1_ffn_w1, L1_ffn_b1, L1_ffn_w2, L1_ffn_b2, L2_xattn_wq, L2_xattn_bq, L2_xattn_wk, L2_xattn_bk, L2_xattn_wv, L2_xattn_bv, L2_xattn_wo, L2_xattn_bo, L2_ffn_Wr, L2_ffn_br, L2_ffn_W1, L2_ffn_b1, L2_ffn_W2, L2_ffn_b2, L3_xattn_Wq, L3_xattn_bq, L3_xattn_Wk, L3_xattn_bk, L3_xattn_Wv, L3_xattn_bv, L3_xattn_Wo, L3_xattn_bo, L3_xattn_ln_gamma, L3_xattn_ln_beta, L3_ffn_router_w, L3_ffn_router_b, L3_ffn_w_gate, L3_ffn_w_up, L3_ffn_w_down, L3_ffn_sw_gate, L3_ffn_sw_up, L3_ffn_sw_down):
    import jax
    import jax.numpy as jnp

    def _L0_xattn_ref(x, context, context_mask, Wq, Wk, Wv, Wo):
        import jax, jax.numpy as jnp
        import numpy as np
        DIM = 256
        CTX_DIM = 192
        HEADS = 16
        B, N, _ = x.shape
        M = context.shape[1]
        hd = DIM // HEADS
        scale = hd ** (-0.5)
        q = (x @ Wq).reshape(B, N, HEADS, hd).transpose(0, 2, 1, 3)
        k = (context @ Wk).reshape(B, M, HEADS, hd).transpose(0, 2, 1, 3)
        v = (context @ Wv).reshape(B, M, HEADS, hd).transpose(0, 2, 1, 3)
        scores = jnp.einsum('bhid,bhjd->bhij', q, k) * scale
        max_neg = -jnp.finfo(scores.dtype).max
        scores = jnp.where(context_mask[:, None, None, :], scores, max_neg)
        attn = jax.nn.softmax(scores, axis=-1)
        out = jnp.einsum('bhij,bhjd->bhid', attn, v)
        out = out.transpose(0, 2, 1, 3).reshape(B, N, DIM)
        return out @ Wo

    def _L0_ffn_ref(x, cn_w1, cn_b1, cn_w2, cn_b2, cn_w3, cn_b3, cn_w4, cn_b4, gc_w1, gc_b1, gc_w2, gc_b2, gc_w3, gc_b3, adaptive_range):
        import jax, jax.numpy as jnp
        import numpy as np
        B, S, DIM = (4, 1024, 256)
        BASE_COUPLING = 0.1
        NUM_CYCLES = 3

        def _gelu(x):
            return jax.nn.gelu(x, approximate=False)

        def _coupling_net(h, w1, b1, w2, b2, w3, b3, w4, b4):
            h = _gelu(h @ w1 + b1)
            h = _gelu(h @ w2 + b2)
            h = _gelu(h @ w3 + b3)
            return jax.nn.sigmoid(h @ w4 + b4)

        def _global_net(h, w1, b1, w2, b2, w3, b3):
            h = _gelu(h @ w1 + b1)
            h = _gelu(h @ w2 + b2)
            return jax.nn.sigmoid(h @ w3 + b3)

        def _twist(x):
            o_r, o_i, p_r, p_i = jnp.split(x, 4, axis=-1)
            return jnp.concatenate([p_r, -p_i, -o_r, o_i], axis=-1)
        global_context = x.mean(axis=1, keepdims=True)
        gf = _global_net(global_context, gc_w1, gc_b1, gc_w2, gc_b2, gc_w3, gc_b3)
        out = x
        for _ in range(NUM_CYCLES):
            tf = _coupling_net(out, cn_w1, cn_b1, cn_w2, cn_b2, cn_w3, cn_b3, cn_w4, cn_b4)
            combined = 0.7 * gf + 0.3 * tf
            coupling = BASE_COUPLING + adaptive_range * (combined - 0.5) * 2.0
            out = out + coupling * _twist(out)
        return out

    def _L1_xattn_ref(x, context, Wq, Wk, Wv, Wout, bout):
        import jax, jax.numpy as jnp
        import numpy as np
        HEADS = 8
        DIM_HEAD = 64
        SCALE = DIM_HEAD ** (-0.5)
        b, n, _ = x.shape
        m = context.shape[1]
        q = (x @ Wq).reshape(b, n, HEADS, DIM_HEAD)
        k = (context @ Wk).reshape(b, m, HEADS, DIM_HEAD)
        v = (context @ Wv).reshape(b, m, HEADS, DIM_HEAD)
        sim = jnp.einsum('bihd,bjhd->bhij', q, k) * SCALE
        attn = jax.nn.softmax(sim, axis=-1)
        out = jnp.einsum('bhij,bjhd->bihd', attn, v).reshape(b, n, HEADS * DIM_HEAD)
        return out @ Wout + bout

    def _L1_ffn_ref(x, w1, b1, w2, b2):
        import jax, jax.numpy as jnp
        import numpy as np
        EPS = 1e-08

        def _ste(x, q):
            return x + jax.lax.stop_gradient(q - x)

        def quant_act_uint8(x):
            s = jax.lax.stop_gradient(jnp.maximum(jnp.max(x), EPS)) / 255.0
            q = jnp.clip(jnp.round(x / s), 0.0, 255.0) * s
            return (_ste(x, q), s)

        def quant_weight_int8_perchannel(w):
            s = jax.lax.stop_gradient(jnp.maximum(jnp.max(jnp.abs(w), axis=1, keepdims=True), EPS)) / 127.0
            q = jnp.clip(jnp.round(w / s), -128.0, 127.0) * s
            return (_ste(w, q), s[:, 0])

        def quant_bias_int32(b, s_in, s_w):
            s = jax.lax.stop_gradient(s_in * s_w)
            q = jnp.round(b / s) * s
            return _ste(b, q)

        def quant_linear(x, w, b):
            xq, s_in = quant_act_uint8(x)
            wq, s_w = quant_weight_int8_perchannel(w)
            bq = quant_bias_int32(b, s_in, s_w)
            return jnp.einsum('btd,fd->btf', xq, wq) + bq
        h = jax.nn.relu(quant_linear(x, w1, b1))
        return quant_linear(h, w2, b2)

    def _L2_xattn_ref(x, y, wq, bq, wk, bk, wv, bv, wo, bo):
        import jax, jax.numpy as jnp
        import numpy as np
        N_HEADS = 16
        DIM_EMBED = 256
        DIM_CROSS = 192
        DIM_HEAD = DIM_EMBED // N_HEADS
        B, Sq, E = x.shape
        H, D = (N_HEADS, DIM_HEAD)
        q = (x @ wq + bq).reshape(B, Sq, H, D).transpose(0, 2, 1, 3)
        k = (y @ wk + bk).reshape(B, -1, H, D).transpose(0, 2, 1, 3)
        v = (y @ wv + bv).reshape(B, -1, H, D).transpose(0, 2, 1, 3)
        scores = jnp.einsum('bhqd,bhkd->bhqk', q, k) / jnp.sqrt(jnp.asarray(D, x.dtype))
        attn = jax.nn.softmax(scores, axis=-1)
        out = jnp.einsum('bhqk,bhkd->bhqd', attn, v)
        out = out.transpose(0, 2, 1, 3).reshape(B, Sq, E)
        return out @ wo + bo

    def _L2_ffn_ref(x, Wr, br, W1, b1, W2, b2):
        import jax, jax.numpy as jnp
        import numpy as np
        B, T, D, E, K = (2, 512, 256, 8, 2)
        H = 2 * D
        logits = jnp.einsum('btd,de->bte', x, Wr) + br
        topv, topi = jax.lax.top_k(logits, K)
        sel_mask = jax.nn.one_hot(topi, E, dtype=logits.dtype).sum(-2) > 0
        neg_inf = jnp.finfo(logits.dtype).min
        gates = jax.nn.softmax(jnp.where(sel_mask, logits, neg_inf), axis=-1)
        h = jax.nn.relu(jnp.einsum('btd,edh->bteh', x, W1) + b1)
        out = jnp.einsum('bte,bteh,ehd->btd', gates, h, W2)
        out = out + jnp.einsum('bte,ed->btd', gates, b2)
        return out

    def _L3_xattn_ref(query, key, value, Wq, bq, Wk, bk, Wv, bv, Wo, bo, ln_gamma, ln_beta):
        import jax, jax.numpy as jnp
        import numpy as np
        QUERY_DIM, KV_DIM, EMBED_DIM, NUM_HEADS = (256, 192, 256, 16)
        HEAD_DIM = EMBED_DIM // NUM_HEADS
        SCALE = HEAD_DIM ** (-0.5)
        LN_EPS = 1e-05

        def _l2norm(x, eps=1e-12):
            n = jnp.sqrt(jnp.sum(x * x, axis=-1, keepdims=True))
            return x / jnp.maximum(n, eps)
        B, Nq, _ = query.shape
        Nk = key.shape[1]
        Qp = query @ Wq + bq
        K = _l2norm(key @ Wk + bk)
        V = value @ Wv + bv
        Q = _l2norm(Qp)
        Q = Q.reshape(B, Nq, NUM_HEADS, HEAD_DIM).transpose(0, 2, 1, 3)
        K = K.reshape(B, Nk, NUM_HEADS, HEAD_DIM).transpose(0, 2, 1, 3)
        V = V.reshape(B, Nk, NUM_HEADS, HEAD_DIM).transpose(0, 2, 1, 3)
        scores = jnp.einsum('bhqd,bhkd->bhqk', Q, K) * SCALE
        attn = jax.nn.softmax(scores, axis=-1)
        out = jnp.einsum('bhqk,bhkd->bhqd', attn, V)
        out = out.transpose(0, 2, 1, 3).reshape(B, Nq, EMBED_DIM)
        out = out @ Wo + bo
        x = out + Qp
        mu = jnp.mean(x, axis=-1, keepdims=True)
        var = jnp.mean((x - mu) ** 2, axis=-1, keepdims=True)
        return (x - mu) / jnp.sqrt(var + LN_EPS) * ln_gamma + ln_beta

    def _L3_ffn_ref(x, router_w, router_b, w_gate, w_up, w_down, sw_gate, sw_up, sw_down):
        import jax, jax.numpy as jnp
        import numpy as np
        B, S, D = (1, 512, 256)
        F = 352
        E = 16
        K = 2
        CAP_FACTOR = 1.25

        def _mlp(h, wg, wu, wd):
            return jax.nn.silu(h @ wg) * (h @ wu) @ wd
        b, s, d = x.shape
        N = b * s
        NK = N * K
        C = int(np.ceil(CAP_FACTOR * NK / E))
        x_tokens = x.reshape(N, d)
        logits = x_tokens @ router_w + router_b
        probs = jax.nn.softmax(logits, axis=-1)
        vals, idx = jax.lax.top_k(probs, K)
        vals = vals / (jnp.sum(vals, axis=-1, keepdims=True) + 1e-09)
        idx_flat = idx.reshape(NK)
        vals_flat = vals.reshape(NK)
        oh_e = jax.nn.one_hot(idx_flat, E, dtype=x.dtype)
        pos = (jnp.cumsum(oh_e, axis=0) * oh_e).sum(axis=1) - 1
        within = (pos < C).astype(x.dtype)
        pos_c = jnp.clip(pos, 0, C - 1).astype(jnp.int32)
        token_ids = jnp.arange(NK) // K
        x_pair = x_tokens[token_ids] * within[:, None]
        expert_inputs = jnp.zeros((E, C, d), x.dtype).at[idx_flat, pos_c].add(x_pair)
        expert_outputs = jax.vmap(_mlp)(expert_inputs, w_gate, w_up, w_down)
        gathered = expert_outputs[idx_flat, pos_c] * (vals_flat * within)[:, None]
        output_tokens = gathered.reshape(N, K, d).sum(axis=1)
        return x + _mlp(x, sw_gate, sw_up, sw_down) + output_tokens.reshape(b, s, d)
    x = x + jnp.tanh(g_xattn[0]) * _L0_xattn_ref(_layernorm(x, axis=-1), ctx_768, mask_BxS2_bf1, L0_xattn_Wq, L0_xattn_Wk, L0_xattn_Wv, L0_xattn_Wo)
    x = x + jnp.tanh(g_ffn[0]) * _L0_ffn_ref(_layernorm(x, axis=-1), L0_ffn_cn_w1, L0_ffn_cn_b1, L0_ffn_cn_w2, L0_ffn_cn_b2, L0_ffn_cn_w3, L0_ffn_cn_b3, L0_ffn_cn_w4, L0_ffn_cn_b4, L0_ffn_gc_w1, L0_ffn_gc_b1, L0_ffn_gc_w2, L0_ffn_gc_b2, L0_ffn_gc_w3, L0_ffn_gc_b3, L0_ffn_adaptive_range)
    x = x + jnp.tanh(g_xattn[1]) * _L1_xattn_ref(_layernorm(x, axis=-1), ctx_768, L1_xattn_Wq, L1_xattn_Wk, L1_xattn_Wv, L1_xattn_Wout, L1_xattn_bout)
    x = x + jnp.tanh(g_ffn[1]) * _L1_ffn_ref(_layernorm(x, axis=-1), L1_ffn_w1, L1_ffn_b1, L1_ffn_w2, L1_ffn_b2)
    x = x + jnp.tanh(g_xattn[2]) * _L2_xattn_ref(_layernorm(x, axis=-1), ctx_768, L2_xattn_wq, L2_xattn_bq, L2_xattn_wk, L2_xattn_bk, L2_xattn_wv, L2_xattn_bv, L2_xattn_wo, L2_xattn_bo)
    x = x + jnp.tanh(g_ffn[2]) * _L2_ffn_ref(_layernorm(x, axis=-1), L2_ffn_Wr, L2_ffn_br, L2_ffn_W1, L2_ffn_b1, L2_ffn_W2, L2_ffn_b2)
    x = x + jnp.tanh(g_xattn[3]) * _L3_xattn_ref(_layernorm(x, axis=-1), ctx_768, ctx_768, L3_xattn_Wq, L3_xattn_bq, L3_xattn_Wk, L3_xattn_bk, L3_xattn_Wv, L3_xattn_bv, L3_xattn_Wo, L3_xattn_bo, L3_xattn_ln_gamma, L3_xattn_ln_beta)
    x = x + jnp.tanh(g_ffn[3]) * _L3_ffn_ref(_layernorm(x, axis=-1), L3_ffn_router_w, L3_ffn_router_b, L3_ffn_w_gate, L3_ffn_w_up, L3_ffn_w_down, L3_ffn_sw_gate, L3_ffn_sw_up, L3_ffn_sw_down)
    return x

_drawn_inputs = setup_inputs


def setup_inputs(seed=0):
    import zlib

    import numpy as np

    out = dict(_drawn_inputs(seed))
    spreads = {'L0_ffn_cn_b1': (0.0, 0.8),
     'L0_ffn_cn_b2': (0.0, 0.739),
     'L0_ffn_cn_b3': (0.0, 0.681),
     'L0_ffn_gc_b1': (0.0, 0.8),
     'L0_ffn_gc_b2': (0.0, 0.591),
     'L2_ffn_br': (0.0, 0.1),
     'L2_ffn_b1': (0.0, 0.446),
     'L2_ffn_b2': (0.0, 0.1),
     'L3_xattn_bq': (0.0, 0.1),
     'L3_xattn_bk': (0.0, 0.8),
     'L3_xattn_bv': (0.0, 0.1),
     'L3_xattn_bo': (0.0, 0.1),
     'L3_xattn_ln_gamma': (1.0, 0.2),
     'L3_xattn_ln_beta': (0.0, 0.1),
     'L3_ffn_router_b': (0.0, 0.8)}
    factors = {'L0_ffn_cn_w1': 3.047,
     'L0_ffn_cn_w2': 3.063,
     'L0_ffn_cn_w4': 2.899,
     'L0_ffn_gc_w2': 5.125,
     'L1_xattn_bout': 3.337,
     'L1_ffn_b1': 4.955,
     'L1_ffn_b2': 4.893,
     'L2_xattn_bq': 8.0,
     'L2_xattn_bk': 8.0,
     'L2_xattn_bv': 6.005,
     'L2_xattn_bo': 5.248,
     'L3_xattn_Wk': 8.0,
     'L3_ffn_router_w': 8.0,
     'L3_ffn_w_gate': 8.0,
     'L3_ffn_w_up': 8.0,
     'L3_ffn_w_down': 8.0,
     'L3_ffn_sw_gate': 6.804,
     'L3_ffn_sw_up': 6.245,
     'L3_ffn_sw_down': 6.189}
    for name, (base, spread) in spreads.items():
        noise = np.random.default_rng([zlib.crc32(name.encode()), seed]).standard_normal(out[name].shape)
        drawn = base * np.exp(spread * noise) if base else spread * noise
        out[name] = jnp.asarray(drawn.astype(out[name].dtype))
    for name, factor in factors.items():
        out[name] = (out[name] * factor).astype(out[name].dtype)
    return out
```

```python
import concourse.bass as bass
from concourse import mybir
from contextlib import ExitStack

F32 = mybir.dt.float32
BF16 = mybir.dt.bfloat16
U32 = mybir.dt.uint32
U8 = mybir.dt.uint8
ALU = mybir.AluOpType
ACT = mybir.ActivationFunctionType
AX = mybir.AxisListType
RMAX = bass.bass_isa.ReduceOp.max

P = 128
B, S, D = 2, 1024, 256
T = B * S
NT = T // P
CH = 512
NC = T // CH
TPC = CH // P
CPB = NC // B
DK = D // P
M, CD = 154, 192
MR = M - P
BIG = float(2.0 ** 100)
ROUND = 12582912.0
PHASES = 8

HEADS = {0: (16, 16), 1: (8, 64), 2: (16, 16), 3: (16, 16)}
E2, H2 = 8, 512
E3, F3 = 16, 352
CAP = 320
F3T = [128, 128, 96]
F1 = 1024
FT1 = F1 // P


class Ring:

    def __init__(self, banks, filled, read):
        self.banks, self.filled, self.read, self.order, self.emptied = banks, filled, read, {}, 0

    def take(self, pe, *key):
        i = len(self.order)
        assert key not in self.order, key
        self.order[key] = i
        if i >= len(self.banks):
            pe.wait_ge(self.read, i - len(self.banks) + 1)
        return self.banks[i % len(self.banks)]

    def n(self, *key):
        return self.order[key] + 1

    def get(self, eng, *key):
        assert self.order[key] == self.emptied, (key, self.order[key], self.emptied)
        self.emptied += 1
        eng.wait_ge(self.filled, self.order[key] + 1)
        return self.banks[self.order[key] % len(self.banks)]


class Steps:

    def __init__(self, eng, sem):
        self.eng, self.sem, self.count = eng, sem, 0

    def did(self, ins):
        self.count += 1
        ins.then_inc(self.sem, 1)
        return self.count

    def wait(self, count=None):
        self.eng.wait_ge(self.sem, self.count if count is None else count)


class Arena:
    def __init__(self, tensor, words):
        self.t, self.words, self.at = tensor, words, 0

    def reset(self):
        self.at = 0

    def take(self, shape, dt=F32):
        n = 1
        for s in shape:
            n *= s
        words = n if dt in (F32, U32) else (n + 1) // 2 if dt == BF16 else (n + 3) // 4
        ap = self.t[:, self.at:self.at + words]
        self.at += (words + 7) // 8 * 8
        assert self.at <= self.words, (self.at, self.words)
        if dt != F32:
            ap = ap.bitcast(dt)[:, 0:n]
        if len(shape) > 1:
            names = "abcd"[:len(shape)]
            ap = ap.rearrange("p (" + " ".join(names) + ") -> p " + " ".join(names),
                              **{k: s for k, s in zip(names, shape)})
        return ap


def bc(ap, shape):
    return ap.broadcast_to(shape)


def build(nc, A, out):
    ctx = ExitStack()
    with ctx:
        def sb(name, shape, dt=F32):
            return ctx.enter_context(nc.sbuf_tensor(name, shape, dt))

        def sem(name):
            return ctx.enter_context(nc.semaphore(name))

        banks = [ctx.enter_context(nc.psum_tensor(f"bank{i}", [P, 512], F32)) for i in range(8)]
        RA = Ring(banks[0:2], sem("a_bank_filled"), sem("a_bank_read"))
        RB = Ring(banks[2:4], sem("b_bank_filled"), sem("b_bank_read"))
        RC = Ring(banks[4:8], sem("c_bank_filled"), sem("c_bank_read"))

        X = sb("X", [P, NT, D])
        ident = sb("ident", [P, P])
        identb = sb("identb", [P, P], BF16)
        ones = sb("ones", [P, P])
        before = sb("before", [P, P], BF16)
        onesb = sb("onesb", [P, P], BF16)
        hmask = {16: sb("hmask16", [P, 8]), 64: sb("hmask64", [P, 2])}
        sel = sb("sel", [65, 16, P], BF16)
        selr = sb("selr", [65, 4, 4, 32], BF16)
        sgn = sb("sgn", [P, 1])
        nhalf = sb("nhalf", [P, NT])
        iota = sb("iota", [P, 16])
        gates = sb("gates", [P, 8])
        tg = sb("tg", [P, 8])
        ctxT = sb("ctxT", [P, 2, B * M])
        stats = sb("stats", [P, NT, 6])
        mv = sb("mv", [P, NT, 2])
        rstd = sb("rstd", [P, NT])
        WA = 4864
        warena = [Arena(sb(f"weights{i}", [P, WA]), WA) for i in range(2)]
        SA = 36200
        scratch = Arena(sb("scratch", [P, SA]), SA)

        w_loaded = [sem(f"weights_loaded_{p}") for p in range(8)]
        in_loaded = sem("inputs_loaded")
        consts = sem("constants_made")
        tg_made = sem("gates_made")
        ctxT_made = sem("context_transposed")
        ln_stats = sem("ln_statistics")
        ln_rstd = sem("ln_rstd_made")
        ln_y = sem("ln_normalised")
        phase_over = sem("phase_over")
        kv_clear = sem("kv_buffers_cleared")
        kz_made = sem("keys_spread")
        kr_made = sem("last_keys_spread")
        v_made = sem("values_made")
        negm_clear = sem("negated_maxima_cleared")
        xbias = sem("bias_added_to_x")
        pool_st = sem("pool_steps")
        act_st = sem("act_steps")
        dve_st = sem("dve_steps")
        kn_made = sem("keys_normalised")
        kn_clear = sem("key_buffers_cleared")
        kss_made = sem("key_squares_summed")
        qss_made = sem("query_squares_summed")
        qn_made = sem("queries_normalised")
        qbo_made = sem("residual_query_ready")
        post_stats = sem("post_ln_statistics")
        post_z = sem("post_ln_normalised")
        mb_made = sem("mask_bias_made")
        sel0_made = sem("selectors_with_mask_made")
        gbo_made = sem("gated_bias_made")
        gc_ready = sem("global_net_inputs_ready")
        state_made = sem("coupled_state_made")
        wq_made = sem("weights_rounded")
        diag_made = sem("scales_on_the_diagonal")
        xmax_made = sem("largest_of_partition")
        xall_made = sem("largest_of_all")
        xi_made = sem("x_rounded")
        hscale_made = sem("hidden_scale_and_bias_made")
        hi_made = sem("hidden_rounded")
        rows_made = sem("output_scale_rows_made")
        oh_made = sem("one_hots_made")
        g_made = sem("gate_weights_made")
        ex_ready = sem("exponents_ready")
        ex_made = sem("exponentials_made")
        XB = {2: 1, 3: 2, 4: 3, 6: 4}
        EWN = {2: 2, 3: 4}
        ew_loaded = {2: [sem(f"expert2_loaded_{i}") for i in range(3)], 3: [sem(f"expert3_loaded_{i}") for i in range(2)]}
        stored = sem("output_stored")

        NIN = 2 * B + 3
        NCONST = 5

        ph = []
        loads = []

        def col(ap, n):
            return ap.rearrange("(m p) -> p m", p=P)

        def row(ap, n):
            return bc(ap.rearrange("(o n) -> o n", o=1), (P, n))

        def kin(ap):
            return ap.rearrange("(k p) n -> p k n", p=P)

        def ctxw(w, dst):
            return [(dst[:, 0, :], w[0:P, :]), (dst[0:CD - P, 1, :], w[P:CD, :])]

        for L in range(4):
            H, hd = HEADS[L]
            HD = H * hd
            MT, hpm, G = HD // P, P // hd, H // 4
            w = warena[(2 * L) % 2]
            w.reset()
            scratch.reset()
            v = dict(H=H, hd=hd, HD=HD, MT=MT, hpm=hpm, G=G)
            pre = f"L{L}_xattn_"
            nm = dict(Wq="wq", Wk="wk", Wv="wv", Wo="wo") if L == 2 else dict(Wq="Wq", Wk="Wk", Wv="Wv", Wo="Wo")
            if L == 1:
                nm["Wo"] = "Wout"
            ld = []
            v["Wq"] = w.take((DK, HD))
            v["Wk"] = w.take((2, HD))
            v["Wv"] = w.take((2, HD))
            v["Wo"] = w.take((MT, D))
            ld += ctxw(A[pre + nm["Wk"]], v["Wk"])
            ld += ctxw(A[pre + nm["Wv"]], v["Wv"])
            ld.append((v["Wq"], kin(A[pre + nm["Wq"]])))
            if L == 2:
                v["bq"], v["bk"], v["bv"], v["bo"] = w.take((DK,)), w.take((DK,)), w.take((HD,)), w.take((D,))
                ld += [(v["bq"], col(A[pre + "bq"], DK)), (v["bk"], col(A[pre + "bk"], DK)),
                       (v["bv"], row(A[pre + "bv"], HD)), (v["bo"], row(A[pre + "bo"], D))]
            if L == 1:
                v["bo"] = w.take((D,))
                ld.append((v["bo"], row(A[pre + "bout"], D)))
            if L == 3:
                for k, s in (("bq", "bq"), ("bk", "bk"), ("bv", "bv"), ("bo", "bo"), ("lg", "ln_gamma"), ("lb", "ln_beta")):
                    v[k] = w.take((D,))
                    ld.append((v[k], row(A[pre + s], D)))
            ld.append((v["Wo"], kin(A[pre + nm["Wo"]]) if MT == 2 else
                       A[pre + nm["Wo"]].rearrange("(k p) n -> p k n", p=P)))
            if L == 0:
                v["m8"] = w.take((B * M,), U8)
                ld.append((v["m8"], bc(A["mask_BxS2_bf1"].rearrange("(o b) k -> o (b k)", o=1), (P, B * M))))
                v["m01"] = w.take((B * M,))
                v["mb"] = w.take((B, M), BF16)
            v["Y"] = scratch.take((NT, D))
            v["yT"] = scratch.take((DK, T))
            v["QT"] = scratch.take((MT, T))
            v["Kz"] = scratch.take((MT * B, hpm, M))
            v["Kr"] = scratch.take((MT * B, hpm, 32))
            v["V"] = scratch.take((B, H, hd + 1))
            v["Vr"] = scratch.take((B, G, 4, hd + 1))
            v["KTs"] = scratch.take((MT, B * M))
            v["NPT"] = 2 if L in (1, 3) else 3
            v["PT"] = scratch.take((v["NPT"], 5, CH))
            v["O"] = scratch.take((2, TPC, HD)) if L != 3 else scratch.take((1, TPC, HD))
            v["NO"] = 2 if L != 3 else 1
            v["rden"] = scratch.take((2, 16))
            v["mx"] = scratch.take((NT, H))
            v["negm"] = scratch.take((NC, CH), BF16)
            if L == 0:
                ctxN = scratch.take((2 * B, CD))
                v["sel"] = scratch.take((B * H, P), BF16)
                v["selr"] = scratch.take((B * 4, 4, 32), BF16)
            v["gbo"] = scratch.take((D,))
            if L == 3:
                v["Qp"] = scratch.take((NT, D))
                v["ss"] = scratch.take((NT + 4,))
                v["rs"] = scratch.take((NT + 4,))
                v["Kp"] = scratch.take((4, D))
                v["gb"] = scratch.take((D,))
                v["junk"] = scratch.take((D,))
            ph.append(v)
            loads.append(ld)

            w = warena[1]
            w.reset()
            scratch.reset()
            pre = f"L{L}_ffn_"
            v = dict()
            ld = []
            v["Y"] = scratch.take((NT, D))
            if L != 1:
                v["yT"] = scratch.take((DK, T))
            if L == 0:
                v["w1"], v["w2"], v["w3"], v["w4"] = w.take((DK, 256)), w.take((DK, 128)), w.take((64,)), w.take((1,))
                v["b1"], v["b2"], v["b3"], v["b4"] = w.take((DK,)), w.take((1,)), w.take((1,)), w.take((1,))
                v["g1"], v["g2"], v["g3"] = w.take((DK, 128)), w.take((64,)), w.take((1,))
                v["gb1"], v["gb2"], v["gb3"], v["ar"] = w.take((1,)), w.take((1,)), w.take((1,)), w.take((1,))
                o1 = lambda a: a.rearrange("(p o) -> p o", o=1)
                ld += [(v["g1"], kin(A[pre + "gc_w1"])), (v["g2"], A[pre + "gc_w2"]), (v["g3"][0:64], A[pre + "gc_w3"]),
                       (v["gb1"], o1(A[pre + "gc_b1"])), (v["gb2"][0:64], o1(A[pre + "gc_b2"])),
                       (v["gb3"], bc(o1(A[pre + "gc_b3"]), (P, 1))),
                       (v["w1"], kin(A[pre + "cn_w1"])), (v["w2"], kin(A[pre + "cn_w2"])),
                       (v["w3"], A[pre + "cn_w3"]), (v["w4"][0:64], A[pre + "cn_w4"]),
                       (v["b1"], col(A[pre + "cn_b1"], DK)), (v["b2"], o1(A[pre + "cn_b2"])),
                       (v["b3"][0:64], o1(A[pre + "cn_b3"])), (v["b4"], bc(o1(A[pre + "cn_b4"]), (P, 1))),
                       (v["ar"], bc(o1(A[pre + "adaptive_range"]), (P, 1)))]
                v["w4r"], v["g3r"] = scratch.take((P,)), scratch.take((P,))
                v["yS"] = scratch.take((DK, T))
                v["h1"] = scratch.take((DK, T))
                v["h2"] = scratch.take((T,))
                v["h3"] = scratch.take((T,))
                v["th"] = scratch.take((NC, CH))
                v["tmp"] = scratch.take((2, CH))
                v["msum"] = scratch.take((DK, NC))
                v["mean"] = scratch.take((DK, B))
                v["gh1"], v["gh2"], v["gt"] = scratch.take((B,)), scratch.take((B,)), scratch.take((B,))
                v["al"], v["be"] = scratch.take((1,)), scratch.take((B,))
                v["hb"] = scratch.take((2,))
            if L == 1:
                v["w1"], v["w2"] = w.take((FT1, D)), w.take((DK, F1))
                v["b1"] = w.take((FT1,))
                v["b2"] = w.take((D,))
                ld += [(v["w1"], A[pre + "w1"].rearrange("(f p) d -> p f d", p=P)),
                       (v["w2"], A[pre + "w2"].rearrange("(k p) f -> p k f", p=P)),
                       (v["b1"], col(A[pre + "b1"], FT1)), (v["b2"], row(A[pre + "b2"], D))]
                v["xi"] = scratch.take((NT, D), BF16)
                v["xT"] = scratch.take((DK, T), BF16)
                v["hi"] = scratch.t[:, 0:FT1 * T // 2].bitcast(BF16).rearrange("p (f t) -> p f t", f=FT1)
                assert scratch.at == FT1 * T // 2
                v["wi1"] = scratch.take((FT1, D), BF16)
                v["wi2"] = scratch.take((DK, F1), BF16)
                v["w1T"] = scratch.take((DK, F1), BF16)
                v["w2T"] = scratch.take((FT1, D), BF16)
                v["h"] = scratch.take((FT1, T))
                v["sw1"], v["iw1"] = scratch.take((FT1,)), scratch.take((FT1,))
                v["sw2"], v["iw2"] = scratch.take((DK,)), scratch.take((DK,))
                v["diag"] = scratch.take((DK, P))
                v["sw2r"] = scratch.take((D,))
                v["rowS"], v["rowT"], v["rowB"], v["rowI"] = (scratch.take((D,)) for _ in range(4))
                v["m"] = scratch.take((64,))
                v["sc"] = scratch.take((16,))
                v["sb1"], v["ib1"], v["bq1"] = scratch.take((FT1,)), scratch.take((FT1,)), scratch.take((FT1,))
                v["dn"] = scratch.take((2, 2, D))
                v["rnd"] = scratch.take((1,))
            if L >= 2:
                E = E2 if L == 2 else E3
                v["Wr"], v["br"] = w.take((DK, E)), w.take((E,))
                ld += [(v["Wr"], kin(A[pre + ("Wr" if L == 2 else "router_w")])),
                       (v["br"], row(A[pre + ("br" if L == 2 else "router_b")], E))]
                v["lg"], v["G"], v["oh"], v["pre"] = (scratch.take((NT, E)) for _ in range(4))
                v["oh2"] = scratch.take((NT, E))
                v["top"] = scratch.take((NT, 8))
                v["idx"] = scratch.take((NT, 8), U32)
                v["idf"] = scratch.take((NT, 8))
                v["r"] = scratch.take((12, NT))
                v["GT"] = scratch.take((T,))
            if L == 2:
                v["b1"], v["b2"] = w.take((E2, H2 // P)), w.take((D,))
                ld += [(v["b1"][:, e, :], A[pre + "b1"][e, :].rearrange("(m p) -> p m", p=P)) for e in range(E2)]
                ld += [(v["b2"][0:E2], A[pre + "b2"])]
                v["W1"] = scratch.take((3, DK, H2))
                v["W2"] = scratch.take((3, H2 // P, D))
                v["hT"] = scratch.take((3, H2 // P, CH))
            if L == 3:
                v["ohb"] = scratch.take((NT, E), BF16)
                v["ohs"] = scratch.take((NT, E), BF16)
                v["Wg"] = scratch.take((2, DK, F3))
                v["Wu"] = scratch.take((2, DK, F3))
                v["Wd"] = scratch.take((2, 3, D))
                v["sg"] = scratch.take((4, CH))
                v["hT"] = scratch.take((3 * 3, CH))
            ph.append(v)
            loads.append(ld)
        NPH = PHASES

        def lnorm(p, c):
            return NC * p + c + 1

        ATT = [("front", 0), ("front", 1), ("back", 0), ("front", 2), ("tail", 0), ("back", 1),
               ("front", 3), ("tail", 1), ("back", 2), ("tail", 2), ("back", 3), ("tail", 3)]
        UNITS = [(c, q) for c in range(NC) for q in range(2)]

        def expert_order(E):
            ups = [(e, c) for e in range(E) for c in range(NC)]
            o = []
            for i, u in enumerate(ups):
                o.append(("up",) + u)
                if i >= 1:
                    o.append(("down",) + ups[i - 1])
            o.append(("down",) + ups[-1])
            return o

        block = ctx.enter_context(nc.Block())

        @block.tensor
        def _(pe):
            def transpose_y(p, v, c):
                pe.wait_ge(ln_y, lnorm(p, c))
                for d in range(DK):
                    bk = RA.take(pe, p, "yT", c, d)
                    for i in range(TPC):
                        last = pe.transpose(bk[:, i * P:(i + 1) * P], v["Y"][:, TPC * c + i, d * P:(d + 1) * P], ident[:])
                    last.then_inc(RA.filled, 1)

            def attention(p, L):
                v = ph[p]
                H, hd, MT, hpm, G, HD = (v[k] for k in ("H", "hd", "MT", "hpm", "G", "HD"))
                pe.wait_ge(w_loaded[p], 16 * len(loads[p]))
                if L == 0:
                    pe.wait_ge(consts, NCONST)
                    pe.wait_ge(in_loaded, 16 * NIN)
                    for b in range(B):
                        bk = RA.take(pe, p, "ctx", b)
                        pe.transpose(bk[:, 0:P], ctxN[:, b, 0:P], ident[:])
                        pe.transpose(bk[:, P:M], ctxN[0:MR, B + b, 0:P], ident[0:MR, 0:MR])
                        pe.transpose(bk[0:CD - P, 160:160 + P], ctxN[:, b, P:CD], ident[:])
                        pe.transpose(bk[0:CD - P, 160 + P:160 + M], ctxN[0:MR, B + b, P:CD],
                                     ident[0:MR, 0:MR]).then_inc(RA.filled, 1)
                    pe.wait_ge(RA.read, RA.n(p, "ctx", B - 1))
                if L < 3:
                    for m in range(MT):
                        bk = RB.take(pe, p, "k", m)
                        pe.matmul(bk[:, 0:B * M], v["Wk"][:, 0, m * P:(m + 1) * P], ctxT[:, 0, :], start=True, stop=False)
                        pe.matmul(bk[:, 0:B * M], v["Wk"][0:CD - P, 1, m * P:(m + 1) * P], ctxT[0:CD - P, 1, :],
                                  start=False, stop=True).then_inc(RB.filled, 1)

                def ctx_rows(kind, w):
                    for b in range(B):
                        for s, (k0, kn) in enumerate(((0, P), (P, MR))):
                            bk = RB.take(pe, p, kind, b, s)
                            o = b * M + k0
                            pe.matmul(bk[0:kn, 0:HD], ctxT[:, 0, o:o + kn], w[:, 0, :], start=True, stop=False)
                            pe.matmul(bk[0:kn, 0:HD], ctxT[0:CD - P, 1, o:o + kn], w[0:CD - P, 1, :],
                                      start=False, stop=True).then_inc(RB.filled, 1)

                ctx_rows("v", v["Wv"])
                if L == 3:
                    ctx_rows("kp", v["Wk"])
                    pe.wait_ge(kn_made, 1)
                    for m in range(MT):
                        bk = RB.take(pe, p, "k", m)
                        for b in range(B):
                            pe.transpose(bk[:, b * M:b * M + P], v["Kp"][:, 2 * b, m * P:(m + 1) * P], ident[:])
                            last = pe.transpose(bk[:, b * M + P:(b + 1) * M], v["Kp"][0:MR, 2 * b + 1, m * P:(m + 1) * P],
                                                ident[0:MR, 0:MR])
                        last.then_inc(RB.filled, 1)
                for what, c in ATT:
                    b = c // CPB
                    cs = slice(c * CH, (c + 1) * CH)
                    if what == "front":
                        transpose_y(p, v, c)
                        pe.wait_ge(RA.read, RA.n(p, "yT", c, DK - 1))
                        if L == 3:
                            for q in range(2):
                                bk = RB.take(pe, p, "qp", c, q)
                                for i in range(2):
                                    t = (2 * c + q) * 2 + i
                                    for k in range(DK):
                                        last = pe.matmul(bk[:, i * D:(i + 1) * D], v["yT"][:, k, t * P:(t + 1) * P],
                                                         v["Wq"][:, k, :], start=k == 0, stop=k == DK - 1)
                                last.then_inc(RB.filled, 1)
                            pe.wait_ge(qn_made, c + 1)
                            for m in range(MT):
                                bk = RA.take(pe, p, "q", c, m)
                                for i in range(TPC):
                                    last = pe.transpose(bk[:, i * P:(i + 1) * P],
                                                        v["Y"][:, TPC * c + i, m * P:(m + 1) * P], ident[:])
                                last.then_inc(RA.filled, 1)
                            continue
                        for m in range(MT):
                            bk = RA.take(pe, p, "q", c, m)
                            for k in range(DK):
                                last = pe.matmul(bk[:], v["Wq"][:, k, m * P:(m + 1) * P], v["yT"][:, k, cs],
                                                 start=k == 0, stop=k == DK - 1)
                            last.then_inc(RA.filled, 1)
                        pe.wait_ge(RA.read, RA.n(p, "q", c, MT - 1))
                        pe.wait_ge(kz_made, sum(B * ph[2 * l]["MT"] for l in range(L + 1)))
                        if L == 0:
                            pe.wait_ge(mb_made, 1)
                        for i in range(TPC):
                            q0 = c * CH + i * P
                            for m in range(MT):
                                for h0 in range(0, hpm, 3):
                                    hn = min(3, hpm - h0)
                                    bk = RB.take(pe, p, "mxs", c, i, m, h0)
                                    last = pe.matmul(bk[:, 0:hn * M], v["QT"][:, m, q0:q0 + P],
                                                     v["Kz"][:, m * B + b, h0:h0 + hn, :].rearrange("p h k -> p (h k)"),
                                                     start=True, stop=L > 0)
                                    if L == 0:
                                        for j in range(hn):
                                            last = pe.matmul(bk[:, j * M:(j + 1) * M], onesb[64:65, :], v["mb"][64:65, b, :],
                                                             start=False, stop=j == hn - 1)
                                    last.then_inc(RB.filled, 1)
                    elif what == "back":
                        pe.wait_ge(kr_made, sum(B * ph[2 * l]["MT"] for l in range(L + 1)))
                        if L == 3:
                            pe.wait_ge(RA.read, RA.n(p, "q", c, MT - 1))
                            pe.wait_ge(kz_made, sum(B * ph[2 * l]["MT"] for l in range(L + 1)))
                        pe.wait_ge(v_made, 4 * (L + 1))
                        if L < 3:
                            pe.wait_ge(RB.read, RB.n(p, "mxs", c, TPC - 1, MT - 1, (hpm - 1) // 3 * 3))
                            bk = RB.take(pe, p, "mx", c)
                            for i in range(TPC):
                                last = pe.transpose(bk[0:H, i * P:(i + 1) * P], v["mx"][:, TPC * c + i, :], ident[:])
                            last.then_inc(RB.filled, 1)
                        if L == 0:
                            pe.wait_ge(sel0_made, 1)
                        KM = 65 if L == 0 else 64
                        for g in range(G + 1):
                            if g < G:
                                for j in range(4):
                                    h = 4 * g + j
                                    bk = RC.take(pe, p, "s", c, g, j)
                                    last = pe.matmul(bk[:], v["Kz"][:, (h // hpm) * B + b, h % hpm, 0:P], v["QT"][:, h // hpm, cs],
                                                     start=True, stop=L == 3)
                                    if L < 3:
                                        if g == 0 and j == 0:
                                            pe.wait_ge(RB.read, RB.n(p, "mx", c))
                                        s = v["sel"][0:KM, b * H + h, :] if L == 0 else sel[0:KM, h, :]
                                        last = pe.matmul(bk[:], s, v["negm"][0:KM, c, :], start=False, stop=True)
                                    last.then_inc(RC.filled, 1)
                                bk = RC.take(pe, p, "s", c, g, 4)
                                mts = sorted({(4 * g + j) // hpm for j in range(4)})
                                if L < 3:
                                    s = v["selr"][0:KM, b * 4 + g, :, :] if L == 0 else selr[0:KM, g, :, :]
                                    pe.matmul(bk[:], s.rearrange("p j k -> p (j k)"), v["negm"][0:KM, c, :],
                                              start=True, stop=False)
                                for m in mts:
                                    n = P // len(mts)
                                    o = (m - mts[0]) * n
                                    h0 = (4 * g) % hpm
                                    last = pe.matmul(bk[o:o + n, :],
                                                     v["Kr"][:, m * B + b, h0:h0 + n // 32, :].rearrange("p h k -> p (h k)"),
                                                     v["QT"][:, m, cs], start=L == 3, stop=True)
                                last.then_inc(RC.filled, 1)
                            if g > 0:
                                gg = g - 1
                                slot = (c * G + gg) % v["NPT"]
                                pe.wait_ge(RC.read, RC.n(p, "s", c, gg, 4))
                                w = hd + 1
                                for i in range(TPC):
                                    if hd == 16:
                                        bk = RB.take(pe, p, "av", c, gg) if i == 0 else bk
                                        o = i * 4 * w
                                    else:
                                        bk = RB.take(pe, p, "av", c, gg, i)
                                        o = 0
                                    qs = slice(i * P, (i + 1) * P)
                                    pe.matmul(bk[:, o:o + 4 * w], v["PT"][:, slot, 4, qs],
                                              v["Vr"][:, b, gg, :, :].rearrange("p j d -> p (j d)"), start=True, stop=False)
                                    for j in range(4):
                                        last = pe.matmul(bk[:, o + j * w:o + (j + 1) * w], v["PT"][:, slot, j, qs],
                                                         v["V"][:, b, 4 * gg + j, :], start=False, stop=j == 3)
                                    if hd != 16 or i == TPC - 1:
                                        last.then_inc(RB.filled, 1)
                    else:
                        if hd == 16:
                            pe.wait_ge(RB.read, RB.n(p, "av", c, G - 1))
                        else:
                            pe.wait_ge(RB.read, RB.n(p, "av", c, G - 1, TPC - 1))
                        for m in range(MT):
                            bk = RA.take(pe, p, "oT", c, m)
                            for i in range(TPC):
                                last = pe.transpose(bk[:, i * P:(i + 1) * P], v["O"][:, c % v["NO"], i, m * P:(m + 1) * P], ident[:])
                            last.then_inc(RA.filled, 1)
                        pe.wait_ge(RA.read, RA.n(p, "oT", c, MT - 1))
                        for q in range(2):
                            bk = RB.take(pe, p, "out", c, q)
                            for i in range(2):
                                t = (2 * c + q) * 2 + i
                                for m in range(MT):
                                    last = pe.matmul(bk[:, i * D:(i + 1) * D], v["QT"][:, m, t * P:(t + 1) * P],
                                                     v["Wo"][:, m, :], start=m == 0, stop=m == MT - 1)
                            last.then_inc(RB.filled, 1)

            def coupling(p):
                v = ph[p]
                pe.wait_ge(w_loaded[p], 16 * len(loads[p]))
                for c in range(NC):
                    transpose_y(p, v, c)
                pe.wait_ge(gc_ready, 1)
                bk = RA.take(pe, p, "g1")
                for k in range(DK):
                    last = pe.matmul(bk[:, 0:B], v["g1"][:, k, :], v["mean"][:, k, :], start=k == 0, stop=k == DK - 1)
                last.then_inc(RA.filled, 1)
                pe.wait_ge(RA.read, RA.n(p, "g1"))
                bk = RA.take(pe, p, "g2")
                pe.matmul(bk[0:64, 0:B], v["g2"][:], v["gh1"][:], start=True, stop=True).then_inc(RA.filled, 1)
                pe.wait_ge(RA.read, RA.n(p, "g2"))
                bk = RA.take(pe, p, "g3")
                pe.matmul(bk[:, 0:B], v["g3r"][0:64], v["gh2"][0:64], start=True, stop=True).then_inc(RA.filled, 1)
                st = [v["yT"], v["yS"]]
                for r in range(3):
                    for c in range(NC):
                        cs = slice(c * CH, (c + 1) * CH)
                        if r:
                            pe.wait_ge(state_made, NC * (r - 1) + c + 1)
                        for m in range(DK):
                            bk = RC.take(pe, p, r, "l1", c, m)
                            for k in range(DK):
                                last = pe.matmul(bk[:], v["w1"][:, k, m * P:(m + 1) * P], st[r % 2][:, k, cs],
                                                 start=k == 0, stop=k == DK - 1)
                            last.then_inc(RC.filled, 1)
                    for c in range(NC):
                        cs = slice(c * CH, (c + 1) * CH)
                        pe.wait_ge(RC.read, RC.n(p, r, "l1", c, DK - 1))
                        bk = RC.take(pe, p, r, "l2", c)
                        for k in range(DK):
                            last = pe.matmul(bk[:], v["w2"][:, k, :], v["h1"][:, k, cs], start=k == 0, stop=k == DK - 1)
                        last.then_inc(RC.filled, 1)
                    for c in range(NC):
                        cs = slice(c * CH, (c + 1) * CH)
                        pe.wait_ge(RC.read, RC.n(p, r, "l2", c))
                        bk = RC.take(pe, p, r, "l3", c)
                        pe.matmul(bk[0:64, :], v["w3"][:], v["h2"][:, cs], start=True, stop=True).then_inc(RC.filled, 1)
                    for c in range(NC):
                        cs = slice(c * CH, (c + 1) * CH)
                        pe.wait_ge(RC.read, RC.n(p, r, "l3", c))
                        bk = RC.take(pe, p, r, "l4", c)
                        pe.matmul(bk[:], v["w4r"][0:64], v["h3"][0:64, cs], start=True, stop=True).then_inc(RC.filled, 1)
                for c in range(NC):
                    pe.wait_ge(state_made, NC * 2 + c + 1)
                    for q in range(2):
                        bk = RB.take(pe, p, "fin", c, q)
                        for i in range(2):
                            t = (2 * c + q) * 2 + i
                            for k in range(DK):
                                last = pe.transpose(bk[:, i * D + k * P:i * D + (k + 1) * P], st[1][:, k, t * P:(t + 1) * P], ident[:])
                        last.then_inc(RB.filled, 1)

            def quantised(p):
                v = ph[p]
                pe.wait_ge(wq_made, 1)
                for d in range(DK):
                    bk = RA.take(pe, p, "w1T", d)
                    o = bk[:].bitcast(BF16)
                    for f in range(FT1):
                        last = pe.transpose(o[:, f * P:(f + 1) * P], v["wi1"][:, f, d * P:(d + 1) * P], identb[:])
                    last.then_inc(RA.filled, 1)
                for d in range(DK):
                    bk = RA.take(pe, p, "w2T", d)
                    o = bk[:].bitcast(BF16)
                    for f in range(FT1):
                        last = pe.transpose(o[:, f * P:(f + 1) * P], v["wi2"][:, d, f * P:(f + 1) * P], identb[:])
                    last.then_inc(RA.filled, 1)
                pe.wait_ge(diag_made, 1)
                bk = RB.take(pe, p, "sw2r")
                for d in range(DK):
                    last = pe.matmul(bk[:, d * P:(d + 1) * P], ones[:], v["diag"][:, d, :], start=True, stop=True)
                last.then_inc(RB.filled, 1)
                for c in range(NC):
                    pe.wait_ge(xi_made, c + 1)
                    bk = RA.take(pe, p, "xT", c)
                    o = bk[:].bitcast(BF16)
                    for d in range(DK):
                        for i in range(TPC):
                            last = pe.transpose(o[:, d * CH + i * P:d * CH + (i + 1) * P],
                                                v["xi"][:, TPC * c + i, d * P:(d + 1) * P], identb[:])
                    last.then_inc(RA.filled, 1)
                for c in range(NC):
                    cs = slice(c * CH, (c + 1) * CH)
                    pe.wait_ge(RA.read, RA.n(p, "xT", c))
                    for f in range(FT1):
                        bk = RC.take(pe, p, "up", c, f)
                        for k in range(DK):
                            last = pe.matmul(bk[:], v["w1T"][:, k, f * P:(f + 1) * P], v["xT"][:, k, cs], start=k == 0, stop=k == DK - 1)
                        last.then_inc(RC.filled, 1)
                for c in range(NC):
                    pe.wait_ge(hi_made, c + 1)
                    for q in range(2):
                        bk = RB.take(pe, p, "dn", c, q)
                        for i in range(2):
                            t = (2 * c + q) * 2 + i
                            for f in range(FT1):
                                last = pe.matmul(bk[:, i * D:(i + 1) * D], v["hi"][:, f, t * P:(t + 1) * P], v["w2T"][:, f, :],
                                                 start=f == 0, stop=f == FT1 - 1)
                        last.then_inc(RB.filled, 1)

            def experts(p, L):
                v = ph[p]
                E = E2 if L == 2 else E3
                pe.wait_ge(w_loaded[p], 16 * len(loads[p]))
                for c in range(NC):
                    transpose_y(p, v, c)
                    pe.wait_ge(RA.read, RA.n(p, "yT", c, DK - 1))
                    bk = RB.take(pe, p, "lg", c)
                    for i in range(TPC):
                        t = TPC * c + i
                        for k in range(DK):
                            last = pe.matmul(bk[:, i * E:(i + 1) * E], v["yT"][:, k, t * P:(t + 1) * P], v["Wr"][:, k, :],
                                             start=k == 0, stop=k == DK - 1)
                    last.then_inc(RB.filled, 1)
                if L == 3:
                    pe.wait_ge(oh_made, 1)
                    bk = RB.take(pe, p, "pos")
                    for t in range(NT):
                        pe.matmul(bk[:, t * E:(t + 1) * E], before[:], v["ohb"][:, t, :], start=True, stop=t == 0)
                        if t:
                            last = pe.matmul(bk[:, t * E:(t + 1) * E], onesb[:], v["ohs"][:, t, :], start=False, stop=True)
                    last.then_inc(RB.filled, 1)
                if L == 2:
                    pe.wait_ge(g_made, 1)
                    for c in range(NC):
                        bk = RA.take(pe, p, "gT", c)
                        for i in range(TPC):
                            last = pe.transpose(bk[0:E, i * P:(i + 1) * P], v["G"][:, TPC * c + i, :], ident[:])
                        last.then_inc(RA.filled, 1)
                    for c in range(NC):
                        pe.wait_ge(RA.read, RA.n(p, "gT", c))
                        for q in range(2):
                            bk = RB.take(pe, p, "b2", c, q)
                            for i in range(2):
                                t = (2 * c + q) * 2 + i
                                last = pe.matmul(bk[:, i * D:(i + 1) * D], v["GT"][0:E, t * P:(t + 1) * P], v["b2"][0:E, :],
                                                 start=True, stop=True)
                            last.then_inc(RB.filled, 1)
                EE = E if L == 2 else E + 1
                HT = H2 // P if L == 2 else 3
                NW = 3 if L == 2 else 2
                for n, (what, e, c) in enumerate(expert_order(EE)):
                    s = e % NW
                    hs = (e * NC + c) % 3
                    cs = slice(c * CH, (c + 1) * CH)
                    if what == "up":
                        if c == 0:
                            pe.wait_ge(ew_loaded[L][s], 16 * EWN[L] * (e // NW + 1))
                        for m in range(HT):
                            if L == 2:
                                bk = RC.take(pe, p, "up", e, c, m)
                                for k in range(DK):
                                    last = pe.matmul(bk[:], v["W1"][:, s, k, m * P:(m + 1) * P], v["yT"][:, k, cs],
                                                     start=k == 0, stop=k == DK - 1)
                                last.then_inc(RC.filled, 1)
                            else:
                                fn = F3T[m]
                                for ring, w, key in ((RA, v["Wg"], "gate"), (RB, v["Wu"], "up")):
                                    bk = ring.take(pe, p, key, e, c, m)
                                    for k in range(DK):
                                        last = pe.matmul(bk[0:fn, :], w[:, s, k, m * P:m * P + fn], v["yT"][:, k, cs],
                                                         start=k == 0, stop=k == DK - 1)
                                    last.then_inc(ring.filled, 1)
                    else:
                        if L == 2:
                            pe.wait_ge(RC.read, RC.n(p, "up", e, c, HT - 1))
                        else:
                            pe.wait_ge(RB.read, RB.n(p, "up", e, c, HT - 1))
                        for q in range(2):
                            bk = RB.take(pe, p, "dn", e, c, q)
                            for i in range(2):
                                tt = q * 2 + i
                                for m in range(HT):
                                    fn = P if L == 2 else F3T[m]
                                    if L == 2:
                                        lh, rh = v["hT"][:, hs, m, tt * P:(tt + 1) * P], v["W2"][:, s, m, :]
                                    else:
                                        lh, rh = v["hT"][0:fn, hs * 3 + m, tt * P:(tt + 1) * P], v["Wd"][0:fn, s, m, :]
                                    last = pe.matmul(bk[:, i * D:(i + 1) * D], lh, rh, start=m == 0, stop=m == HT - 1)
                            last.then_inc(RB.filled, 1)

            for p in range(NPH):
                L = p // 2
                if p:
                    pe.wait_ge(phase_over, p)
                if p % 2 == 0:
                    attention(p, L)
                elif L == 0:
                    coupling(p)
                elif L == 1:
                    quantised(p)
                else:
                    experts(p, L)

        @block.scalar
        def _(act):
            st = Steps(act, act_st)
            act.wait_ge(in_loaded, 16 * NIN)
            act.activation(tg[:], gates[:], ACT.Tanh).then_inc(tg_made, 1)

            def yT(p, v, c):
                for d in range(DK):
                    bk = RA.get(act, p, "yT", c, d)
                    act.activation(v["yT"][:, d, c * CH:(c + 1) * CH], bk[:], ACT.Copy).then_inc(RA.read, 1)

            def attention(p, L):
                v = ph[p]
                H, hd, MT, hpm, G, HD = (v[k] for k in ("H", "hd", "MT", "hpm", "G", "HD"))
                if L == 0:
                    for b in range(B):
                        bk = RA.get(act, p, "ctx", b)
                        act.activation(ctxT[:, 0, b * M:(b + 1) * M], bk[:, 0:M], ACT.Copy)
                        act.activation(ctxT[0:CD - P, 1, b * M:(b + 1) * M], bk[0:CD - P, 160:160 + M], ACT.Copy)\
                           .then_inc(RA.read, 1)
                if L == 2:
                    act.wait_ge(w_loaded[p], 16 * len(loads[p]))
                if L == 3:
                    act.wait_ge(kn_clear, 1)
                    for i in range(4):
                        n = P if i % 2 == 0 else MR
                        act.wait_ge(RB.read, RB.n(p, "kp", i // 2, i % 2))
                        if i:
                            st.wait()
                        st.did(act.activation(v["junk"][0:n], v["Kp"][0:n, i, :], ACT.Square,
                                              accum_out=v["ss"][0:n, NT + i:NT + i + 1]))
                    st.wait()
                    act.sem_inc(kss_made, 1)
                for what, c in ATT:
                    cs = slice(c * CH, (c + 1) * CH)
                    if what == "front":
                        yT(p, v, c)
                        if L == 3:
                            act.wait_ge(RB.read, RB.n(p, "qp", c, 1))
                            for i in range(TPC):
                                t = TPC * c + i
                                st.wait()
                                ins = act.activation(v["junk"][:], v["Qp"][:, t, :], ACT.Square, accum_out=v["ss"][:, t:t + 1])
                                st.did(ins)
                            st.wait()
                            act.sem_inc(qss_made, 1)
                        for m in range(MT):
                            bk = RA.get(act, p, "q", c, m)
                            if L == 2:
                                ins = act.activation(v["QT"][:, m, cs], bk[:], ACT.Identity, bias=v["bq"][:, m:m + 1])
                            else:
                                ins = act.activation(v["QT"][:, m, cs], bk[:], ACT.Copy)
                            ins.then_inc(RA.read, 1)
                    elif what == "back":
                        for g in range(G):
                            n = c * G + g
                            if n >= v["NPT"]:
                                pc, pg = divmod(n - v["NPT"], G)
                                act.wait_ge(RB.filled, RB.n(p, "av", pc, pg) if hd == 16 else RB.n(p, "av", pc, pg, TPC - 1))
                            for j in range(5):
                                bk = RC.get(act, p, "s", c, g, j)
                                act.activation(v["PT"][:, n % v["NPT"], j, :], bk[:], ACT.Exp, scale=float(hd) ** -0.5)\
                                   .then_inc(RC.read, 1)
                    else:
                        for m in range(MT):
                            bk = RA.get(act, p, "oT", c, m)
                            act.activation(v["QT"][:, m, cs], bk[:], ACT.Copy).then_inc(RA.read, 1)

            def coupling(p):
                v = ph[p]
                act.wait_ge(w_loaded[p], 16 * len(loads[p]))
                for c in range(NC):
                    yT(p, v, c)
                bk = RA.get(act, p, "g1")
                act.activation(v["gh1"][:], bk[:, 0:B], ACT.Gelu, bias=v["gb1"][:]).then_inc(RA.read, 1)
                bk = RA.get(act, p, "g2")
                act.activation(v["gh2"][0:64], bk[0:64, 0:B], ACT.Gelu, bias=v["gb2"][0:64]).then_inc(RA.read, 1)
                bk = RA.get(act, p, "g3")
                act.activation(v["gt"][:], bk[:, 0:B], ACT.Tanh, bias=v["hb"][:, 1:2], scale=0.5).then_inc(RA.read, 1)
                for r in range(3):
                    for c in range(NC):
                        for m in range(DK):
                            bk = RC.get(act, p, r, "l1", c, m)
                            act.activation(v["h1"][:, m, c * CH:(c + 1) * CH], bk[:], ACT.Gelu, bias=v["b1"][:, m:m + 1])\
                               .then_inc(RC.read, 1)
                    for c in range(NC):
                        bk = RC.get(act, p, r, "l2", c)
                        act.activation(v["h2"][:, c * CH:(c + 1) * CH], bk[:], ACT.Gelu, bias=v["b2"][:]).then_inc(RC.read, 1)
                    for c in range(NC):
                        bk = RC.get(act, p, r, "l3", c)
                        act.activation(v["h3"][0:64, c * CH:(c + 1) * CH], bk[0:64, :], ACT.Gelu, bias=v["b3"][0:64])\
                           .then_inc(RC.read, 1)
                    for c in range(NC):
                        bk = RC.get(act, p, r, "l4", c)
                        act.activation(v["th"][:, c, :], bk[:], ACT.Tanh, bias=v["hb"][:, 0:1], scale=0.5).then_inc(RC.read, 1)

            def quantised(p):
                v = ph[p]
                for d in range(DK):
                    bk = RA.get(act, p, "w1T", d)
                    act.activation(v["w1T"][:, d, :], bk[:].bitcast(BF16), ACT.Copy).then_inc(RA.read, 1)
                for d in range(DK):
                    bk = RA.get(act, p, "w2T", d)
                    act.activation(v["w2T"][:, :, d * P:(d + 1) * P],
                                   bk[:].bitcast(BF16).rearrange("p (f j) -> p f j", j=P), ACT.Copy).then_inc(RA.read, 1)
                for c in range(NC):
                    bk = RA.get(act, p, "xT", c)
                    act.activation(v["xT"][:, :, c * CH:(c + 1) * CH],
                                   bk[:].bitcast(BF16).rearrange("p (d j) -> p d j", d=DK), ACT.Copy).then_inc(RA.read, 1)
                act.wait_ge(hscale_made, 1)
                for c in range(NC):
                    for f in range(FT1):
                        bk = RC.get(act, p, "up", c, f)
                        act.activation(v["h"][:, f, c * CH:(c + 1) * CH], bk[:], ACT.Relu,
                                       bias=v["bq1"][:, f:f + 1], scale=v["sb1"][:, f:f + 1]).then_inc(RC.read, 1)

            def experts(p, L):
                v = ph[p]
                act.wait_ge(w_loaded[p], 16 * len(loads[p]))
                for c in range(NC):
                    yT(p, v, c)
                act.wait_ge(ex_ready, L - 1)
                if L == 2:
                    act.activation(v["r"][:, 1, :], v["r"][:, 0, :], ACT.Exp).then_inc(ex_made, 1)
                    for c in range(NC):
                        bk = RA.get(act, p, "gT", c)
                        act.activation(v["GT"][0:E2, c * CH:(c + 1) * CH], bk[0:E2, :], ACT.Copy).then_inc(RA.read, 1)
                    for what, e, c in expert_order(E2):
                        if what == "up":
                            for m in range(H2 // P):
                                bk = RC.get(act, p, "up", e, c, m)
                                act.activation(v["hT"][:, (e * NC + c) % 3, m, :], bk[:], ACT.Relu,
                                               bias=v["b1"][:, e, m:m + 1]).then_inc(RC.read, 1)
                else:
                    act.activation(v["pre"][:], v["lg"][:], ACT.Exp).then_inc(ex_made, 1)
                    items = [(e, c, m) for what, e, c in expert_order(E3 + 1) if what == "up" for m in range(3)]
                    for n, (e, c, m) in enumerate(items):
                        fn = F3T[m]
                        if n >= 4:
                            act.wait_ge(RB.read, RB.n(p, "up", *items[n - 4]))
                        bk = RA.get(act, p, "gate", e, c, m)
                        act.activation(v["sg"][0:fn, n % 4, :], bk[0:fn, :], ACT.Silu).then_inc(RA.read, 1)

            for p in range(NPH):
                L = p // 2
                if p:
                    act.wait_ge(phase_over, p)
                if p % 2 == 0:
                    attention(p, L)
                elif L == 0:
                    coupling(p)
                elif L == 1:
                    quantised(p)
                else:
                    experts(p, L)

        @block.gpsimd
        def _(pool):
            st = Steps(pool, pool_st)
            for a in (ident, identb, sel, selr):
                st.did(pool.memset(a[:], 0.0))
            for a in (hmask[16], hmask[64], before, ones, sgn):
                st.did(pool.memset(a[:], 1.0))
            st.did(pool.memset(nhalf[:], -0.5))
            st.did(pool.memset(onesb[:], 1.0))
            st.wait()
            for a in (ident, identb):
                st.did(pool.affine_select(out=a[:], in_=a[:], compare_op=ALU.not_equal, fill=1.0, base=0,
                                          pattern=[[-1, P]], channel_multiplier=1))
            st.did(pool.affine_select(out=before[:], in_=before[:], compare_op=ALU.is_gt, fill=0.0, base=0,
                                      pattern=[[1, P]], channel_multiplier=-1))
            st.did(pool.affine_select(out=sgn[:], in_=sgn[:], compare_op=ALU.is_gt, fill=-1.0, base=64,
                                      pattern=[[0, 1]], channel_multiplier=-1))
            for hd, n in ((16, 8), (64, 2)):
                a = hmask[hd]
                st.wait()
                st.did(pool.affine_select(out=a[:], in_=a[:], compare_op=ALU.is_ge, fill=0.0, base=0,
                                          pattern=[[-hd, n]], channel_multiplier=1))
                st.wait()
                st.did(pool.affine_select(out=a[:], in_=a[:], compare_op=ALU.is_ge, fill=0.0, base=hd - 1,
                                          pattern=[[hd, n]], channel_multiplier=-1))
            for base in (0, -32):
                st.wait()
                st.did(pool.affine_select(out=sel[:], in_=sel[:], compare_op=ALU.not_equal, fill=1.0, base=base,
                                          pattern=[[-1, 16], [0, P]], channel_multiplier=1))
                a = selr[:, :, :, 0:MR]
                st.did(pool.affine_select(out=a, in_=a, compare_op=ALU.not_equal, fill=1.0, base=base,
                                          pattern=[[-4, 4], [-1, 4], [0, MR]], channel_multiplier=1))
            st.did(pool.iota(iota[:], [[1, 16]], base=0, channel_multiplier=0, allow_small_or_imprecise_dtypes=True))
            st.wait()
            pool.sem_inc(consts, NCONST)

            def norm(p, v):
                for c in range(NC):
                    ts = slice(TPC * c, TPC * (c + 1))
                    pool.wait_ge(ln_stats, lnorm(p, c))
                    st.did(pool.tensor_scalar(rstd[:, ts], mv[:, ts, 1], 1e-5, None, ALU.add))
                    st.wait()
                    st.did(pool.tensor_tensor(rstd[:, ts], rstd[:, ts], nhalf[:, ts], ALU.pow))
                    st.wait()
                    for t in range(TPC * c, TPC * (c + 1)):
                        last = pool.tensor_scalar(v["Y"][:, t, :], X[:, t, :], mv[:, t, 0:1], rstd[:, t:t + 1],
                                                  ALU.subtract, ALU.mult)
                    last.then_inc(ln_y, 1)

            def add_row(row, made, n, p):
                pool.wait_ge(ln_y, lnorm(p, NC - 1))
                pool.wait_ge(made, n)
                for c in range(NC):
                    a = X[:, TPC * c:TPC * (c + 1), :]
                    last = pool.tensor_tensor(a, a, bc(row.unsqueeze(1), (P, TPC, D)), ALU.add)
                last.then_inc(xbias, 1)

            def attention(p, L):
                v = ph[p]
                H, hd, MT, hpm, G = (v[k] for k in ("H", "hd", "MT", "hpm", "G"))
                st.did(pool.memset(v["V"][:], 1.0))
                st.did(pool.memset(v["Vr"][:], 0.0))
                st.did(pool.memset(v["Kr"][:], 0.0))
                if L == 3:
                    st.did(pool.memset(v["ss"][:], 1.0))
                    st.did(pool.memset(v["Kp"][:], 0.0))
                else:
                    st.did(pool.memset(v["negm"][0:64], 0.0))
                    if L == 0:
                        st.wait()
                        st.did(pool.memset(v["negm"][64:65], 1.0))
                for j in range(4):
                    st.wait()
                    st.did(pool.memset(v["Vr"][32 * j:32 * j + MR, :, :, j, hd:hd + 1], 1.0))
                st.wait()
                pool.sem_inc(kv_clear, 1)
                if L == 3:
                    pool.sem_inc(kn_clear, 1)
                norm(p, v)
                if L == 3:
                    pool.wait_ge(kss_made, 1)
                    a = v["rs"][:, NT:NT + 4]
                    st.did(pool.tensor_scalar(a, v["ss"][:, NT:NT + 4], 1e-24, None, ALU.max))
                    st.wait()
                    st.did(pool.tensor_tensor(a, a, nhalf[:, 0:4], ALU.pow))
                    st.wait()
                    for i in range(4):
                        n = P if i % 2 == 0 else MR
                        st.did(pool.tensor_scalar(v["Kp"][0:n, i, :], v["Kp"][0:n, i, :], v["rs"][0:n, NT + i:NT + i + 1], None,
                                                  ALU.mult))
                    st.wait()
                    pool.sem_inc(kn_made, 1)
                base = sum(B * ph[2 * l]["MT"] for l in range(L))

                def last_keys():
                    for n in range(MT * B):
                        pool.wait_ge(kz_made, base + n + 1)
                        pool.tensor_copy(v["Kr"][:, n, :, 0:MR], v["Kz"][:, n, :, P:M]).then_inc(kr_made, 1)

                def queries(c):
                    ts = slice(TPC * c, TPC * (c + 1))
                    pool.wait_ge(qss_made, c + 1)
                    st.did(pool.tensor_scalar(v["rs"][:, ts], v["ss"][:, ts], 1e-24, None, ALU.max))
                    st.wait()
                    st.did(pool.tensor_tensor(v["rs"][:, ts], v["rs"][:, ts], nhalf[:, ts], ALU.pow))
                    st.wait()
                    for t in range(TPC * c, TPC * (c + 1)):
                        last = pool.tensor_scalar(v["Y"][:, t, :], v["Qp"][:, t, :], v["rs"][:, t:t + 1], None, ALU.mult)
                    last.then_inc(qn_made, 1)
                    pool.wait_ge(qn_made, c + 1)
                    a = v["Qp"][:, ts, :]
                    pool.tensor_tensor(a, a, bc(v["bo"][:].unsqueeze(1), (P, TPC, D)), ALU.add).then_inc(qbo_made, 1)

                def post(c):
                    ts = slice(TPC * c, TPC * (c + 1))
                    pool.wait_ge(post_stats, c + 1)
                    st.did(pool.tensor_scalar(rstd[:, ts], mv[:, ts, 1], 1e-5, None, ALU.add))
                    st.wait()
                    st.did(pool.tensor_tensor(rstd[:, ts], rstd[:, ts], nhalf[:, ts], ALU.pow))
                    st.wait()
                    for t in range(TPC * c, TPC * (c + 1)):
                        last = pool.tensor_scalar(v["Qp"][:, t, :], v["Qp"][:, t, :], mv[:, t, 0:1], rstd[:, t:t + 1],
                                                  ALU.subtract, ALU.mult)
                    last.then_inc(post_z, 1)

                if L != 3:
                    last_keys()
                if L in (1, 2):
                    add_row(v["gbo"][:], gbo_made, L, p)
                if L == 3:
                    queries(0)
                    last_keys()
                    queries(1)
                    add_row(v["gb"][:], gbo_made, L, p)
                    queries(2)
                    post(0)
                    queries(3)
                    for c in range(1, NC):
                        post(c)

            for p in range(NPH):
                L = p // 2
                v = ph[p]
                if p:
                    pool.wait_ge(phase_over, p)
                if p % 2 == 0:
                    attention(p, L)
                    continue
                norm(p, v)
                if L == 1:
                    for n in range(2):
                        pool.wait_ge(xmax_made, n + 1)
                        pool.partition_all_reduce(v["sc"][:, n:n + 1], v["m"][:, 60 + n:61 + n], P, RMAX).then_inc(xall_made, 1)
                    add_row(v["rowB"][:], rows_made, 1, p)

        @block.vector
        def _(dve):
            st = Steps(dve, dve_st)
            dve.wait_ge(in_loaded, 16 * NIN)
            dve.wait_ge(tg_made, 1)
            dve.wait_ge(consts, NCONST)

            def x_stats(p):
                for c in range(NC):
                    for t in range(TPC * c, TPC * (c + 1)):
                        st.did(dve.bn_stats(stats[:, t, :], X[:, t, :]))
                    st.wait()
                    for t in range(TPC * c, TPC * (c + 1)):
                        last = dve.bn_aggr(mv[:, t, :], stats[:, t, :])
                    last.then_inc(ln_stats, 1)

            def add_out(p, bk, q, scalar, end):
                a = X[:, 2 * q:2 * q + 2, :]
                return dve.scalar_tensor_tensor(a, bk[:].rearrange("p (t d) -> p t d", t=2), scalar, a, ALU.mult, ALU.add)

            def over(p):
                dve.wait_ge(RB.read, RB.emptied)
                dve.sem_inc(phase_over, 1)

            def attention(p, L):
                v = ph[p]
                H, hd, MT, hpm, G, HD = (v[k] for k in ("H", "hd", "MT", "hpm", "G", "HD"))
                dve.wait_ge(w_loaded[p], 16 * len(loads[p]))
                if L == 0:
                    st.did(dve.tensor_copy(v["m01"][:], v["m8"][:]))
                    dve.tensor_scalar(v["mb"][64:65].rearrange("p b k -> p (b k)"), v["m8"][64:65], -1.0, BIG,
                                      ALU.add, ALU.mult).then_inc(mb_made, 1)
                if L in (1, 2):
                    dve.tensor_scalar(v["gbo"][:], v["bo"][:], tg[:, L:L + 1], None, ALU.mult).then_inc(gbo_made, 1)
                if L == 3:
                    st.did(dve.tensor_scalar(v["lg"][:], v["lg"][:], tg[:, L:L + 1], None, ALU.mult))
                    dve.tensor_scalar(v["gb"][:], v["lb"][:], tg[:, L:L + 1], None, ALU.mult).then_inc(gbo_made, 1)
                x_stats(p)
                dve.wait_ge(kv_clear, L + 1)

                def keys():
                    for m in range(MT):
                        bk = RB.get(dve, p, "k", m)
                        if L == 2:
                            ins = dve.tensor_scalar(v["KTs"][:, m, :], bk[:, 0:B * M], v["bk"][:, m:m + 1], None, ALU.add)
                        elif L == 0:
                            ins = dve.tensor_tensor(v["KTs"][:, m, :], bk[:, 0:B * M], v["m01"][:], ALU.mult)
                        else:
                            ins = dve.tensor_copy(v["KTs"][:, m, :], bk[:, 0:B * M])
                        ins.then_inc(RB.read, 1)
                        dve.wait_ge(RB.read, RB.emptied)
                        for b in range(B):
                            dve.tensor_tensor(v["Kz"][:, m * B + b, :, :],
                                              bc(v["KTs"][:, m, b * M:(b + 1) * M].unsqueeze(1), (P, hpm, M)),
                                              bc(hmask[hd][:].unsqueeze(2), (P, hpm, M)), ALU.mult).then_inc(kz_made, 1)

                def values():
                    for b in range(B):
                        bk = RB.get(dve, p, "v", b, 0)
                        a = bk[:, 0:HD].rearrange("p (h d) -> p h d", d=hd)
                        o = v["V"][:, b, :, 0:hd]
                        if L >= 2:
                            ins = dve.tensor_tensor(o, a, v["bv"][:].rearrange("p (h d) -> p h d", d=hd), ALU.add)
                        else:
                            ins = dve.tensor_copy(o, a)
                        st.did(ins)
                        st.wait()
                        dve.sem_inc(RB.read, 1)
                        dve.sem_inc(v_made, 1)
                        bk = RB.get(dve, p, "v", b, 1)
                        a = bk[0:MR, 0:HD].rearrange("p (g j d) -> p g j d", j=4, d=hd)
                        for j in range(4):
                            o = v["Vr"][32 * j:32 * j + MR, b, :, j, 0:hd]
                            if L >= 2:
                                bv = v["bv"][0:MR].rearrange("p (g j d) -> p g j d", j=4, d=hd)[:, :, j, :]
                                ins = dve.tensor_tensor(o, a[:, :, j, :], bv, ALU.add)
                            else:
                                ins = dve.tensor_copy(o, a[:, :, j, :])
                            st.did(ins)
                        st.wait()
                        dve.sem_inc(RB.read, 1)
                        dve.sem_inc(v_made, 1)

                if L < 3:
                    keys()
                    if L == 0:
                        for b in range(B):
                            st.did(dve.tensor_copy(v["sel"][0:65, b * H:(b + 1) * H, :], sel[:]))
                            st.did(dve.tensor_copy(v["selr"][0:65, b * 4:(b + 1) * 4, :, :], selr[:]))
                        st.wait()
                        dve.wait_ge(mb_made, 1)
                        for b in range(B):
                            st.did(dve.tensor_copy(v["sel"][64:65, b * H:(b + 1) * H, :],
                                                   bc(v["mb"][64:65, b, 0:P].unsqueeze(1), (1, H, P))))
                            st.did(dve.tensor_copy(v["selr"][64:65, b * 4:(b + 1) * 4, :, 0:MR]
                                                   .rearrange("p g j k -> p (g j) k"),
                                                   bc(v["mb"][64:65, b, P:M].unsqueeze(1), (1, 16, MR))))
                        st.wait()
                        dve.sem_inc(sel0_made, 1)
                values()
                if L == 3:
                    for b in range(B):
                        for s in range(2):
                            n = P if s == 0 else MR
                            bk = RB.get(dve, p, "kp", b, s)
                            dve.tensor_tensor(v["Kp"][0:n, 2 * b + s, :], bk[0:n, 0:HD], v["bk"][0:n], ALU.add)\
                               .then_inc(RB.read, 1)
                    keys()
                for what, c in ATT:
                    if what == "front":
                        if L == 3:
                            for q in range(2):
                                bk = RB.get(dve, p, "qp", c, q)
                                t = (2 * c + q) * 2
                                dve.tensor_tensor(v["Qp"][:, t:t + 2, :], bk[:].rearrange("p (t d) -> p t d", t=2),
                                                  bc(v["bq"][:].unsqueeze(1), (P, 2, D)), ALU.add).then_inc(RB.read, 1)
                            continue
                        for i in range(TPC):
                            for m in range(MT):
                                for h0 in range(0, hpm, 3):
                                    hn = min(3, hpm - h0)
                                    bk = RB.get(dve, p, "mxs", c, i, m, h0)
                                    hh = m * hpm + h0
                                    dve.tensor_reduce(v["mx"][:, TPC * c + i, hh:hh + hn],
                                                      bk[:, 0:hn * M].rearrange("p (h k) -> p h k", k=M), AX.X, ALU.max)\
                                       .then_inc(RB.read, 1)
                    elif what == "back":
                        if L < 3:
                            bk = RB.get(dve, p, "mx", c)
                            st.did(dve.tensor_scalar(v["negm"][0:H, c, :], bk[0:H, :], -1.0, None, ALU.mult))
                            st.wait()
                            dve.scalar_tensor_tensor(v["negm"][32:32 + H, c, :], bk[0:H, :], -1.0, v["negm"][0:H, c, :],
                                                     ALU.mult, ALU.subtract).then_inc(RB.read, 1)
                        for g in range(G):
                            for i in range(1 if hd == 16 else TPC):
                                nq = TPC if hd == 16 else 1
                                bk = RB.get(dve, p, "av", c, g) if hd == 16 else RB.get(dve, p, "av", c, g, i)
                                a = bk[:, 0:nq * 4 * (hd + 1)].rearrange("p (q j d) -> p q j d", j=4, d=hd + 1)
                                r = v["rden"][:, RB.emptied % 2, 0:nq * 4].rearrange("p (q j) -> p q j", j=4)
                                st.did(dve.reciprocal(r, a[:, :, :, hd]))
                                st.wait()
                                o = v["O"][:, c % v["NO"], i:i + nq, g * 4 * hd:(g + 1) * 4 * hd]\
                                    .rearrange("p q (j d) -> p q j d", j=4)
                                dve.tensor_tensor(o, a[:, :, :, 0:hd], bc(r.unsqueeze(3), (P, nq, 4, hd)), ALU.mult)\
                                   .then_inc(RB.read, 1)
                    else:
                        if L in (1, 2):
                            dve.wait_ge(xbias, XB[p])
                        if L < 3:
                            for q in range(2):
                                bk = RB.get(dve, p, "out", c, q)
                                add_out(p, bk, 2 * c + q, tg[:, L:L + 1], False).then_inc(RB.read, 1)
                            continue
                        dve.wait_ge(qbo_made, c + 1)
                        for q in range(2):
                            bk = RB.get(dve, p, "out", c, q)
                            a = v["Qp"][:, (2 * c + q) * 2:(2 * c + q) * 2 + 2, :]
                            dve.tensor_tensor(a, bk[:].rearrange("p (t d) -> p t d", t=2), a, ALU.add).then_inc(RB.read, 1)
                        dve.wait_ge(RB.read, RB.emptied)
                        for t in range(TPC * c, TPC * (c + 1)):
                            st.did(dve.bn_stats(stats[:, t, :], v["Qp"][:, t, :]))
                        st.wait()
                        for t in range(TPC * c, TPC * (c + 1)):
                            last = dve.bn_aggr(mv[:, t, :], stats[:, t, :])
                        last.then_inc(post_stats, 1)
                        dve.wait_ge(post_z, c + 1)
                        dve.wait_ge(xbias, XB[p])
                        z = v["Qp"][:, TPC * c:TPC * (c + 1), :]
                        xx = X[:, TPC * c:TPC * (c + 1), :]
                        st.did(dve.tensor_tensor(z, z, bc(v["lg"][:].unsqueeze(1), (P, TPC, D)), ALU.mult))
                        st.wait()
                        st.did(dve.tensor_tensor(xx, xx, z, ALU.add))
                if L == 3:
                    st.wait()
                over(p)

            def coupling(p):
                v = ph[p]
                x_stats(p)
                dve.wait_ge(w_loaded[p], 16 * len(loads[p]))
                st.did(dve.tensor_copy(v["w4r"][0:64], bc(v["w4"][0:64], (64, P))))
                st.did(dve.tensor_copy(v["g3r"][0:64], bc(v["g3"][0:64], (64, P))))
                st.did(dve.tensor_scalar(v["hb"][:, 0:1], v["b4"][:], 0.5, None, ALU.mult))
                st.did(dve.tensor_scalar(v["hb"][:, 1:2], v["gb3"][:], 0.5, None, ALU.mult))
                for c in range(NC):
                    for d in range(DK):
                        dve.wait_ge(RA.read, RA.n(p, "yT", c, d))
                        st.did(dve.tensor_reduce(v["msum"][:, d, c:c + 1], v["yT"][:, d, c * CH:(c + 1) * CH], AX.X, ALU.add))
                st.wait()
                for b in range(B):
                    st.did(dve.tensor_tensor(v["mean"][:, :, b], v["msum"][:, :, CPB * b], v["msum"][:, :, CPB * b + 1], ALU.add))
                st.wait()
                a = v["mean"][:].rearrange("p k b -> p (k b)")
                dve.tensor_scalar(a, a, 1.0 / S, None, ALU.mult).then_inc(gc_ready, 1)
                dve.wait_ge(RA.read, RA.n(p, "g3"))
                st.did(dve.tensor_scalar(v["al"][:], v["ar"][:], 0.3, sgn[:, 0:1], ALU.mult, ALU.mult))
                st.did(dve.tensor_scalar(v["be"][:], v["gt"][:], v["ar"][:, 0:1], 0.7, ALU.mult, ALU.mult))
                st.wait()
                st.did(dve.tensor_scalar(v["be"][:], v["be"][:], 0.1, sgn[:, 0:1], ALU.add, ALU.mult))
                st.wait()
                s2 = [v["yT"], v["yS"]]
                for r in range(3):
                    old, new = s2[r % 2], s2[(r + 1) % 2]
                    for c in range(NC):
                        cs = slice(c * CH, (c + 1) * CH)
                        b = c // CPB
                        dve.wait_ge(RC.read, RC.n(p, r, "l4", c))
                        k, w = v["tmp"][:, 0, :], v["tmp"][:, 1, :]
                        st.did(dve.tensor_scalar(k, v["th"][:, c, :], v["al"][:, 0:1], v["be"][:, b:b + 1], ALU.mult, ALU.add))
                        st.wait()
                        st.did(dve.tensor_tensor(w, k, old[:, 1, cs], ALU.mult))
                        st.wait()
                        st.did(dve.tensor_tensor(new[:, 0, cs], w, old[:, 0, cs], ALU.add))
                        st.wait()
                        st.did(dve.tensor_tensor(w, k, old[:, 0, cs], ALU.mult))
                        st.wait()
                        dve.tensor_tensor(new[:, 1, cs], old[:, 1, cs], w, ALU.subtract).then_inc(state_made, 1)
                        dve.wait_ge(state_made, NC * r + c + 1)
                for c in range(NC):
                    for q in range(2):
                        bk = RB.get(dve, p, "fin", c, q)
                        add_out(p, bk, 2 * c + q, tg[:, 4:5], False).then_inc(RB.read, 1)
                over(p)

            def quantised(p):
                v = ph[p]
                x_stats(p)
                dve.wait_ge(w_loaded[p], 16 * len(loads[p]))
                for w, n, sw, iw, wi in (("w1", FT1, "sw1", "iw1", "wi1"), ("w2", DK, "sw2", "iw2", "wi2")):
                    st.did(dve.tensor_reduce(v[sw][:], v[w][:], AX.X, ALU.max, apply_absolute_value=True))
                    st.wait()
                    st.did(dve.tensor_scalar(v[sw][:], v[sw][:], 1e-8, 1.0 / 127.0, ALU.max, ALU.mult))
                    st.wait()
                    st.did(dve.reciprocal(v[iw][:], v[sw][:]))
                    st.wait()
                    for i in range(n):
                        st.did(dve.tensor_scalar(v[w][:, i, :], v[w][:, i, :], v[iw][:, i:i + 1], 127.0, ALU.mult, ALU.min))
                    st.wait()
                    st.did(dve.tensor_scalar(v[w][:], v[w][:], -128.0, ROUND, ALU.max, ALU.add))
                    st.wait()
                    st.did(dve.tensor_scalar(v[wi][:], v[w][:], ROUND, None, ALU.subtract))
                st.wait()
                dve.sem_inc(wq_made, 1)
                for d in range(DK):
                    last = st.did(dve.tensor_scalar(v["diag"][:, d, :], ident[:], v["sw2"][:, d:d + 1], None, ALU.mult))
                st.wait()
                dve.sem_inc(diag_made, 1)
                bk = RB.get(dve, p, "sw2r")
                dve.tensor_copy(v["sw2r"][:], bk[:, 0:D]).then_inc(RB.read, 1)

                def scale(n):
                    st.wait()
                    dve.sem_inc(xmax_made, 1)
                    dve.wait_ge(xall_made, n + 1)
                    st.did(dve.tensor_scalar(v["sc"][:, 4 + n:5 + n], v["sc"][:, n:n + 1], 1e-8, 1.0 / 255.0, ALU.max, ALU.mult))
                    st.wait()
                    st.did(dve.reciprocal(v["sc"][:, 6 + n:7 + n], v["sc"][:, 4 + n:5 + n]))
                    st.wait()

                for c in range(NC):
                    dve.wait_ge(ln_y, lnorm(p, c))
                    st.did(dve.tensor_reduce(v["m"][:, c:c + 1], v["Y"][:, TPC * c:TPC * (c + 1), :], AX.XY, ALU.max))
                st.wait()
                st.did(dve.tensor_reduce(v["m"][:, 60:61], v["m"][:, 0:NC], AX.X, ALU.max))
                scale(0)
                for c in range(NC):
                    a = v["Y"][:, TPC * c:TPC * (c + 1), :]
                    st.did(dve.tensor_scalar(a, a, v["sc"][:, 6:7], 255.0, ALU.mult, ALU.min))
                    st.wait()
                    st.did(dve.tensor_scalar(a, a, 0.0, ROUND, ALU.max, ALU.add))
                    st.wait()
                    dve.tensor_scalar(v["xi"][:, TPC * c:TPC * (c + 1), :], a, ROUND, None, ALU.subtract).then_inc(xi_made, 1)
                st.did(dve.tensor_scalar(v["sb1"][:], v["sw1"][:], v["sc"][:, 4:5], None, ALU.mult))
                st.wait()
                st.did(dve.reciprocal(v["ib1"][:], v["sb1"][:]))
                st.wait()
                st.did(dve.tensor_tensor(v["bq1"][:], v["b1"][:], v["ib1"][:], ALU.mult))
                st.wait()
                st.did(dve.tensor_scalar(v["bq1"][:], v["bq1"][:], ROUND, ROUND, ALU.add, ALU.subtract))
                st.wait()
                dve.tensor_tensor(v["bq1"][:], v["bq1"][:], v["sb1"][:], ALU.mult).then_inc(hscale_made, 1)
                for c in range(NC):
                    for f in range(FT1):
                        dve.wait_ge(RC.read, RC.n(p, "up", c, f))
                        n = 8 + c * FT1 + f
                        st.did(dve.tensor_reduce(v["m"][:, n:n + 1], v["h"][:, f, c * CH:(c + 1) * CH], AX.X, ALU.max))
                st.wait()
                st.did(dve.tensor_reduce(v["m"][:, 61:62], v["m"][:, 8:8 + NC * FT1], AX.X, ALU.max))
                scale(1)
                for c in range(NC):
                    a = v["h"][:, :, c * CH:(c + 1) * CH]
                    st.did(dve.tensor_scalar(a, a, v["sc"][:, 7:8], ROUND, ALU.mult, ALU.add))
                    st.wait()
                    dve.tensor_scalar(v["hi"][:, :, c * CH:(c + 1) * CH], a, ROUND, 255.0, ALU.subtract, ALU.min)\
                       .then_inc(hi_made, 1)
                    if c == 0:
                        dve.wait_ge(RB.read, RB.n(p, "sw2r"))
                        st.did(dve.tensor_scalar(v["rowS"][:], v["sw2r"][:], v["sc"][:, 5:6], None, ALU.mult))
                        st.wait()
                        st.did(dve.reciprocal(v["rowI"][:], v["rowS"][:]))
                        st.wait()
                        st.did(dve.tensor_tensor(v["rowB"][:], v["b2"][:], v["rowI"][:], ALU.mult))
                        st.wait()
                        st.did(dve.tensor_scalar(v["rowB"][:], v["rowB"][:], ROUND, ROUND, ALU.add, ALU.subtract))
                        st.wait()
                        st.did(dve.tensor_tensor(v["rowB"][:], v["rowB"][:], v["rowS"][:], ALU.mult))
                        st.wait()
                        st.did(dve.tensor_scalar(v["rowB"][:], v["rowB"][:], tg[:, 5:6], None, ALU.mult))
                        st.did(dve.tensor_scalar(v["rowT"][:], v["rowS"][:], tg[:, 5:6], None, ALU.mult))
                        st.wait()
                        dve.sem_inc(rows_made, 1)
                dve.wait_ge(xbias, XB[p])
                for c in range(NC):
                    for q in range(2):
                        bk = RB.get(dve, p, "dn", c, q)
                        o = v["dn"][:, q, :, :]
                        dve.tensor_tensor(o, bk[:].rearrange("p (t d) -> p t d", t=2),
                                          bc(v["rowT"][:].unsqueeze(1), (P, 2, D)), ALU.mult).then_inc(RB.read, 1)
                        dve.wait_ge(RB.read, RB.emptied)
                        a = X[:, (2 * c + q) * 2:(2 * c + q) * 2 + 2, :]
                        st.did(dve.tensor_tensor(a, a, o, ALU.add))
                st.wait()
                over(p)

            def experts(p, L):
                v = ph[p]
                E = E2 if L == 2 else E3
                r = v["r"]
                gate = tg[:, 4 + L:5 + L]
                x_stats(p)
                dve.wait_ge(w_loaded[p], 16 * len(loads[p]))
                for c in range(NC):
                    bk = RB.get(dve, p, "lg", c)
                    dve.tensor_tensor(v["lg"][:, TPC * c:TPC * (c + 1), :],
                                      bk[:, 0:TPC * E].rearrange("p (t e) -> p t e", e=E),
                                      bc(v["br"][:].unsqueeze(1), (P, TPC, E)), ALU.add).then_inc(RB.read, 1)
                dve.wait_ge(RB.read, RB.emptied)
                if L == 3:
                    st.did(dve.tensor_reduce(r[:, 0, :], v["lg"][:], AX.X, ALU.max))
                    st.wait()
                    st.did(dve.tensor_tensor(v["lg"][:], v["lg"][:], bc(r[:, 0, :].unsqueeze(2), (P, NT, E)), ALU.subtract))
                    st.wait()
                    dve.sem_inc(ex_ready, 1)
                    dve.wait_ge(ex_made, 2)
                    st.did(dve.tensor_reduce(r[:, 0, :], v["pre"][:], AX.X, ALU.add))
                    st.wait()
                    st.did(dve.reciprocal(r[:, 1, :], r[:, 0, :]))
                    st.wait()
                    st.did(dve.tensor_tensor(v["lg"][:], v["pre"][:], bc(r[:, 1, :].unsqueeze(2), (P, NT, E)), ALU.mult))
                    st.wait()
                for t in range(NT):
                    st.did(dve.max(v["top"][:, t, :], v["lg"][:, t, :]))
                st.wait()
                for t in range(NT):
                    st.did(dve.max_index(v["idx"][:, t, :], v["top"][:, t, :], v["lg"][:, t, :]))
                st.wait()
                st.did(dve.tensor_copy(v["idf"][:], v["idx"][:]))
                st.wait()
                io = bc(iota[:, 0:E].unsqueeze(1), (P, NT, E))
                st.did(dve.tensor_tensor(v["oh"][:], io, bc(v["idf"][:, :, 0:1], (P, NT, E)), ALU.is_equal))
                st.did(dve.tensor_tensor(v["oh2"][:], io, bc(v["idf"][:, :, 1:2], (P, NT, E)), ALU.is_equal))
                if L == 2:
                    st.did(dve.tensor_tensor(r[:, 0, :], v["top"][:, :, 1], v["top"][:, :, 0], ALU.subtract))
                    st.wait()
                    dve.sem_inc(ex_ready, 1)
                    dve.wait_ge(ex_made, 1)
                    st.did(dve.tensor_scalar(r[:, 2, :], r[:, 1, :], 1.0, None, ALU.add))
                    st.wait()
                    st.did(dve.reciprocal(r[:, 3, :], r[:, 2, :]))
                    st.wait()
                    st.did(dve.tensor_tensor(r[:, 4, :], r[:, 1, :], r[:, 3, :], ALU.mult))
                    g0, g1 = r[:, 3, :], r[:, 4, :]
                else:
                    st.wait()
                    st.did(dve.tensor_tensor(v["ohb"][:], v["oh"][:], v["oh2"][:], ALU.add))
                    st.did(dve.memset(v["ohs"][:, 0, :], 0.0))
                    for t in range(1, NT):
                        st.wait()
                        st.did(dve.tensor_tensor(v["ohs"][:, t, :], v["ohs"][:, t - 1, :], v["ohb"][:, t - 1, :], ALU.add))
                    st.wait()
                    dve.sem_inc(oh_made, 1)
                    st.did(dve.tensor_tensor(r[:, 2, :], v["top"][:, :, 0], v["top"][:, :, 1], ALU.add))
                    st.wait()
                    st.did(dve.tensor_scalar(r[:, 3, :], r[:, 2, :], 1e-9, None, ALU.add))
                    st.wait()
                    st.did(dve.reciprocal(r[:, 4, :], r[:, 3, :]))
                    st.wait()
                    st.did(dve.tensor_tensor(r[:, 5, :], v["top"][:, :, 0], r[:, 4, :], ALU.mult))
                    st.did(dve.tensor_tensor(r[:, 6, :], v["top"][:, :, 1], r[:, 4, :], ALU.mult))
                    g0, g1 = r[:, 5, :], r[:, 6, :]
                st.wait()
                st.did(dve.tensor_tensor(v["oh"][:], v["oh"][:], bc(g0.unsqueeze(2), (P, NT, E)), ALU.mult))
                st.did(dve.tensor_tensor(v["oh2"][:], v["oh2"][:], bc(g1.unsqueeze(2), (P, NT, E)), ALU.mult))
                st.wait()
                st.did(dve.tensor_tensor(v["G"][:], v["oh"][:], v["oh2"][:], ALU.add))
                st.wait()
                st.did(dve.tensor_scalar(v["G"][:], v["G"][:], gate, None, ALU.mult))
                st.wait()
                if L == 3:
                    bk = RB.get(dve, p, "pos")
                    dve.tensor_scalar(v["pre"][:], bk[:, 0:NT * E].rearrange("p (t e) -> p t e", e=E), float(CAP), None,
                                      ALU.is_lt).then_inc(RB.read, 1)
                    dve.wait_ge(RB.read, RB.emptied)
                    st.did(dve.tensor_tensor(v["G"][:], v["G"][:], v["pre"][:], ALU.mult))
                    dve.wait_ge(ln_y, lnorm(p, NC - 1))
                    st.did(dve.scalar_tensor_tensor(X[:], v["Y"][:], gate, X[:], ALU.mult, ALU.add))
                    st.wait()
                else:
                    dve.sem_inc(g_made, 1)
                    dve.wait_ge(ln_y, lnorm(p, NC - 1))
                    for c in range(NC):
                        for q in range(2):
                            bk = RB.get(dve, p, "b2", c, q)
                            a = X[:, (2 * c + q) * 2:(2 * c + q) * 2 + 2, :]
                            dve.tensor_tensor(a, a, bk[:].rearrange("p (t d) -> p t d", t=2), ALU.add).then_inc(RB.read, 1)
                    dve.wait_ge(RB.read, RB.emptied)
                n = 0
                for what, e, c in expert_order(E if L == 2 else E + 1):
                    if what == "up":
                        if L == 3:
                            for m in range(3):
                                fn = F3T[m]
                                dve.wait_ge(RA.read, RA.n(p, "gate", e, c, m))
                                bk = RB.get(dve, p, "up", e, c, m)
                                dve.tensor_tensor(v["hT"][0:fn, ((e * NC + c) % 3) * 3 + m, :], v["sg"][0:fn, n % 4, :],
                                                  bk[0:fn, :], ALU.mult).then_inc(RB.read, 1)
                                n += 1
                        continue
                    for q in range(2):
                        bk = RB.get(dve, p, "dn", e, c, q)
                        for i in range(2):
                            t = (2 * c + q) * 2 + i
                            a = X[:, t, :]
                            s = v["G"][:, t, e:e + 1] if e < E else gate
                            ins = dve.scalar_tensor_tensor(a, bk[:, i * D:(i + 1) * D], s, a, ALU.mult, ALU.add)
                        ins.then_inc(RB.read, 1)
                over(p)

            for p in range(NPH):
                L = p // 2
                if p:
                    dve.wait_ge(phase_over, p)
                if p % 2 == 0:
                    attention(p, L)
                elif L == 0:
                    coupling(p)
                elif L == 1:
                    quantised(p)
                else:
                    experts(p, L)

        @block.sync
        def _(sp):
            def load(p):
                if p >= 2:
                    sp.wait_ge(phase_over, p - 1)
                for dst, src in loads[p]:
                    sp.dma_start(dst, src, allow_slow_non_contiguous=True).then_inc(w_loaded[p], 16)

            x_v = A["x"].rearrange("b (t p) d -> p (b t) d", p=P)
            sp.dma_start(X[:], x_v).then_inc(in_loaded, 16)
            for b in range(B):
                sp.dma_start(ctxN[:, b, :], A["ctx_768"][b, 0:P, :]).then_inc(in_loaded, 16)
                sp.dma_start(ctxN[0:MR, B + b, :], A["ctx_768"][b, P:M, :]).then_inc(in_loaded, 16)
            sp.dma_start(gates[:, 0:4], row(A["g_xattn"], 4)).then_inc(in_loaded, 16)
            sp.dma_start(gates[:, 4:8], row(A["g_ffn"], 4)).then_inc(in_loaded, 16)
            load(0)
            for p in range(1, NPH):
                load(p)
                L = p // 2
                if p % 2 == 0 or L < 2:
                    continue
                v = ph[p]
                sp.wait_ge(phase_over, p)
                NW = len(ew_loaded[L])
                pre = f"L{L}_ffn_"
                for e in range(E2 if L == 2 else E3 + 1):
                    s = e % NW
                    if e >= NW:
                        sp.wait_ge(RB.filled, RB.n(p, "dn", e - NW, NC - 1, 1))
                    if L == 2:
                        pairs = [(v["W1"][:, s], kin(A[pre + "W1"][e])),
                                 (v["W2"][:, s], A[pre + "W2"][e].rearrange("(m p) n -> p m n", p=P))]
                    else:
                        g, u, d = (A[pre + n][e] if e < E3 else A[pre + "s" + n] for n in ("w_gate", "w_up", "w_down"))\
                            if e < E3 else (A[pre + n] for n in ("sw_gate", "sw_up", "sw_down"))
                        pairs = [(v["Wg"][:, s], kin(g)), (v["Wu"][:, s], kin(u)),
                                 (v["Wd"][:, s, 0:2], d[0:2 * P, :].rearrange("(m p) n -> p m n", p=P)),
                                 (v["Wd"][0:F3 - 2 * P, s, 2], d[2 * P:F3, :])]
                    for dst, src in pairs:
                        sp.dma_start(dst, src).then_inc(ew_loaded[L][s], 16)
            sp.wait_ge(phase_over, NPH)
            sp.dma_start(out.rearrange("b (t p) d -> p (b t) d", p=P), X[:]).then_inc(stored, 16)
            sp.wait_ge(stored, 16)


def kernel(**inputs):
    import numpy as np
    import concourse.bacc as bacc
    from concourse.bass_utils import run_bass_kernel_spmd

    nc = bacc.Bacc("TRN2", target_bir_lowering=False, num_devices=1)
    arrays, aps = {}, {}
    for name, value in inputs.items():
        a = np.ascontiguousarray(value)
        arrays[f"in_{name}"] = a
        aps[name] = nc.dram_tensor(f"in_{name}", a.shape, mybir.dt.from_np(a.dtype), kind="ExternalInput").ap()
    out = nc.dram_tensor("out_x", (B, S, D), F32, kind="ExternalOutput").ap()
    build(nc, aps, out)
    r = run_bass_kernel_spmd(nc, [arrays], core_ids=[0])
    return r.results[0]["out_x"]
```

```python
import concourse.bass as bass
from concourse import mybir
from contextlib import ExitStack

F32 = mybir.dt.float32
BF16 = mybir.dt.bfloat16
U32 = mybir.dt.uint32
U8 = mybir.dt.uint8
ALU = mybir.AluOpType
ACT = mybir.ActivationFunctionType
AX = mybir.AxisListType
RMAX = bass.bass_isa.ReduceOp.max

P = 128
B, S, D = 2, 1024, 256
T = B * S
NT = T // P
CH = 512
NC = T // CH
TPC = CH // P
CPB = NC // B
DK = D // P
M, CD = 154, 192
MR = M - P
BIG = float(2.0 ** 100)
ROUND = 12582912.0
PHASES = 8

HEADS = {0: (16, 16), 1: (8, 64), 2: (16, 16), 3: (16, 16)}
E2, H2 = 8, 512
E3, F3 = 16, 352
CAP = 320
F3T = [128, 128, 96]
F1 = 1024
FT1 = F1 // P


class Ring:

    def __init__(self, banks, filled, read):
        self.banks, self.filled, self.read, self.order, self.emptied = banks, filled, read, {}, 0

    def take(self, pe, *key):
        i = len(self.order)
        assert key not in self.order, key
        self.order[key] = i
        if i >= len(self.banks):
            pe.wait_ge(self.read, i - len(self.banks) + 1)
        return self.banks[i % len(self.banks)]

    def n(self, *key):
        return self.order[key] + 1

    def get(self, eng, *key):
        assert self.order[key] == self.emptied, (key, self.order[key], self.emptied)
        self.emptied += 1
        eng.wait_ge(self.filled, self.order[key] + 1)
        return self.banks[self.order[key] % len(self.banks)]


class Steps:

    def __init__(self, eng, sem):
        self.eng, self.sem, self.count = eng, sem, 0

    def did(self, ins):
        self.count += 1
        ins.then_inc(self.sem, 1)
        return self.count

    def wait(self, count=None):
        self.eng.wait_ge(self.sem, self.count if count is None else count)


class Arena:
    def __init__(self, tensor, words):
        self.t, self.words, self.at = tensor, words, 0

    def reset(self):
        self.at = 0

    def take(self, shape, dt=F32):
        n = 1
        for s in shape:
            n *= s
        words = n if dt in (F32, U32) else (n + 1) // 2 if dt == BF16 else (n + 3) // 4
        ap = self.t[:, self.at:self.at + words]
        self.at += (words + 7) // 8 * 8
        assert self.at <= self.words, (self.at, self.words)
        if dt != F32:
            ap = ap.bitcast(dt)[:, 0:n]
        if len(shape) > 1:
            names = "abcd"[:len(shape)]
            ap = ap.rearrange("p (" + " ".join(names) + ") -> p " + " ".join(names),
                              **{k: s for k, s in zip(names, shape)})
        return ap


def bc(ap, shape):
    return ap.broadcast_to(shape)


def build(nc, A, out):
    ctx = ExitStack()
    with ctx:
        def sb(name, shape, dt=F32):
            return ctx.enter_context(nc.sbuf_tensor(name, shape, dt))

        def sem(name):
            return ctx.enter_context(nc.semaphore(name))

        banks = [ctx.enter_context(nc.psum_tensor(f"bank{i}", [P, 512], F32)) for i in range(8)]
        RA = Ring(banks[0:2], sem("a_bank_filled"), sem("a_bank_read"))
        RB = Ring(banks[2:4], sem("b_bank_filled"), sem("b_bank_read"))
        RC = Ring(banks[4:8], sem("c_bank_filled"), sem("c_bank_read"))

        X = sb("X", [P, NT, D])
        ident = sb("ident", [P, P])
        identb = sb("identb", [P, P], BF16)
        ones = sb("ones", [P, P])
        zeros = sb("zeros", [P, D])
        before = sb("before", [P, P], BF16)
        onesb = sb("onesb", [P, P], BF16)
        hmask = {16: sb("hmask16", [P, 8]), 64: sb("hmask64", [P, 2])}
        sel = sb("sel", [65, 16, P], BF16)
        selr = sb("selr", [65, 4, 4, 32], BF16)
        sgn = sb("sgn", [P, 1])
        nhalf = sb("nhalf", [P, NT])
        iota = sb("iota", [P, 16])
        gates = sb("gates", [P, 8])
        tg = sb("tg", [P, 8])
        ctxT = sb("ctxT", [P, 2, B * M])
        stats = sb("stats", [P, NT, 6])
        mv = sb("mv", [P, NT, 2])
        rstd = sb("rstd", [P, NT])
        WoP = sb("WoP", [P, 4, D])
        WA = 4864
        warena = [Arena(sb(f"weights{i}", [P, WA]), WA) for i in range(2)]
        SA = 35500
        scratch = Arena(sb("scratch", [P, SA]), SA)

        w_loaded = [sem(f"weights_loaded_{p}") for p in range(8)]
        in_loaded = sem("inputs_loaded")
        consts = sem("constants_made")
        tg_made = sem("gates_made")
        ctxT_made = sem("context_transposed")
        ln_stats = sem("ln_statistics")
        ln_rstd = sem("ln_rstd_made")
        ln_y = sem("ln_normalised")
        phase_over = sem("phase_over")
        kv_clear = sem("kv_buffers_cleared")
        kz_made = sem("keys_spread")
        kr_made = sem("last_keys_spread")
        v_made = sem("values_made")
        negm_clear = sem("negated_maxima_cleared")
        xbias = sem("bias_added_to_x")
        pool_st = sem("pool_steps")
        act_st = sem("act_steps")
        dve_st = sem("dve_steps")
        kn_made = sem("keys_normalised")
        kn_clear = sem("key_buffers_cleared")
        kss_made = sem("key_squares_summed")
        qss_made = sem("query_squares_summed")
        qn_made = sem("queries_normalised")
        qbo_made = sem("residual_query_ready")
        post_stats = sem("post_ln_statistics")
        post_z = sem("post_ln_normalised")
        mb_made = sem("mask_bias_made")
        sel0_made = sem("selectors_with_mask_made")
        gbo_made = sem("gated_bias_made")
        gc_ready = sem("global_net_inputs_ready")
        state_made = sem("coupled_state_made")
        wq_made = sem("weights_rounded")
        diag_made = sem("scales_on_the_diagonal")
        xmax_made = sem("largest_of_partition")
        xall_made = sem("largest_of_all")
        xi_made = sem("x_rounded")
        hscale_made = sem("hidden_scale_and_bias_made")
        hi_made = sem("hidden_rounded")
        rows_made = sem("output_scale_rows_made")
        oh_made = sem("one_hots_made")
        g_made = sem("gate_weights_made")
        ex_ready = sem("exponents_ready")
        ex_made = sem("exponentials_made")
        XB = {2: 1, 3: 2, 4: 3, 6: 4}
        x_out = sem("x_final")
        zero_made = sem("zeros_made")
        slots_clear = sem("slots_cleared")
        idx_made = sem("slot_indices_made")
        dumps_made = sem("spare_rows_numbered")
        scattered = sem("tokens_scattered")
        xe_loaded = [sem(f"expert_tokens_loaded_{i}") for i in range(3)]
        ye_stored = [sem(f"expert_results_stored_{i}") for i in range(3)]
        gathered = [sem(f"results_gathered_{i}") for i in range(8)]
        EWN = {2: 2, 3: 4}
        ew_loaded = {2: [sem(f"expert2_loaded_{i}") for i in range(3)], 3: [sem(f"expert3_loaded_{i}") for i in range(3)]}
        stored = sem("output_stored")

        NIN = 2 * B + 3
        NCONST = 5

        ph = []
        loads = []

        def col(ap, n):
            return ap.rearrange("(m p) -> p m", p=P)

        def row(ap, n):
            return bc(ap.rearrange("(o n) -> o n", o=1), (P, n))

        def kin(ap):
            return ap.rearrange("(k p) n -> p k n", p=P)

        def ctxw(w, dst):
            return [(dst[:, 0, :], w[0:P, :]), (dst[0:CD - P, 1, :], w[P:CD, :])]

        for L in range(4):
            H, hd = HEADS[L]
            HD = H * hd
            MT, hpm, G = HD // P, P // hd, H // 4
            w = warena[(2 * L) % 2]
            w.reset()
            scratch.reset()
            v = dict(H=H, hd=hd, HD=HD, MT=MT, hpm=hpm, G=G)
            pre = f"L{L}_xattn_"
            nm = dict(Wq="wq", Wk="wk", Wv="wv", Wo="wo") if L == 2 else dict(Wq="Wq", Wk="Wk", Wv="Wv", Wo="Wo")
            if L == 1:
                nm["Wo"] = "Wout"
            ld = []
            v["Wq"] = w.take((DK, HD))
            v["Wk"] = w.take((2, HD))
            v["Wv"] = w.take((2, HD))
            v["vw"] = 32 if hd == 16 else hd + 1
            v["Wo"] = WoP if hd == 16 else w.take((MT, D))
            ld += ctxw(A[pre + nm["Wk"]], v["Wk"])
            ld += ctxw(A[pre + nm["Wv"]], v["Wv"])
            ld.append((v["Wq"], kin(A[pre + nm["Wq"]])))
            if L == 2:
                v["bq"], v["bk"], v["bv"], v["bo"] = w.take((DK,)), w.take((DK,)), w.take((HD,)), w.take((D,))
                ld += [(v["bq"], col(A[pre + "bq"], DK)), (v["bk"], col(A[pre + "bk"], DK)),
                       (v["bv"], row(A[pre + "bv"], HD)), (v["bo"], row(A[pre + "bo"], D))]
            if L == 1:
                v["bo"] = w.take((D,))
                ld.append((v["bo"], row(A[pre + "bout"], D)))
            if L == 3:
                for k, s in (("bq", "bq"), ("bk", "bk"), ("bv", "bv"), ("bo", "bo"), ("lg", "ln_gamma"), ("lb", "ln_beta")):
                    v[k] = w.take((D,))
                    ld.append((v[k], row(A[pre + s], D)))
            if L == 0:
                v["m8"] = w.take((B * M,), U8)
                ld.append((v["m8"], bc(A["mask_BxS2_bf1"].rearrange("(o b) k -> o (b k)", o=1), (P, B * M))))
                v["m01"] = w.take((B * M,))
                v["mb"] = w.take((B, M), BF16)
            if hd == 16:
                wo = A[pre + nm["Wo"]].rearrange("(g j d) n -> j d g n", j=4, d=hd)
                ld += [(WoP[32 * j:32 * j + hd, :, :], wo[j]) for j in range(4)]
            else:
                ld.append((v["Wo"], A[pre + nm["Wo"]].rearrange("(k p) n -> p k n", p=P)))
            v["Y"] = scratch.take((NT, D))
            v["yT"] = scratch.take((DK, CH))
            v["QT"] = scratch.take((MT, T))
            v["Kz"] = scratch.take((MT * B, hpm, M))
            v["Kr"] = scratch.take((MT * B, hpm, 32))
            v["V"] = scratch.take((B, H, v["vw"]))
            v["Vr"] = scratch.take((B, G, 4, v["vw"]))
            v["KTs"] = scratch.take((MT, B * M))
            v["NPT"] = 2 if L in (1, 3) else 3
            v["PT"] = scratch.take((v["NPT"], 5, CH))
            if hd == 16:
                v["OT"] = scratch.take((G, CH))
                v["rden"] = scratch.take((2, CH))
            else:
                v["O"] = scratch.take((2, TPC, HD))
                v["rden"] = scratch.take((2, 16))
            v["mx"] = scratch.take((NT, H))
            v["negm"] = scratch.take((NC, CH), BF16)
            if L == 0:
                ctxN = scratch.take((2 * B, CD))
                v["sel"] = scratch.take((B * H, P), BF16)
                v["selr"] = scratch.take((B * 4, 4, 32), BF16)
            v["gbo"] = scratch.take((D,))
            if L == 3:
                v["Qp"] = scratch.take((NT, D))
                v["ss"] = scratch.take((NT + 4,))
                v["rs"] = scratch.take((NT + 4,))
                v["Kp"] = scratch.take((4, D))
                v["gb"] = scratch.take((D,))
                v["junk"] = scratch.take((D,))
            ph.append(v)
            loads.append(ld)

            w = warena[1]
            w.reset()
            scratch.reset()
            pre = f"L{L}_ffn_"
            v = dict()
            ld = []
            v["Y"] = scratch.take((NT, D))
            if L != 1:
                v["yT"] = scratch.take((DK, T))
            if L == 0:
                v["w1"], v["w2"], v["w3"], v["w4"] = w.take((DK, 256)), w.take((DK, 128)), w.take((64,)), w.take((1,))
                v["b1"], v["b2"], v["b3"], v["b4"] = w.take((DK,)), w.take((1,)), w.take((1,)), w.take((1,))
                v["g1"], v["g2"], v["g3"] = w.take((DK, 128)), w.take((64,)), w.take((1,))
                v["gb1"], v["gb2"], v["gb3"], v["ar"] = w.take((1,)), w.take((1,)), w.take((1,)), w.take((1,))
                o1 = lambda a: a.rearrange("(p o) -> p o", o=1)
                ld += [(v["g1"], kin(A[pre + "gc_w1"])), (v["g2"], A[pre + "gc_w2"]), (v["g3"][0:64], A[pre + "gc_w3"]),
                       (v["gb1"], o1(A[pre + "gc_b1"])), (v["gb2"][0:64], o1(A[pre + "gc_b2"])),
                       (v["gb3"], bc(o1(A[pre + "gc_b3"]), (P, 1))),
                       (v["w1"], kin(A[pre + "cn_w1"])), (v["w2"], kin(A[pre + "cn_w2"])),
                       (v["w3"], A[pre + "cn_w3"]), (v["w4"][0:64], A[pre + "cn_w4"]),
                       (v["b1"], col(A[pre + "cn_b1"], DK)), (v["b2"], o1(A[pre + "cn_b2"])),
                       (v["b3"][0:64], o1(A[pre + "cn_b3"])), (v["b4"], bc(o1(A[pre + "cn_b4"]), (P, 1))),
                       (v["ar"], bc(o1(A[pre + "adaptive_range"]), (P, 1)))]
                v["w4r"], v["g3r"] = scratch.take((P,)), scratch.take((P,))
                v["yS"] = scratch.take((DK, T))
                v["h1"] = scratch.take((DK, T))
                v["h2"] = scratch.take((T,))
                v["h3"] = scratch.take((T,))
                v["th"] = scratch.take((NC, CH))
                v["tmp"] = scratch.take((2, CH))
                v["msum"] = scratch.take((DK, NC))
                v["mean"] = scratch.take((DK, B))
                v["gh1"], v["gh2"], v["gt"] = scratch.take((B,)), scratch.take((B,)), scratch.take((B,))
                v["al"], v["be"] = scratch.take((1,)), scratch.take((B,))
                v["hb"] = scratch.take((2,))
            if L == 1:
                v["w1"], v["w2"] = w.take((FT1, D)), w.take((DK, F1))
                v["b1"] = w.take((FT1,))
                v["b2"] = w.take((D,))
                ld += [(v["w1"], A[pre + "w1"].rearrange("(f p) d -> p f d", p=P)),
                       (v["w2"], A[pre + "w2"].rearrange("(k p) f -> p k f", p=P)),
                       (v["b1"], col(A[pre + "b1"], FT1)), (v["b2"], row(A[pre + "b2"], D))]
                v["xi"] = scratch.take((NT, D), BF16)
                v["xT"] = scratch.take((DK, T), BF16)
                v["hi"] = scratch.t[:, 0:FT1 * T // 2].bitcast(BF16).rearrange("p (f t) -> p f t", f=FT1)
                assert scratch.at == FT1 * T // 2
                v["wi1"] = scratch.take((FT1, D), BF16)
                v["wi2"] = scratch.take((DK, F1), BF16)
                v["w1T"] = scratch.take((DK, F1), BF16)
                v["w2T"] = scratch.take((FT1, D), BF16)
                v["h"] = scratch.take((FT1, T))
                v["sw1"], v["iw1"] = scratch.take((FT1,)), scratch.take((FT1,))
                v["sw2"], v["iw2"] = scratch.take((DK,)), scratch.take((DK,))
                v["diag"] = scratch.take((DK, P))
                v["sw2r"] = scratch.take((D,))
                v["rowS"], v["rowT"], v["rowB"], v["rowI"] = (scratch.take((D,)) for _ in range(4))
                v["m"] = scratch.take((64,))
                v["sc"] = scratch.take((16,))
                v["sb1"], v["ib1"], v["bq1"] = scratch.take((FT1,)), scratch.take((FT1,)), scratch.take((FT1,))
                v["dn"] = scratch.take((2, 2, D))
                v["rnd"] = scratch.take((1,))
            if L >= 2:
                E = E2 if L == 2 else E3
                v["Wr"], v["br"] = w.take((DK, E)), w.take((E,))
                ld += [(v["Wr"], kin(A[pre + ("Wr" if L == 2 else "router_w")])),
                       (v["br"], row(A[pre + ("br" if L == 2 else "router_b")], E))]
                v["lg"], v["G"], v["oh"], v["pre"] = (scratch.take((NT, E)) for _ in range(4))
                v["oh2"] = scratch.take((NT, E))
                v["top"] = scratch.take((NT, 8))
                v["idx"] = scratch.take((NT, 8), U32)
                v["idf"] = scratch.take((NT, 8))
                v["r"] = scratch.take((12, NT))
                v["GT"] = scratch.take((T,))
            if L == 2:
                v["b1"], v["b2"] = w.take((E2, H2 // P)), w.take((D,))
                ld += [(v["b1"][:, e, :], A[pre + "b1"][e, :].rearrange("(m p) -> p m", p=P)) for e in range(E2)]
                ld += [(v["b2"][0:E2], A[pre + "b2"])]
                v["W1"] = scratch.take((3, DK, H2))
                v["W2"] = scratch.take((3, H2 // P, D))
                v["hT"] = scratch.take((3, H2 // P, CH))
            if L == 3:
                v["ohb"] = scratch.take((NT, E), BF16)
                v["ohs"] = scratch.take((NT, E), BF16)
                v["Wg"] = scratch.take((3, DK, F3))
                v["Wu"] = scratch.take((3, DK, F3))
                v["Wd"] = scratch.take((3, 3, D))
                v["sg"] = scratch.take((4, CH))
                v["hT"] = scratch.take((2 * 3, CH))
                v["xe"] = scratch.take((3, 3, D))
                v["xeT"] = scratch.take((2 * DK, CAP))
                v["ye"] = scratch.take((3, 3, D))
                v["dump"], v["slot"], v["row"] = scratch.take((NT, 2)), scratch.take((NT, 2)), scratch.take((NT, 2))
                v["pk"], v["wk"] = scratch.take((NT, 2)), scratch.take((NT, 2))
                v["sidx"], v["gidx"] = scratch.take((2 * NT,), U32), scratch.take((2 * NT,), U32)
                v["yk"] = scratch.take((NT, D))
            ph.append(v)
            loads.append(ld)
        NPH = PHASES

        x_slots = nc.dram_tensor("x_slots", (E3 * CAP + 2 * T, D), F32, kind="Internal").ap()
        y_slots = nc.dram_tensor("y_slots", (E3 * CAP, D), F32, kind="Internal").ap()
        ROUTED = [(E3, -1)] + [(e, e) for e in range(E3)]

        def lnorm(p, c):
            return NC * p + c + 1

        ATT = [("front", 0), ("front", 1), ("back", 0), ("front", 2), ("tail", 0), ("back", 1),
               ("front", 3), ("tail", 1), ("back", 2), ("tail", 2), ("back", 3), ("tail", 3)]
        UNITS = [(c, q) for c in range(NC) for q in range(2)]

        def expert_order(E):
            ups = [(e, c) for e in range(E) for c in range(NC)]
            o = []
            for i, u in enumerate(ups):
                o.append(("up",) + u)
                if i >= 1:
                    o.append(("down",) + ups[i - 1])
            o.append(("down",) + ups[-1])
            return o

        block = ctx.enter_context(nc.Block())

        @block.tensor
        def _(pe):
            def transpose_y(p, v, c):
                pe.wait_ge(ln_y, lnorm(p, c))
                for d in range(DK):
                    bk = RA.take(pe, p, "yT", c, d)
                    for i in range(TPC):
                        last = pe.transpose(bk[:, i * P:(i + 1) * P], v["Y"][:, TPC * c + i, d * P:(d + 1) * P], ident[:])
                    last.then_inc(RA.filled, 1)

            def attention(p, L):
                v = ph[p]
                H, hd, MT, hpm, G, HD = (v[k] for k in ("H", "hd", "MT", "hpm", "G", "HD"))
                pe.wait_ge(w_loaded[p], 16 * len(loads[p]))
                if L == 0:
                    pe.wait_ge(consts, NCONST)
                    pe.wait_ge(in_loaded, 16 * NIN)
                    for b in range(B):
                        bk = RA.take(pe, p, "ctx", b)
                        pe.transpose(bk[:, 0:P], ctxN[:, b, 0:P], ident[:])
                        pe.transpose(bk[:, P:M], ctxN[0:MR, B + b, 0:P], ident[0:MR, 0:MR])
                        pe.transpose(bk[0:CD - P, 160:160 + P], ctxN[:, b, P:CD], ident[:])
                        pe.transpose(bk[0:CD - P, 160 + P:160 + M], ctxN[0:MR, B + b, P:CD],
                                     ident[0:MR, 0:MR]).then_inc(RA.filled, 1)
                    pe.wait_ge(RA.read, RA.n(p, "ctx", B - 1))
                if L < 3:
                    for m in range(MT):
                        bk = RB.take(pe, p, "k", m)
                        pe.matmul(bk[:, 0:B * M], v["Wk"][:, 0, m * P:(m + 1) * P], ctxT[:, 0, :], start=True, stop=False)
                        pe.matmul(bk[:, 0:B * M], v["Wk"][0:CD - P, 1, m * P:(m + 1) * P], ctxT[0:CD - P, 1, :],
                                  start=False, stop=True).then_inc(RB.filled, 1)

                def ctx_rows(kind, w):
                    for b in range(B):
                        for s, (k0, kn) in enumerate(((0, P), (P, MR))):
                            bk = RB.take(pe, p, kind, b, s)
                            o = b * M + k0
                            pe.matmul(bk[0:kn, 0:HD], ctxT[:, 0, o:o + kn], w[:, 0, :], start=True, stop=False)
                            pe.matmul(bk[0:kn, 0:HD], ctxT[0:CD - P, 1, o:o + kn], w[0:CD - P, 1, :],
                                      start=False, stop=True).then_inc(RB.filled, 1)

                ctx_rows("v", v["Wv"])
                if L == 3:
                    ctx_rows("kp", v["Wk"])
                    pe.wait_ge(kn_made, 1)
                    for m in range(MT):
                        bk = RB.take(pe, p, "k", m)
                        for b in range(B):
                            pe.transpose(bk[:, b * M:b * M + P], v["Kp"][:, 2 * b, m * P:(m + 1) * P], ident[:])
                            last = pe.transpose(bk[:, b * M + P:(b + 1) * M], v["Kp"][0:MR, 2 * b + 1, m * P:(m + 1) * P],
                                                ident[0:MR, 0:MR])
                        last.then_inc(RB.filled, 1)
                for what, c in ATT:
                    b = c // CPB
                    cs = slice(c * CH, (c + 1) * CH)
                    if what == "front":
                        transpose_y(p, v, c)
                        pe.wait_ge(RA.read, RA.n(p, "yT", c, DK - 1))
                        if L == 3:
                            for q in range(2):
                                bk = RB.take(pe, p, "qp", c, q)
                                for i in range(2):
                                    tt = 2 * q + i
                                    for k in range(DK):
                                        last = pe.matmul(bk[:, i * D:(i + 1) * D], v["yT"][:, k, tt * P:(tt + 1) * P],
                                                         v["Wq"][:, k, :], start=k == 0, stop=k == DK - 1)
                                last.then_inc(RB.filled, 1)
                            pe.wait_ge(qn_made, c + 1)
                            for m in range(MT):
                                bk = RA.take(pe, p, "q", c, m)
                                for i in range(TPC):
                                    last = pe.transpose(bk[:, i * P:(i + 1) * P],
                                                        v["Y"][:, TPC * c + i, m * P:(m + 1) * P], ident[:])
                                last.then_inc(RA.filled, 1)
                            continue
                        for m in range(MT):
                            bk = RA.take(pe, p, "q", c, m)
                            for k in range(DK):
                                last = pe.matmul(bk[:], v["Wq"][:, k, m * P:(m + 1) * P], v["yT"][:, k, :],
                                                 start=k == 0, stop=k == DK - 1)
                            last.then_inc(RA.filled, 1)
                        pe.wait_ge(RA.read, RA.n(p, "q", c, MT - 1))
                        pe.wait_ge(kz_made, sum(B * ph[2 * l]["MT"] for l in range(L + 1)))
                        if L == 0:
                            pe.wait_ge(mb_made, 1)
                        for i in range(TPC):
                            q0 = c * CH + i * P
                            for m in range(MT):
                                for h0 in range(0, hpm, 3):
                                    hn = min(3, hpm - h0)
                                    bk = RB.take(pe, p, "mxs", c, i, m, h0)
                                    last = pe.matmul(bk[:, 0:hn * M], v["QT"][:, m, q0:q0 + P],
                                                     v["Kz"][:, m * B + b, h0:h0 + hn, :].rearrange("p h k -> p (h k)"),
                                                     start=True, stop=L > 0)
                                    if L == 0:
                                        for j in range(hn):
                                            last = pe.matmul(bk[:, j * M:(j + 1) * M], onesb[64:65, :], v["mb"][64:65, b, :],
                                                             start=False, stop=j == hn - 1)
                                    last.then_inc(RB.filled, 1)
                    elif what == "back":
                        pe.wait_ge(kr_made, sum(B * ph[2 * l]["MT"] for l in range(L + 1)))
                        if L == 3:
                            pe.wait_ge(RA.read, RA.n(p, "q", c, MT - 1))
                            pe.wait_ge(kz_made, sum(B * ph[2 * l]["MT"] for l in range(L + 1)))
                        pe.wait_ge(v_made, 4 * (L + 1))
                        if L < 3:
                            pe.wait_ge(RB.read, RB.n(p, "mxs", c, TPC - 1, MT - 1, (hpm - 1) // 3 * 3))
                            bk = RB.take(pe, p, "mx", c)
                            for i in range(TPC):
                                last = pe.transpose(bk[0:H, i * P:(i + 1) * P], v["mx"][:, TPC * c + i, :], ident[:])
                            last.then_inc(RB.filled, 1)
                        if L == 0:
                            pe.wait_ge(sel0_made, 1)
                        for g in range(G + 1):
                            if g < G:
                                for j in range(4):
                                    h = 4 * g + j
                                    bk = RC.take(pe, p, "s", c, g, j)
                                    last = pe.matmul(bk[:], v["Kz"][:, (h // hpm) * B + b, h % hpm, 0:P], v["QT"][:, h // hpm, cs],
                                                     start=True, stop=L == 3)
                                    if L < 3:
                                        if g == 0 and j == 0:
                                            pe.wait_ge(RB.read, RB.n(p, "mx", c))
                                        s = v["sel"][0:65, b * H + h, :] if L == 0 else sel[0:65, h, :]
                                        last = pe.matmul(bk[:], s, v["negm"][0:65, c, :], start=False, stop=True)
                                    last.then_inc(RC.filled, 1)
                                bk = RC.take(pe, p, "s", c, g, 4)
                                mts = sorted({(4 * g + j) // hpm for j in range(4)})
                                if L < 3:
                                    s = v["selr"][0:65, b * 4 + g, :, :] if L == 0 else selr[0:65, g, :, :]
                                    pe.matmul(bk[:], s.rearrange("p j k -> p (j k)"), v["negm"][0:65, c, :],
                                              start=True, stop=False)
                                for m in mts:
                                    n = P // len(mts)
                                    o = (m - mts[0]) * n
                                    h0 = (4 * g) % hpm
                                    last = pe.matmul(bk[o:o + n, :],
                                                     v["Kr"][:, m * B + b, h0:h0 + n // 32, :].rearrange("p h k -> p (h k)"),
                                                     v["QT"][:, m, cs], start=L == 3, stop=True)
                                last.then_inc(RC.filled, 1)
                            if g > 0:
                                gg = g - 1
                                slot = (c * G + gg) % v["NPT"]
                                pe.wait_ge(RC.read, RC.n(p, "s", c, gg, 4))
                                if hd == 16:
                                    bk = RB.take(pe, p, "av", c, gg)
                                    for j in range(4):
                                        pe.matmul(bk[32 * j:32 * (j + 1), :], v["V"][:, b, 4 * gg + j, :],
                                                  v["PT"][:, slot, j, :], start=True, stop=False)
                                    for j in range(4):
                                        last = pe.matmul(bk[32 * j:32 * (j + 1), :], v["Vr"][:, b, gg, j, :],
                                                         v["PT"][:, slot, 4, :], start=False, stop=True)
                                    last.then_inc(RB.filled, 1)
                                    continue
                                w = hd + 1
                                for i in range(TPC):
                                    bk = RB.take(pe, p, "av", c, gg, i)
                                    qs = slice(i * P, (i + 1) * P)
                                    pe.matmul(bk[:, 0:4 * w], v["PT"][:, slot, 4, qs],
                                              v["Vr"][:, b, gg, :, :].rearrange("p j d -> p (j d)"), start=True, stop=False)
                                    for j in range(4):
                                        last = pe.matmul(bk[:, j * w:(j + 1) * w], v["PT"][:, slot, j, qs],
                                                         v["V"][:, b, 4 * gg + j, :], start=False, stop=j == 3)
                                    last.then_inc(RB.filled, 1)
                    else:
                        if hd == 16:
                            pe.wait_ge(RB.read, RB.n(p, "av", c, G - 1))
                            outs = [v["OT"][:, g, :] for g in range(G)]
                        else:
                            pe.wait_ge(RB.read, RB.n(p, "av", c, G - 1, TPC - 1))
                            for m in range(MT):
                                bk = RA.take(pe, p, "oT", c, m)
                                for i in range(TPC):
                                    last = pe.transpose(bk[:, i * P:(i + 1) * P], v["O"][:, c % 2, i, m * P:(m + 1) * P], ident[:])
                                last.then_inc(RA.filled, 1)
                            pe.wait_ge(RA.read, RA.n(p, "oT", c, MT - 1))
                            outs = [v["QT"][:, m, cs] for m in range(MT)]
                        for q in range(2):
                            bk = RB.take(pe, p, "out", c, q)
                            for i in range(2):
                                tt = 2 * q + i
                                for m, o in enumerate(outs):
                                    last = pe.matmul(bk[:, i * D:(i + 1) * D], o[:, tt * P:(tt + 1) * P],
                                                     v["Wo"][:, m, :], start=m == 0, stop=m == len(outs) - 1)
                            last.then_inc(RB.filled, 1)

            def coupling(p):
                v = ph[p]
                pe.wait_ge(w_loaded[p], 16 * len(loads[p]))
                for c in range(NC):
                    transpose_y(p, v, c)
                pe.wait_ge(gc_ready, 1)
                bk = RA.take(pe, p, "g1")
                for k in range(DK):
                    last = pe.matmul(bk[:, 0:B], v["g1"][:, k, :], v["mean"][:, k, :], start=k == 0, stop=k == DK - 1)
                last.then_inc(RA.filled, 1)
                pe.wait_ge(RA.read, RA.n(p, "g1"))
                bk = RA.take(pe, p, "g2")
                pe.matmul(bk[0:64, 0:B], v["g2"][:], v["gh1"][:], start=True, stop=True).then_inc(RA.filled, 1)
                pe.wait_ge(RA.read, RA.n(p, "g2"))
                bk = RA.take(pe, p, "g3")
                pe.matmul(bk[:, 0:B], v["g3r"][0:64], v["gh2"][0:64], start=True, stop=True).then_inc(RA.filled, 1)
                st = [v["yT"], v["yS"]]
                for r in range(3):
                    for c in range(NC):
                        cs = slice(c * CH, (c + 1) * CH)
                        if r:
                            pe.wait_ge(state_made, NC * (r - 1) + c + 1)
                        for m in range(DK):
                            bk = RC.take(pe, p, r, "l1", c, m)
                            for k in range(DK):
                                last = pe.matmul(bk[:], v["w1"][:, k, m * P:(m + 1) * P], st[r % 2][:, k, cs],
                                                 start=k == 0, stop=k == DK - 1)
                            last.then_inc(RC.filled, 1)
                    for c in range(NC):
                        cs = slice(c * CH, (c + 1) * CH)
                        pe.wait_ge(RC.read, RC.n(p, r, "l1", c, DK - 1))
                        bk = RC.take(pe, p, r, "l2", c)
                        for k in range(DK):
                            last = pe.matmul(bk[:], v["w2"][:, k, :], v["h1"][:, k, cs], start=k == 0, stop=k == DK - 1)
                        last.then_inc(RC.filled, 1)
                    for c in range(NC):
                        cs = slice(c * CH, (c + 1) * CH)
                        pe.wait_ge(RC.read, RC.n(p, r, "l2", c))
                        bk = RC.take(pe, p, r, "l3", c)
                        pe.matmul(bk[0:64, :], v["w3"][:], v["h2"][:, cs], start=True, stop=True).then_inc(RC.filled, 1)
                    for c in range(NC):
                        cs = slice(c * CH, (c + 1) * CH)
                        pe.wait_ge(RC.read, RC.n(p, r, "l3", c))
                        bk = RC.take(pe, p, r, "l4", c)
                        pe.matmul(bk[:], v["w4r"][:], v["h3"][:, cs], start=True, stop=True).then_inc(RC.filled, 1)
                for c in range(NC):
                    pe.wait_ge(state_made, NC * 2 + c + 1)
                    for q in range(2):
                        bk = RB.take(pe, p, "fin", c, q)
                        for i in range(2):
                            t = (2 * c + q) * 2 + i
                            for k in range(DK):
                                last = pe.transpose(bk[:, i * D + k * P:i * D + (k + 1) * P], st[1][:, k, t * P:(t + 1) * P], ident[:])
                        last.then_inc(RB.filled, 1)

            def quantised(p):
                v = ph[p]
                pe.wait_ge(wq_made, 1)
                for d in range(DK):
                    bk = RA.take(pe, p, "w1T", d)
                    o = bk[:].bitcast(BF16)
                    for f in range(FT1):
                        last = pe.transpose(o[:, f * P:(f + 1) * P], v["wi1"][:, f, d * P:(d + 1) * P], identb[:])
                    last.then_inc(RA.filled, 1)
                for d in range(DK):
                    bk = RA.take(pe, p, "w2T", d)
                    o = bk[:].bitcast(BF16)
                    for f in range(FT1):
                        last = pe.transpose(o[:, f * P:(f + 1) * P], v["wi2"][:, d, f * P:(f + 1) * P], identb[:])
                    last.then_inc(RA.filled, 1)
                pe.wait_ge(diag_made, 1)
                bk = RB.take(pe, p, "sw2r")
                for d in range(DK):
                    last = pe.matmul(bk[:, d * P:(d + 1) * P], ones[:], v["diag"][:, d, :], start=True, stop=True)
                last.then_inc(RB.filled, 1)
                for c in range(NC):
                    pe.wait_ge(xi_made, c + 1)
                    bk = RA.take(pe, p, "xT", c)
                    o = bk[:].bitcast(BF16)
                    for d in range(DK):
                        for i in range(TPC):
                            last = pe.transpose(o[:, d * CH + i * P:d * CH + (i + 1) * P],
                                                v["xi"][:, TPC * c + i, d * P:(d + 1) * P], identb[:])
                    last.then_inc(RA.filled, 1)
                for c in range(NC):
                    cs = slice(c * CH, (c + 1) * CH)
                    pe.wait_ge(RA.read, RA.n(p, "xT", c))
                    for f in range(FT1):
                        bk = RC.take(pe, p, "up", c, f)
                        for k in range(DK):
                            last = pe.matmul(bk[:], v["w1T"][:, k, f * P:(f + 1) * P], v["xT"][:, k, cs], start=k == 0, stop=k == DK - 1)
                        last.then_inc(RC.filled, 1)
                for c in range(NC):
                    pe.wait_ge(hi_made, c + 1)
                    for q in range(2):
                        bk = RB.take(pe, p, "dn", c, q)
                        for i in range(2):
                            t = (2 * c + q) * 2 + i
                            for f in range(FT1):
                                last = pe.matmul(bk[:, i * D:(i + 1) * D], v["hi"][:, f, t * P:(t + 1) * P], v["w2T"][:, f, :],
                                                 start=f == 0, stop=f == FT1 - 1)
                        last.then_inc(RB.filled, 1)

            def route(p, L):
                v = ph[p]
                E = E2 if L == 2 else E3
                pe.wait_ge(w_loaded[p], 16 * len(loads[p]))
                for c in range(NC):
                    transpose_y(p, v, c)
                    pe.wait_ge(RA.read, RA.n(p, "yT", c, DK - 1))
                    bk = RB.take(pe, p, "lg", c)
                    for i in range(TPC):
                        t = TPC * c + i
                        for k in range(DK):
                            last = pe.matmul(bk[:, i * E:(i + 1) * E], v["yT"][:, k, t * P:(t + 1) * P], v["Wr"][:, k, :],
                                             start=k == 0, stop=k == DK - 1)
                    last.then_inc(RB.filled, 1)

            def dense_experts(p):
                v = ph[p]
                E = E2
                route(p, 2)
                pe.wait_ge(g_made, 1)
                for c in range(NC):
                    bk = RA.take(pe, p, "gT", c)
                    for i in range(TPC):
                        last = pe.transpose(bk[0:E, i * P:(i + 1) * P], v["G"][:, TPC * c + i, :], ident[:])
                    last.then_inc(RA.filled, 1)
                for c in range(NC):
                    pe.wait_ge(RA.read, RA.n(p, "gT", c))
                    for q in range(2):
                        bk = RB.take(pe, p, "b2", c, q)
                        for i in range(2):
                            t = (2 * c + q) * 2 + i
                            last = pe.matmul(bk[:, i * D:(i + 1) * D], v["GT"][0:E, t * P:(t + 1) * P], v["b2"][0:E, :],
                                             start=True, stop=True)
                        last.then_inc(RB.filled, 1)
                for what, e, c in expert_order(E):
                    s = e % 3
                    hs = (e * NC + c) % 3
                    cs = slice(c * CH, (c + 1) * CH)
                    if what == "up":
                        if c == 0:
                            pe.wait_ge(ew_loaded[2][s], 16 * EWN[2] * (e // 3 + 1))
                        for m in range(H2 // P):
                            bk = RC.take(pe, p, "up", e, c, m)
                            for k in range(DK):
                                last = pe.matmul(bk[:], v["W1"][:, s, k, m * P:(m + 1) * P], v["yT"][:, k, cs],
                                                 start=k == 0, stop=k == DK - 1)
                            last.then_inc(RC.filled, 1)
                        continue
                    pe.wait_ge(RC.read, RC.n(p, "up", e, c, H2 // P - 1))
                    for q in range(2):
                        bk = RB.take(pe, p, "dn", e, c, q)
                        for i in range(2):
                            tt = q * 2 + i
                            for m in range(H2 // P):
                                last = pe.matmul(bk[:, i * D:(i + 1) * D], v["hT"][:, hs, m, tt * P:(tt + 1) * P],
                                                 v["W2"][:, s, m, :], start=m == 0, stop=m == H2 // P - 1)
                        last.then_inc(RB.filled, 1)

            def routed_experts(p):
                v = ph[p]
                route(p, 3)
                pe.wait_ge(oh_made, 1)
                bk = RB.take(pe, p, "pos")
                for t in range(NT):
                    last = pe.matmul(bk[:, t * E3:(t + 1) * E3], before[:], v["ohb"][:, t, :], start=True, stop=t == 0)
                    if t:
                        last = pe.matmul(bk[:, t * E3:(t + 1) * E3], onesb[:], v["ohs"][:, t, :], start=False, stop=True)
                last.then_inc(RB.filled, 1)

                def gate_up(s, key, moving, n):
                    for m in range(3):
                        fn = F3T[m]
                        for ring, w, name in ((RA, v["Wg"], "gate"), (RB, v["Wu"], "up")):
                            bk = ring.take(pe, p, name, *key, m)
                            for k in range(DK):
                                last = pe.matmul(bk[0:fn, 0:n], w[:, s, k, m * P:m * P + fn], moving(k),
                                                 start=k == 0, stop=k == DK - 1)
                            last.then_inc(ring.filled, 1)

                pe.wait_ge(ew_loaded[3][0], 16 * EWN[3])
                for what, e, c in expert_order(1):
                    if what == "up":
                        gate_up(0, (E3, c), lambda k: v["yT"][:, k, c * CH:(c + 1) * CH], CH)
                        continue
                    pe.wait_ge(RB.read, RB.n(p, "up", E3, c, 2))
                    for q in range(2):
                        bk = RB.take(pe, p, "dn", E3, c, q)
                        for i in range(2):
                            tt = q * 2 + i
                            for m in range(3):
                                fn = F3T[m]
                                last = pe.matmul(bk[:, i * D:(i + 1) * D], v["hT"][0:fn, c % 2 * 3 + m, tt * P:(tt + 1) * P],
                                                 v["Wd"][0:fn, 0, m, :], start=m == 0, stop=m == 2)
                        last.then_inc(RB.filled, 1)

                def tokens_of(e):
                    pe.wait_ge(xe_loaded[e % 3], 16 * 2 * (e // 3 + 1))
                    for d in range(DK):
                        bk = RA.take(pe, p, "xeT", e, d)
                        for i, n in enumerate((P, P, CAP - 2 * P)):
                            last = pe.transpose(bk[:, i * P:i * P + n], v["xe"][0:n, e % 3, i, d * P:(d + 1) * P], ident[0:n, 0:n])
                        last.then_inc(RA.filled, 1)

                tokens_of(0)
                for e in range(E3):
                    s = (e + 1) % 3
                    pe.wait_ge(ew_loaded[3][s], 16 * EWN[3] * ((e + 1) // 3 + 1))
                    pe.wait_ge(RA.read, RA.n(p, "xeT", e, DK - 1))
                    gate_up(s, (e, 0), lambda k: v["xeT"][:, e % 2 * DK + k, :], CAP)
                    if e + 1 < E3:
                        tokens_of(e + 1)
                    pe.wait_ge(RB.read, RB.n(p, "up", e, 0, 2))
                    for q, tiles in enumerate(((0, 1), (2,))):
                        bk = RC.take(pe, p, "dn", e, q)
                        for i in tiles:
                            n = min(P, CAP - i * P)
                            for m in range(3):
                                fn = F3T[m]
                                last = pe.matmul(bk[0:n, i % 2 * D:(i % 2 + 1) * D], v["hT"][0:fn, e % 2 * 3 + m, i * P:i * P + n],
                                                 v["Wd"][0:fn, s, m, :], start=m == 0, stop=m == 2)
                        last.then_inc(RC.filled, 1)

            for p in range(NPH):
                L = p // 2
                if p:
                    pe.wait_ge(phase_over, p)
                if p % 2 == 0:
                    attention(p, L)
                elif L == 0:
                    coupling(p)
                elif L == 1:
                    quantised(p)
                elif L == 2:
                    dense_experts(p)
                else:
                    routed_experts(p)

        @block.scalar
        def _(act):
            st = Steps(act, act_st)
            act.wait_ge(in_loaded, 16 * NIN)
            act.activation(tg[:], gates[:], ACT.Tanh).then_inc(tg_made, 1)

            def yT(p, v, c):
                for d in range(DK):
                    bk = RA.get(act, p, "yT", c, d)
                    o = v["yT"][:, d, :] if p % 2 == 0 else v["yT"][:, d, c * CH:(c + 1) * CH]
                    act.activation(o, bk[:], ACT.Copy).then_inc(RA.read, 1)

            def attention(p, L):
                v = ph[p]
                H, hd, MT, hpm, G, HD = (v[k] for k in ("H", "hd", "MT", "hpm", "G", "HD"))
                if L == 0:
                    for b in range(B):
                        bk = RA.get(act, p, "ctx", b)
                        act.activation(ctxT[:, 0, b * M:(b + 1) * M], bk[:, 0:M], ACT.Copy)
                        act.activation(ctxT[0:CD - P, 1, b * M:(b + 1) * M], bk[0:CD - P, 160:160 + M], ACT.Copy)\
                           .then_inc(RA.read, 1)
                if L == 2:
                    act.wait_ge(w_loaded[p], 16 * len(loads[p]))
                if L == 3:
                    act.wait_ge(kn_clear, 1)
                    for i in range(4):
                        n = P if i % 2 == 0 else MR
                        act.wait_ge(RB.read, RB.n(p, "kp", i // 2, i % 2))
                        if i:
                            st.wait()
                        st.did(act.activation(v["junk"][0:n], v["Kp"][0:n, i, :], ACT.Square,
                                              accum_out=v["ss"][0:n, NT + i:NT + i + 1]))
                    st.wait()
                    act.sem_inc(kss_made, 1)
                for what, c in ATT:
                    cs = slice(c * CH, (c + 1) * CH)
                    if what == "front":
                        yT(p, v, c)
                        if L == 3:
                            act.wait_ge(RB.read, RB.n(p, "qp", c, 1))
                            for i in range(TPC):
                                t = TPC * c + i
                                st.wait()
                                ins = act.activation(v["junk"][:], v["Qp"][:, t, :], ACT.Square, accum_out=v["ss"][:, t:t + 1])
                                st.did(ins)
                            st.wait()
                            act.sem_inc(qss_made, 1)
                        for m in range(MT):
                            bk = RA.get(act, p, "q", c, m)
                            if L == 2:
                                ins = act.activation(v["QT"][:, m, cs], bk[:], ACT.Identity, bias=v["bq"][:, m:m + 1])
                            else:
                                ins = act.activation(v["QT"][:, m, cs], bk[:], ACT.Copy)
                            ins.then_inc(RA.read, 1)
                    elif what == "back":
                        for g in range(G):
                            n = c * G + g
                            if n >= v["NPT"]:
                                pc, pg = divmod(n - v["NPT"], G)
                                act.wait_ge(RB.filled, RB.n(p, "av", pc, pg) if hd == 16 else RB.n(p, "av", pc, pg, TPC - 1))
                            for j in range(5):
                                bk = RC.get(act, p, "s", c, g, j)
                                act.activation(v["PT"][:, n % v["NPT"], j, :], bk[:], ACT.Exp, scale=float(hd) ** -0.5)\
                                   .then_inc(RC.read, 1)
                    elif hd == 64:
                        for m in range(MT):
                            bk = RA.get(act, p, "oT", c, m)
                            act.activation(v["QT"][:, m, cs], bk[:], ACT.Copy).then_inc(RA.read, 1)

            def coupling(p):
                v = ph[p]
                act.wait_ge(w_loaded[p], 16 * len(loads[p]))
                for c in range(NC):
                    yT(p, v, c)
                bk = RA.get(act, p, "g1")
                act.activation(v["gh1"][:], bk[:, 0:B], ACT.Gelu, bias=v["gb1"][:]).then_inc(RA.read, 1)
                bk = RA.get(act, p, "g2")
                act.activation(v["gh2"][0:64], bk[0:64, 0:B], ACT.Gelu, bias=v["gb2"][0:64]).then_inc(RA.read, 1)
                bk = RA.get(act, p, "g3")
                act.activation(v["gt"][:], bk[:, 0:B], ACT.Tanh, bias=v["hb"][:, 1:2], scale=0.5).then_inc(RA.read, 1)
                for r in range(3):
                    for c in range(NC):
                        for m in range(DK):
                            bk = RC.get(act, p, r, "l1", c, m)
                            act.activation(v["h1"][:, m, c * CH:(c + 1) * CH], bk[:], ACT.Gelu, bias=v["b1"][:, m:m + 1])\
                               .then_inc(RC.read, 1)
                    for c in range(NC):
                        bk = RC.get(act, p, r, "l2", c)
                        act.activation(v["h2"][:, c * CH:(c + 1) * CH], bk[:], ACT.Gelu, bias=v["b2"][:]).then_inc(RC.read, 1)
                    for c in range(NC):
                        bk = RC.get(act, p, r, "l3", c)
                        act.activation(v["h3"][0:64, c * CH:(c + 1) * CH], bk[0:64, :], ACT.Gelu, bias=v["b3"][0:64])\
                           .then_inc(RC.read, 1)
                    for c in range(NC):
                        bk = RC.get(act, p, r, "l4", c)
                        act.activation(v["th"][:, c, :], bk[:], ACT.Tanh, bias=v["hb"][:, 0:1], scale=0.5).then_inc(RC.read, 1)

            def quantised(p):
                v = ph[p]
                for d in range(DK):
                    bk = RA.get(act, p, "w1T", d)
                    act.activation(v["w1T"][:, d, :], bk[:].bitcast(BF16), ACT.Copy).then_inc(RA.read, 1)
                for d in range(DK):
                    bk = RA.get(act, p, "w2T", d)
                    act.activation(v["w2T"][:, :, d * P:(d + 1) * P],
                                   bk[:].bitcast(BF16).rearrange("p (f j) -> p f j", j=P), ACT.Copy).then_inc(RA.read, 1)
                for c in range(NC):
                    bk = RA.get(act, p, "xT", c)
                    act.activation(v["xT"][:, :, c * CH:(c + 1) * CH],
                                   bk[:].bitcast(BF16).rearrange("p (d j) -> p d j", d=DK), ACT.Copy).then_inc(RA.read, 1)
                act.wait_ge(hscale_made, 1)
                for c in range(NC):
                    for f in range(FT1):
                        bk = RC.get(act, p, "up", c, f)
                        act.activation(v["h"][:, f, c * CH:(c + 1) * CH], bk[:], ACT.Relu,
                                       bias=v["bq1"][:, f:f + 1], scale=v["sb1"][:, f:f + 1]).then_inc(RC.read, 1)

            def dense_experts(p):
                v = ph[p]
                act.wait_ge(w_loaded[p], 16 * len(loads[p]))
                for c in range(NC):
                    yT(p, v, c)
                act.wait_ge(ex_ready, 1)
                act.activation(v["r"][:, 1, :], v["r"][:, 0, :], ACT.Exp).then_inc(ex_made, 1)
                for c in range(NC):
                    bk = RA.get(act, p, "gT", c)
                    act.activation(v["GT"][0:E2, c * CH:(c + 1) * CH], bk[0:E2, :], ACT.Copy).then_inc(RA.read, 1)
                for what, e, c in expert_order(E2):
                    if what == "up":
                        for m in range(H2 // P):
                            bk = RC.get(act, p, "up", e, c, m)
                            act.activation(v["hT"][:, (e * NC + c) % 3, m, :], bk[:], ACT.Relu,
                                           bias=v["b1"][:, e, m:m + 1]).then_inc(RC.read, 1)

            def routed_experts(p):
                v = ph[p]
                for c in range(NC):
                    yT(p, v, c)
                act.wait_ge(ex_ready, 2)
                act.activation(v["pre"][:], v["lg"][:], ACT.Exp).then_inc(ex_made, 1)
                items = [(E3, c, m) for c in range(NC) for m in range(3)] + [(e, 0, m) for e in range(E3) for m in range(3)]

                def silu(n, width):
                    e, c, m = items[n]
                    fn = F3T[m]
                    if n >= 4:
                        act.wait_ge(RB.read, RB.n(p, "up", *items[n - 4]))
                    bk = RA.get(act, p, "gate", e, c, m)
                    act.activation(v["sg"][0:fn, n % 4, 0:width], bk[0:fn, 0:width], ACT.Silu).then_inc(RA.read, 1)

                for n in range(3 * NC):
                    silu(n, CH)

                def tokens_of(e):
                    for d in range(DK):
                        bk = RA.get(act, p, "xeT", e, d)
                        act.activation(v["xeT"][:, e % 2 * DK + d, :], bk[:, 0:CAP], ACT.Copy).then_inc(RA.read, 1)

                tokens_of(0)
                for e in range(E3):
                    for m in range(3):
                        silu(3 * NC + 3 * e + m, CAP)
                    if e + 1 < E3:
                        tokens_of(e + 1)
                    if e >= 3:
                        act.wait_ge(ye_stored[e % 3], 16 * 2 * (e // 3))
                    bk = RC.get(act, p, "dn", e, 0)
                    act.activation(v["ye"][:, e % 3, 0:2, :], bk[:].rearrange("p (t d) -> p t d", t=2), ACT.Copy)\
                       .then_inc(RC.read, 1)
                    n = CAP - 2 * P
                    bk = RC.get(act, p, "dn", e, 1)
                    act.activation(v["ye"][0:n, e % 3, 2, :], bk[0:n, 0:D], ACT.Copy).then_inc(RC.read, 1)

            for p in range(NPH):
                L = p // 2
                if p:
                    act.wait_ge(phase_over, p)
                if p % 2 == 0:
                    attention(p, L)
                elif L == 0:
                    coupling(p)
                elif L == 1:
                    quantised(p)
                elif L == 2:
                    dense_experts(p)
                else:
                    routed_experts(p)

        @block.gpsimd
        def _(pool):
            st = Steps(pool, pool_st)
            for a in (ident, identb, sel, selr):
                st.did(pool.memset(a[:], 0.0))
            for a in (hmask[16], hmask[64], before, ones, sgn):
                st.did(pool.memset(a[:], 1.0))
            st.did(pool.memset(nhalf[:], -0.5))
            pool.memset(zeros[:], 0.0)
            pool.memset(WoP[:], 0.0).then_inc(zero_made, 1)
            st.did(pool.memset(onesb[:], 1.0))
            st.wait()
            for a in (ident, identb):
                st.did(pool.affine_select(out=a[:], in_=a[:], compare_op=ALU.not_equal, fill=1.0, base=0,
                                          pattern=[[-1, P]], channel_multiplier=1))
            st.did(pool.affine_select(out=before[:], in_=before[:], compare_op=ALU.is_gt, fill=0.0, base=0,
                                      pattern=[[1, P]], channel_multiplier=-1))
            st.did(pool.affine_select(out=sgn[:], in_=sgn[:], compare_op=ALU.is_gt, fill=-1.0, base=64,
                                      pattern=[[0, 1]], channel_multiplier=-1))
            for hd, n in ((16, 8), (64, 2)):
                a = hmask[hd]
                st.wait()
                st.did(pool.affine_select(out=a[:], in_=a[:], compare_op=ALU.is_ge, fill=0.0, base=0,
                                          pattern=[[-hd, n]], channel_multiplier=1))
                st.wait()
                st.did(pool.affine_select(out=a[:], in_=a[:], compare_op=ALU.is_ge, fill=0.0, base=hd - 1,
                                          pattern=[[hd, n]], channel_multiplier=-1))
            for base in (0, -32):
                st.wait()
                st.did(pool.affine_select(out=sel[:], in_=sel[:], compare_op=ALU.not_equal, fill=1.0, base=base,
                                          pattern=[[-1, 16], [0, P]], channel_multiplier=1))
                a = selr[:, :, :, 0:MR]
                st.did(pool.affine_select(out=a, in_=a, compare_op=ALU.not_equal, fill=1.0, base=base,
                                          pattern=[[-4, 4], [-1, 4], [0, MR]], channel_multiplier=1))
            st.did(pool.iota(iota[:], [[1, 16]], base=0, channel_multiplier=0, allow_small_or_imprecise_dtypes=True))
            st.wait()
            pool.sem_inc(consts, NCONST)

            def norm(p, v):
                for c in range(NC):
                    ts = slice(TPC * c, TPC * (c + 1))
                    pool.wait_ge(ln_stats, lnorm(p, c))
                    st.did(pool.tensor_scalar(rstd[:, ts], mv[:, ts, 1], 1e-5, None, ALU.add))
                    st.wait()
                    st.did(pool.tensor_tensor(rstd[:, ts], rstd[:, ts], nhalf[:, ts], ALU.pow))
                    st.wait()
                    pool.sem_inc(ln_rstd, 1)

            def add_row(row, made, n, p):
                pool.wait_ge(ln_y, lnorm(p, NC - 1))
                pool.wait_ge(made, n)
                for c in range(NC):
                    a = X[:, TPC * c:TPC * (c + 1), :]
                    last = pool.tensor_tensor(a, a, bc(row.unsqueeze(1), (P, TPC, D)), ALU.add)
                last.then_inc(xbias, 1)

            def attention(p, L):
                v = ph[p]
                H, hd, MT, hpm, G = (v[k] for k in ("H", "hd", "MT", "hpm", "G"))
                st.did(pool.memset(v["V"][:], 1.0))
                st.did(pool.memset(v["Vr"][:], 0.0))
                st.did(pool.memset(v["Kr"][:], 0.0))
                if L == 3:
                    st.did(pool.memset(v["ss"][:], 1.0))
                    st.did(pool.memset(v["Kp"][:], 0.0))
                else:
                    st.did(pool.memset(v["negm"][0:65], 0.0))
                    if L == 0:
                        st.wait()
                        st.did(pool.memset(v["negm"][64:65], 1.0))
                for j in range(4):
                    st.wait()
                    st.did(pool.memset(v["Vr"][32 * j:32 * j + MR, :, :, j, hd:v["vw"]], 1.0))
                st.wait()
                pool.sem_inc(kv_clear, 1)
                if L == 3:
                    pool.sem_inc(kn_clear, 1)
                norm(p, v)
                if L == 3:
                    pool.wait_ge(kss_made, 1)
                    a = v["rs"][:, NT:NT + 4]
                    st.did(pool.tensor_scalar(a, v["ss"][:, NT:NT + 4], 1e-24, None, ALU.max))
                    st.wait()
                    st.did(pool.tensor_tensor(a, a, nhalf[:, 0:4], ALU.pow))
                    st.wait()
                    for i in range(4):
                        n = P if i % 2 == 0 else MR
                        st.did(pool.tensor_scalar(v["Kp"][0:n, i, :], v["Kp"][0:n, i, :], v["rs"][0:n, NT + i:NT + i + 1], None,
                                                  ALU.mult))
                    st.wait()
                    pool.sem_inc(kn_made, 1)
                base = sum(B * ph[2 * l]["MT"] for l in range(L))

                def last_keys():
                    for n in range(MT * B):
                        pool.wait_ge(kz_made, base + n + 1)
                        pool.tensor_copy(v["Kr"][:, n, :, 0:MR], v["Kz"][:, n, :, P:M]).then_inc(kr_made, 1)

                def queries(c):
                    ts = slice(TPC * c, TPC * (c + 1))
                    pool.wait_ge(qss_made, c + 1)
                    st.did(pool.tensor_scalar(v["rs"][:, ts], v["ss"][:, ts], 1e-24, None, ALU.max))
                    st.wait()
                    st.did(pool.tensor_tensor(v["rs"][:, ts], v["rs"][:, ts], nhalf[:, ts], ALU.pow))
                    st.wait()
                    for t in range(TPC * c, TPC * (c + 1)):
                        last = pool.tensor_scalar(v["Y"][:, t, :], v["Qp"][:, t, :], v["rs"][:, t:t + 1], None, ALU.mult)
                    last.then_inc(qn_made, 1)
                    pool.wait_ge(qn_made, c + 1)
                    a = v["Qp"][:, ts, :]
                    pool.tensor_tensor(a, a, bc(v["bo"][:].unsqueeze(1), (P, TPC, D)), ALU.add).then_inc(qbo_made, 1)

                def post(c):
                    ts = slice(TPC * c, TPC * (c + 1))
                    pool.wait_ge(post_stats, c + 1)
                    st.did(pool.tensor_scalar(rstd[:, ts], mv[:, ts, 1], 1e-5, None, ALU.add))
                    st.wait()
                    st.did(pool.tensor_tensor(rstd[:, ts], rstd[:, ts], nhalf[:, ts], ALU.pow))
                    st.wait()
                    for t in range(TPC * c, TPC * (c + 1)):
                        last = pool.tensor_scalar(v["Qp"][:, t, :], v["Qp"][:, t, :], mv[:, t, 0:1], rstd[:, t:t + 1],
                                                  ALU.subtract, ALU.mult)
                    last.then_inc(post_z, 1)

                if L != 3:
                    last_keys()
                if L in (1, 2):
                    add_row(v["gbo"][:], gbo_made, L, p)
                if L == 3:
                    queries(0)
                    last_keys()
                    queries(1)
                    add_row(v["gb"][:], gbo_made, L, p)
                    queries(2)
                    post(0)
                    queries(3)
                    for c in range(1, NC):
                        post(c)

            for p in range(NPH):
                L = p // 2
                v = ph[p]
                if p:
                    pool.wait_ge(phase_over, p)
                if p % 2 == 0:
                    attention(p, L)
                    continue
                norm(p, v)
                if L == 1:
                    for n in range(2):
                        pool.wait_ge(xmax_made, n + 1)
                        pool.partition_all_reduce(v["sc"][:, n:n + 1], v["m"][:, 60 + n:61 + n], P, RMAX).then_inc(xall_made, 1)
                    add_row(v["rowB"][:], rows_made, 1, p)
                if L == 3:
                    pool.iota(v["dump"][:], [[2 * P, NT], [1, 2]], base=E3 * CAP, channel_multiplier=2,
                              allow_small_or_imprecise_dtypes=True).then_inc(dumps_made, 1)
                    pool.wait_ge(idx_made, 1)
                    pool.wait_ge(slots_clear, 16)
                    pool.wait_ge(ln_y, lnorm(p, NC - 1))
                    for t in range(NT):
                        for k in range(2):
                            i = 2 * t + k
                            pool.indirect_dma_start(x_slots, bass.IndirectOffsetOnAxis(ap=v["sidx"][:, i:i + 1], axis=0),
                                                    v["Y"][:, t, :], None).then_inc(scattered, 16)
                    for i in range(3):
                        pool.wait_ge(ye_stored[i], 16 * 2 * len(range(i, E3, 3)))
                    pool.wait_ge(scattered, 16 * 2 * NT)
                    for t in range(NT):
                        for k in range(2):
                            i = 2 * t + k
                            dst = (v["Y"] if k == 0 else v["yk"])[:, t, :]
                            pool.indirect_dma_start(dst, None, y_slots,
                                                    bass.IndirectOffsetOnAxis(ap=v["gidx"][:, i:i + 1], axis=0))\
                                .then_inc(gathered[t // 2], 16)

        @block.vector
        def _(dve):
            st = Steps(dve, dve_st)
            dve.wait_ge(in_loaded, 16 * NIN)
            dve.wait_ge(tg_made, 1)
            dve.wait_ge(consts, NCONST)

            def x_norm(p):
                for c in range(NC + 1):
                    if c < NC:
                        for t in range(TPC * c, TPC * (c + 1)):
                            st.did(dve.bn_stats(stats[:, t, :], X[:, t, :]))
                        st.wait()
                        for t in range(TPC * c, TPC * (c + 1)):
                            last = dve.bn_aggr(mv[:, t, :], stats[:, t, :])
                        last.then_inc(ln_stats, 1)
                    if c:
                        dve.wait_ge(ln_rstd, lnorm(p, c - 1))
                        for t in range(TPC * (c - 1), TPC * c):
                            last = dve.tensor_scalar(ph[p]["Y"][:, t, :], X[:, t, :], mv[:, t, 0:1], rstd[:, t:t + 1],
                                                     ALU.subtract, ALU.mult)
                        last.then_inc(ln_y, 1)

            def add_out(p, bk, q, scalar, end):
                a = X[:, 2 * q:2 * q + 2, :]
                return dve.scalar_tensor_tensor(a, bk[:].rearrange("p (t d) -> p t d", t=2), scalar, a, ALU.mult, ALU.add)

            def over(p):
                dve.wait_ge(RB.read, RB.emptied)
                dve.sem_inc(phase_over, 1)

            def attention(p, L):
                v = ph[p]
                H, hd, MT, hpm, G, HD = (v[k] for k in ("H", "hd", "MT", "hpm", "G", "HD"))
                dve.wait_ge(w_loaded[p], 16 * len(loads[p]))
                if L == 0:
                    st.did(dve.tensor_copy(v["m01"][:], v["m8"][:]))
                    dve.tensor_scalar(v["mb"][64:65].rearrange("p b k -> p (b k)"), v["m8"][64:65], -1.0, BIG,
                                      ALU.add, ALU.mult).then_inc(mb_made, 1)
                if L in (1, 2):
                    dve.tensor_scalar(v["gbo"][:], v["bo"][:], tg[:, L:L + 1], None, ALU.mult).then_inc(gbo_made, 1)
                if L == 3:
                    st.did(dve.tensor_scalar(v["lg"][:], v["lg"][:], tg[:, L:L + 1], None, ALU.mult))
                    dve.tensor_scalar(v["gb"][:], v["lb"][:], tg[:, L:L + 1], None, ALU.mult).then_inc(gbo_made, 1)
                x_norm(p)
                dve.wait_ge(kv_clear, L + 1)

                def keys():
                    for m in range(MT):
                        bk = RB.get(dve, p, "k", m)
                        if L == 2:
                            ins = dve.tensor_scalar(v["KTs"][:, m, :], bk[:, 0:B * M], v["bk"][:, m:m + 1], None, ALU.add)
                        elif L == 0:
                            ins = dve.tensor_tensor(v["KTs"][:, m, :], bk[:, 0:B * M], v["m01"][:], ALU.mult)
                        else:
                            ins = dve.tensor_copy(v["KTs"][:, m, :], bk[:, 0:B * M])
                        ins.then_inc(RB.read, 1)
                        dve.wait_ge(RB.read, RB.emptied)
                        for b in range(B):
                            dve.tensor_tensor(v["Kz"][:, m * B + b, :, :],
                                              bc(v["KTs"][:, m, b * M:(b + 1) * M].unsqueeze(1), (P, hpm, M)),
                                              bc(hmask[hd][:].unsqueeze(2), (P, hpm, M)), ALU.mult).then_inc(kz_made, 1)

                def values():
                    for b in range(B):
                        bk = RB.get(dve, p, "v", b, 0)
                        a = bk[:, 0:HD].rearrange("p (h d) -> p h d", d=hd)
                        o = v["V"][:, b, :, 0:hd]
                        if L >= 2:
                            ins = dve.tensor_tensor(o, a, v["bv"][:].rearrange("p (h d) -> p h d", d=hd), ALU.add)
                        else:
                            ins = dve.tensor_copy(o, a)
                        st.did(ins)
                        st.wait()
                        dve.sem_inc(RB.read, 1)
                        dve.sem_inc(v_made, 1)
                        bk = RB.get(dve, p, "v", b, 1)
                        a = bk[0:MR, 0:HD].rearrange("p (g j d) -> p g j d", j=4, d=hd)
                        for j in range(4):
                            o = v["Vr"][32 * j:32 * j + MR, b, :, j, 0:hd]
                            if L >= 2:
                                bv = v["bv"][0:MR].rearrange("p (g j d) -> p g j d", j=4, d=hd)[:, :, j, :]
                                ins = dve.tensor_tensor(o, a[:, :, j, :], bv, ALU.add)
                            else:
                                ins = dve.tensor_copy(o, a[:, :, j, :])
                            st.did(ins)
                        st.wait()
                        dve.sem_inc(RB.read, 1)
                        dve.sem_inc(v_made, 1)

                if L < 3:
                    keys()
                    if L == 0:
                        for b in range(B):
                            st.did(dve.tensor_copy(v["sel"][0:65, b * H:(b + 1) * H, :], sel[:]))
                            st.did(dve.tensor_copy(v["selr"][0:65, b * 4:(b + 1) * 4, :, :], selr[:]))
                        st.wait()
                        dve.wait_ge(mb_made, 1)
                        for b in range(B):
                            st.did(dve.tensor_copy(v["sel"][64:65, b * H:(b + 1) * H, :],
                                                   bc(v["mb"][64:65, b, 0:P].unsqueeze(1), (1, H, P))))
                            st.did(dve.tensor_copy(v["selr"][64:65, b * 4:(b + 1) * 4, :, 0:MR]
                                                   .rearrange("p g j k -> p (g j) k"),
                                                   bc(v["mb"][64:65, b, P:M].unsqueeze(1), (1, 16, MR))))
                        st.wait()
                        dve.sem_inc(sel0_made, 1)
                values()
                if L == 3:
                    for b in range(B):
                        for s in range(2):
                            n = P if s == 0 else MR
                            bk = RB.get(dve, p, "kp", b, s)
                            dve.tensor_tensor(v["Kp"][0:n, 2 * b + s, :], bk[0:n, 0:HD], v["bk"][0:n], ALU.add)\
                               .then_inc(RB.read, 1)
                    keys()
                for what, c in ATT:
                    if what == "front":
                        if L == 3:
                            for q in range(2):
                                bk = RB.get(dve, p, "qp", c, q)
                                t = (2 * c + q) * 2
                                dve.tensor_tensor(v["Qp"][:, t:t + 2, :], bk[:].rearrange("p (t d) -> p t d", t=2),
                                                  bc(v["bq"][:].unsqueeze(1), (P, 2, D)), ALU.add).then_inc(RB.read, 1)
                            continue
                        for i in range(TPC):
                            for m in range(MT):
                                for h0 in range(0, hpm, 3):
                                    hn = min(3, hpm - h0)
                                    bk = RB.get(dve, p, "mxs", c, i, m, h0)
                                    hh = m * hpm + h0
                                    dve.tensor_reduce(v["mx"][:, TPC * c + i, hh:hh + hn],
                                                      bk[:, 0:hn * M].rearrange("p (h k) -> p h k", k=M), AX.X, ALU.max)\
                                       .then_inc(RB.read, 1)
                    elif what == "back":
                        if L < 3:
                            bk = RB.get(dve, p, "mx", c)
                            st.did(dve.tensor_scalar(v["negm"][0:H, c, :], bk[0:H, :], -1.0, None, ALU.mult))
                            st.wait()
                            dve.scalar_tensor_tensor(v["negm"][32:32 + H, c, :], bk[0:H, :], -1.0, v["negm"][0:H, c, :],
                                                     ALU.mult, ALU.subtract).then_inc(RB.read, 1)
                        for g in range(G):
                            if hd == 16:
                                bk = RB.get(dve, p, "av", c, g)
                                r = v["rden"][:, g % 2, :]
                                st.did(dve.stream_shuffle(r, bk[:], [16 + i % 16 for i in range(32)]))
                                st.wait()
                                st.did(dve.reciprocal(r, r))
                                st.wait()
                                dve.tensor_tensor(v["OT"][:, g, :], bk[:], r, ALU.mult).then_inc(RB.read, 1)
                                continue
                            for i in range(TPC):
                                bk = RB.get(dve, p, "av", c, g, i)
                                a = bk[:, 0:4 * (hd + 1)].rearrange("p (j d) -> p j d", j=4)
                                r = v["rden"][:, i % 2, 0:4]
                                st.did(dve.reciprocal(r, a[:, :, hd]))
                                st.wait()
                                o = v["O"][:, c % 2, i, g * 4 * hd:(g + 1) * 4 * hd].rearrange("p (j d) -> p j d", j=4)
                                dve.tensor_tensor(o, a[:, :, 0:hd], bc(r.unsqueeze(2), (P, 4, hd)), ALU.mult)\
                                   .then_inc(RB.read, 1)
                    else:
                        if L in (1, 2):
                            dve.wait_ge(xbias, XB[p])
                        if L < 3:
                            for q in range(2):
                                bk = RB.get(dve, p, "out", c, q)
                                add_out(p, bk, 2 * c + q, tg[:, L:L + 1], False).then_inc(RB.read, 1)
                            continue
                        dve.wait_ge(qbo_made, c + 1)
                        for q in range(2):
                            bk = RB.get(dve, p, "out", c, q)
                            a = v["Qp"][:, (2 * c + q) * 2:(2 * c + q) * 2 + 2, :]
                            dve.tensor_tensor(a, bk[:].rearrange("p (t d) -> p t d", t=2), a, ALU.add).then_inc(RB.read, 1)
                        dve.wait_ge(RB.read, RB.emptied)
                        for t in range(TPC * c, TPC * (c + 1)):
                            st.did(dve.bn_stats(stats[:, t, :], v["Qp"][:, t, :]))
                        st.wait()
                        for t in range(TPC * c, TPC * (c + 1)):
                            last = dve.bn_aggr(mv[:, t, :], stats[:, t, :])
                        last.then_inc(post_stats, 1)
                        dve.wait_ge(post_z, c + 1)
                        dve.wait_ge(xbias, XB[p])
                        z = v["Qp"][:, TPC * c:TPC * (c + 1), :]
                        xx = X[:, TPC * c:TPC * (c + 1), :]
                        st.did(dve.tensor_tensor(z, z, bc(v["lg"][:].unsqueeze(1), (P, TPC, D)), ALU.mult))
                        st.wait()
                        st.did(dve.tensor_tensor(xx, xx, z, ALU.add))
                if L == 3:
                    st.wait()
                over(p)

            def coupling(p):
                v = ph[p]
                x_norm(p)
                dve.wait_ge(w_loaded[p], 16 * len(loads[p]))
                st.did(dve.memset(v["w4r"][64:P], 0.0))
                st.did(dve.memset(v["h3"][64:P], 0.0))
                st.did(dve.tensor_copy(v["w4r"][0:64], bc(v["w4"][0:64], (64, P))))
                st.did(dve.tensor_copy(v["g3r"][0:64], bc(v["g3"][0:64], (64, P))))
                st.did(dve.tensor_scalar(v["hb"][:, 0:1], v["b4"][:], 0.5, None, ALU.mult))
                st.did(dve.tensor_scalar(v["hb"][:, 1:2], v["gb3"][:], 0.5, None, ALU.mult))
                for c in range(NC):
                    for d in range(DK):
                        dve.wait_ge(RA.read, RA.n(p, "yT", c, d))
                        st.did(dve.tensor_reduce(v["msum"][:, d, c:c + 1], v["yT"][:, d, c * CH:(c + 1) * CH], AX.X, ALU.add))
                st.wait()
                for b in range(B):
                    st.did(dve.tensor_tensor(v["mean"][:, :, b], v["msum"][:, :, CPB * b], v["msum"][:, :, CPB * b + 1], ALU.add))
                st.wait()
                a = v["mean"][:].rearrange("p k b -> p (k b)")
                dve.tensor_scalar(a, a, 1.0 / S, None, ALU.mult).then_inc(gc_ready, 1)
                dve.wait_ge(RA.read, RA.n(p, "g3"))
                st.did(dve.tensor_scalar(v["al"][:], v["ar"][:], 0.3, sgn[:, 0:1], ALU.mult, ALU.mult))
                st.did(dve.tensor_scalar(v["be"][:], v["gt"][:], v["ar"][:, 0:1], 0.7, ALU.mult, ALU.mult))
                st.wait()
                st.did(dve.tensor_scalar(v["be"][:], v["be"][:], 0.1, sgn[:, 0:1], ALU.add, ALU.mult))
                st.wait()
                s2 = [v["yT"], v["yS"]]
                for r in range(3):
                    old, new = s2[r % 2], s2[(r + 1) % 2]
                    for c in range(NC):
                        cs = slice(c * CH, (c + 1) * CH)
                        b = c // CPB
                        dve.wait_ge(RC.read, RC.n(p, r, "l4", c))
                        k, w = v["tmp"][:, 0, :], v["tmp"][:, 1, :]
                        st.did(dve.tensor_scalar(k, v["th"][:, c, :], v["al"][:, 0:1], v["be"][:, b:b + 1], ALU.mult, ALU.add))
                        st.wait()
                        st.did(dve.tensor_tensor(w, k, old[:, 1, cs], ALU.mult))
                        st.wait()
                        st.did(dve.tensor_tensor(new[:, 0, cs], w, old[:, 0, cs], ALU.add))
                        st.wait()
                        st.did(dve.tensor_tensor(w, k, old[:, 0, cs], ALU.mult))
                        st.wait()
                        dve.tensor_tensor(new[:, 1, cs], old[:, 1, cs], w, ALU.subtract).then_inc(state_made, 1)
                        dve.wait_ge(state_made, NC * r + c + 1)
                for c in range(NC):
                    for q in range(2):
                        bk = RB.get(dve, p, "fin", c, q)
                        add_out(p, bk, 2 * c + q, tg[:, 4:5], False).then_inc(RB.read, 1)
                over(p)

            def quantised(p):
                v = ph[p]
                x_norm(p)
                dve.wait_ge(w_loaded[p], 16 * len(loads[p]))
                for w, n, sw, iw, wi in (("w1", FT1, "sw1", "iw1", "wi1"), ("w2", DK, "sw2", "iw2", "wi2")):
                    st.did(dve.tensor_reduce(v[sw][:], v[w][:], AX.X, ALU.max, apply_absolute_value=True))
                    st.wait()
                    st.did(dve.tensor_scalar(v[sw][:], v[sw][:], 1e-8, 1.0 / 127.0, ALU.max, ALU.mult))
                    st.wait()
                    st.did(dve.reciprocal(v[iw][:], v[sw][:]))
                    st.wait()
                    for i in range(n):
                        st.did(dve.tensor_scalar(v[w][:, i, :], v[w][:, i, :], v[iw][:, i:i + 1], 127.0, ALU.mult, ALU.min))
                    st.wait()
                    st.did(dve.tensor_scalar(v[w][:], v[w][:], -128.0, ROUND, ALU.max, ALU.add))
                    st.wait()
                    st.did(dve.tensor_scalar(v[wi][:], v[w][:], ROUND, None, ALU.subtract))
                st.wait()
                dve.sem_inc(wq_made, 1)
                for d in range(DK):
                    last = st.did(dve.tensor_scalar(v["diag"][:, d, :], ident[:], v["sw2"][:, d:d + 1], None, ALU.mult))
                st.wait()
                dve.sem_inc(diag_made, 1)
                bk = RB.get(dve, p, "sw2r")
                dve.tensor_copy(v["sw2r"][:], bk[:, 0:D]).then_inc(RB.read, 1)

                def scale(n):
                    st.wait()
                    dve.sem_inc(xmax_made, 1)
                    dve.wait_ge(xall_made, n + 1)
                    st.did(dve.tensor_scalar(v["sc"][:, 4 + n:5 + n], v["sc"][:, n:n + 1], 1e-8, 1.0 / 255.0, ALU.max, ALU.mult))
                    st.wait()
                    st.did(dve.reciprocal(v["sc"][:, 6 + n:7 + n], v["sc"][:, 4 + n:5 + n]))
                    st.wait()

                for c in range(NC):
                    dve.wait_ge(ln_y, lnorm(p, c))
                    st.did(dve.tensor_reduce(v["m"][:, c:c + 1], v["Y"][:, TPC * c:TPC * (c + 1), :], AX.XY, ALU.max))
                st.wait()
                st.did(dve.tensor_reduce(v["m"][:, 60:61], v["m"][:, 0:NC], AX.X, ALU.max))
                scale(0)
                for c in range(NC):
                    a = v["Y"][:, TPC * c:TPC * (c + 1), :]
                    st.did(dve.tensor_scalar(a, a, v["sc"][:, 6:7], 255.0, ALU.mult, ALU.min))
                    st.wait()
                    st.did(dve.tensor_scalar(a, a, 0.0, ROUND, ALU.max, ALU.add))
                    st.wait()
                    dve.tensor_scalar(v["xi"][:, TPC * c:TPC * (c + 1), :], a, ROUND, None, ALU.subtract).then_inc(xi_made, 1)
                st.did(dve.tensor_scalar(v["sb1"][:], v["sw1"][:], v["sc"][:, 4:5], None, ALU.mult))
                st.wait()
                st.did(dve.reciprocal(v["ib1"][:], v["sb1"][:]))
                st.wait()
                st.did(dve.tensor_tensor(v["bq1"][:], v["b1"][:], v["ib1"][:], ALU.mult))
                st.wait()
                st.did(dve.tensor_scalar(v["bq1"][:], v["bq1"][:], ROUND, ROUND, ALU.add, ALU.subtract))
                st.wait()
                dve.tensor_tensor(v["bq1"][:], v["bq1"][:], v["sb1"][:], ALU.mult).then_inc(hscale_made, 1)
                for c in range(NC):
                    for f in range(FT1):
                        dve.wait_ge(RC.read, RC.n(p, "up", c, f))
                        n = 8 + c * FT1 + f
                        st.did(dve.tensor_reduce(v["m"][:, n:n + 1], v["h"][:, f, c * CH:(c + 1) * CH], AX.X, ALU.max))
                st.wait()
                st.did(dve.tensor_reduce(v["m"][:, 61:62], v["m"][:, 8:8 + NC * FT1], AX.X, ALU.max))
                scale(1)
                for c in range(NC):
                    a = v["h"][:, :, c * CH:(c + 1) * CH]
                    st.did(dve.tensor_scalar(a, a, v["sc"][:, 7:8], ROUND, ALU.mult, ALU.add))
                    st.wait()
                    dve.tensor_scalar(v["hi"][:, :, c * CH:(c + 1) * CH], a, ROUND, 255.0, ALU.subtract, ALU.min)\
                       .then_inc(hi_made, 1)
                    if c == 0:
                        dve.wait_ge(RB.read, RB.n(p, "sw2r"))
                        st.did(dve.tensor_scalar(v["rowS"][:], v["sw2r"][:], v["sc"][:, 5:6], None, ALU.mult))
                        st.wait()
                        st.did(dve.reciprocal(v["rowI"][:], v["rowS"][:]))
                        st.wait()
                        st.did(dve.tensor_tensor(v["rowB"][:], v["b2"][:], v["rowI"][:], ALU.mult))
                        st.wait()
                        st.did(dve.tensor_scalar(v["rowB"][:], v["rowB"][:], ROUND, ROUND, ALU.add, ALU.subtract))
                        st.wait()
                        st.did(dve.tensor_tensor(v["rowB"][:], v["rowB"][:], v["rowS"][:], ALU.mult))
                        st.wait()
                        st.did(dve.tensor_scalar(v["rowB"][:], v["rowB"][:], tg[:, 5:6], None, ALU.mult))
                        st.did(dve.tensor_scalar(v["rowT"][:], v["rowS"][:], tg[:, 5:6], None, ALU.mult))
                        st.wait()
                        dve.sem_inc(rows_made, 1)
                dve.wait_ge(xbias, XB[p])
                for c in range(NC):
                    for q in range(2):
                        bk = RB.get(dve, p, "dn", c, q)
                        o = v["dn"][:, q, :, :]
                        dve.tensor_tensor(o, bk[:].rearrange("p (t d) -> p t d", t=2),
                                          bc(v["rowT"][:].unsqueeze(1), (P, 2, D)), ALU.mult).then_inc(RB.read, 1)
                        dve.wait_ge(RB.read, RB.emptied)
                        a = X[:, (2 * c + q) * 2:(2 * c + q) * 2 + 2, :]
                        st.did(dve.tensor_tensor(a, a, o, ALU.add))
                st.wait()
                over(p)

            def experts(p, L):
                v = ph[p]
                E = E2 if L == 2 else E3
                r = v["r"]
                gate = tg[:, 4 + L:5 + L]
                x_norm(p)
                dve.wait_ge(w_loaded[p], 16 * len(loads[p]))
                for c in range(NC):
                    bk = RB.get(dve, p, "lg", c)
                    dve.tensor_tensor(v["lg"][:, TPC * c:TPC * (c + 1), :],
                                      bk[:, 0:TPC * E].rearrange("p (t e) -> p t e", e=E),
                                      bc(v["br"][:].unsqueeze(1), (P, TPC, E)), ALU.add).then_inc(RB.read, 1)
                dve.wait_ge(RB.read, RB.emptied)
                if L == 3:
                    st.did(dve.tensor_reduce(r[:, 0, :], v["lg"][:], AX.X, ALU.max))
                    st.wait()
                    st.did(dve.tensor_tensor(v["lg"][:], v["lg"][:], bc(r[:, 0, :].unsqueeze(2), (P, NT, E)), ALU.subtract))
                    st.wait()
                    dve.sem_inc(ex_ready, 1)
                    dve.wait_ge(ex_made, 2)
                    st.did(dve.tensor_reduce(r[:, 0, :], v["pre"][:], AX.X, ALU.add))
                    st.wait()
                    st.did(dve.reciprocal(r[:, 1, :], r[:, 0, :]))
                    st.wait()
                    st.did(dve.tensor_tensor(v["lg"][:], v["pre"][:], bc(r[:, 1, :].unsqueeze(2), (P, NT, E)), ALU.mult))
                    st.wait()
                for t in range(NT):
                    st.did(dve.max(v["top"][:, t, :], v["lg"][:, t, :]))
                st.wait()
                for t in range(NT):
                    st.did(dve.max_index(v["idx"][:, t, :], v["top"][:, t, :], v["lg"][:, t, :]))
                st.wait()
                st.did(dve.tensor_copy(v["idf"][:], v["idx"][:]))
                st.wait()
                io = bc(iota[:, 0:E].unsqueeze(1), (P, NT, E))
                st.did(dve.tensor_tensor(v["oh"][:], io, bc(v["idf"][:, :, 0:1], (P, NT, E)), ALU.is_equal))
                st.did(dve.tensor_tensor(v["oh2"][:], io, bc(v["idf"][:, :, 1:2], (P, NT, E)), ALU.is_equal))
                if L == 2:
                    st.did(dve.tensor_tensor(r[:, 0, :], v["top"][:, :, 1], v["top"][:, :, 0], ALU.subtract))
                    st.wait()
                    dve.sem_inc(ex_ready, 1)
                    dve.wait_ge(ex_made, 1)
                    st.did(dve.tensor_scalar(r[:, 2, :], r[:, 1, :], 1.0, None, ALU.add))
                    st.wait()
                    st.did(dve.reciprocal(r[:, 3, :], r[:, 2, :]))
                    st.wait()
                    st.did(dve.tensor_tensor(r[:, 4, :], r[:, 1, :], r[:, 3, :], ALU.mult))
                    g0, g1 = r[:, 3, :], r[:, 4, :]
                else:
                    st.wait()
                    st.did(dve.tensor_tensor(v["ohb"][:], v["oh"][:], v["oh2"][:], ALU.add))
                    st.did(dve.memset(v["ohs"][:, 0, :], 0.0))
                    for t in range(1, NT):
                        st.wait()
                        st.did(dve.tensor_tensor(v["ohs"][:, t, :], v["ohs"][:, t - 1, :], v["ohb"][:, t - 1, :], ALU.add))
                    st.wait()
                    dve.sem_inc(oh_made, 1)
                    st.did(dve.tensor_tensor(r[:, 2, :], v["top"][:, :, 0], v["top"][:, :, 1], ALU.add))
                    st.wait()
                    st.did(dve.tensor_scalar(r[:, 3, :], r[:, 2, :], 1e-9, None, ALU.add))
                    st.wait()
                    st.did(dve.reciprocal(r[:, 4, :], r[:, 3, :]))
                    st.wait()
                    st.did(dve.tensor_tensor(r[:, 5, :], v["top"][:, :, 0], r[:, 4, :], ALU.mult))
                    st.did(dve.tensor_tensor(r[:, 6, :], v["top"][:, :, 1], r[:, 4, :], ALU.mult))
                    g0, g1 = r[:, 5, :], r[:, 6, :]
                st.wait()
                if L == 3:
                    routed(p, v, gate, g0, g1)
                    return
                st.did(dve.tensor_tensor(v["oh"][:], v["oh"][:], bc(g0.unsqueeze(2), (P, NT, E)), ALU.mult))
                st.did(dve.tensor_tensor(v["oh2"][:], v["oh2"][:], bc(g1.unsqueeze(2), (P, NT, E)), ALU.mult))
                st.wait()
                st.did(dve.tensor_tensor(v["G"][:], v["oh"][:], v["oh2"][:], ALU.add))
                st.wait()
                st.did(dve.tensor_scalar(v["G"][:], v["G"][:], gate, None, ALU.mult))
                st.wait()
                dve.sem_inc(g_made, 1)
                dve.wait_ge(ln_y, lnorm(p, NC - 1))
                for c in range(NC):
                    for q in range(2):
                        bk = RB.get(dve, p, "b2", c, q)
                        a = X[:, (2 * c + q) * 2:(2 * c + q) * 2 + 2, :]
                        dve.tensor_tensor(a, a, bk[:].rearrange("p (t d) -> p t d", t=2), ALU.add).then_inc(RB.read, 1)
                dve.wait_ge(RB.read, RB.emptied)
                for what, e, c in expert_order(E):
                    if what == "down":
                        expert_out(p, e, c, lambda t: v["G"][:, t, e:e + 1])
                over(p)

            def expert_out(p, e, c, gate_of):
                for q in range(2):
                    bk = RB.get(dve, p, "dn", e, c, q)
                    for i in range(2):
                        t = (2 * c + q) * 2 + i
                        ins = dve.scalar_tensor_tensor(X[:, t, :], bk[:, i * D:(i + 1) * D], gate_of(t), X[:, t, :],
                                                       ALU.mult, ALU.add)
                    ins.then_inc(RB.read, 1)

            def routed(p, v, gate, g0, g1):
                bk = RB.get(dve, p, "pos")
                st.did(dve.tensor_copy(v["pre"][:], bk[:, 0:NT * E3].rearrange("p (t e) -> p t e", e=E3)))
                st.wait()
                dve.sem_inc(RB.read, 1)
                for k, (oh, g) in enumerate((("oh", g0), ("oh2", g1))):
                    st.did(dve.tensor_tensor(v[oh][:], v[oh][:], v["pre"][:], ALU.mult))
                    st.wait()
                    st.did(dve.tensor_reduce(v["pk"][:, :, k], v[oh][:], AX.X, ALU.add))
                    st.wait()
                    st.did(dve.tensor_scalar(v["wk"][:, :, k], v["pk"][:, :, k], float(CAP), gate, ALU.is_lt, ALU.mult))
                    st.wait()
                    st.did(dve.tensor_tensor(v["wk"][:, :, k], v["wk"][:, :, k], g, ALU.mult))
                st.did(dve.tensor_scalar(v["slot"][:], v["pk"][:], float(CAP), None, ALU.is_lt))
                st.did(dve.tensor_scalar(v["row"][:], v["pk"][:], float(CAP - 1), None, ALU.min))
                st.wait()
                st.did(dve.scalar_tensor_tensor(v["row"][:], v["idf"][:, :, 0:2], float(CAP), v["row"][:], ALU.mult, ALU.add))
                st.wait()
                dve.wait_ge(dumps_made, 1)
                st.did(dve.tensor_tensor(v["pk"][:], v["row"][:], v["dump"][:], ALU.subtract))
                st.wait()
                st.did(dve.tensor_tensor(v["pk"][:], v["pk"][:], v["slot"][:], ALU.mult))
                st.wait()
                st.did(dve.tensor_tensor(v["pk"][:], v["pk"][:], v["dump"][:], ALU.add))
                st.wait()
                st.did(dve.tensor_copy(v["sidx"][:], v["pk"][:].rearrange("p t k -> p (t k)")))
                st.did(dve.tensor_copy(v["gidx"][:], v["row"][:].rearrange("p t k -> p (t k)")))
                st.wait()
                dve.sem_inc(idx_made, 1)
                dve.wait_ge(ln_y, lnorm(p, NC - 1))
                st.did(dve.scalar_tensor_tensor(X[:], v["Y"][:], gate, X[:], ALU.mult, ALU.add))
                st.wait()
                n = 0

                def product(e, c, slot, width):
                    nonlocal n
                    for m in range(3):
                        fn = F3T[m]
                        dve.wait_ge(RA.read, RA.n(p, "gate", e, c, m))
                        bk = RB.get(dve, p, "up", e, c, m)
                        dve.tensor_tensor(v["hT"][0:fn, slot * 3 + m, 0:width], v["sg"][0:fn, n % 4, 0:width],
                                          bk[0:fn, 0:width], ALU.mult).then_inc(RB.read, 1)
                        n += 1

                for what, e, c in expert_order(1):
                    if what == "up":
                        product(E3, c, c % 2, CH)
                    else:
                        expert_out(p, E3, c, lambda t: gate)
                for e in range(E3):
                    if e >= 2:
                        dve.wait_ge(RC.filled, RC.n(p, "dn", e - 2, 1))
                    product(e, 0, e % 2, CAP)
                dve.wait_ge(RB.read, RB.emptied)
                for t in range(NT):
                    if t % 2 == 0:
                        dve.wait_ge(gathered[t // 2], 16 * 4)
                    for k in range(2):
                        src = (v["Y"] if k == 0 else v["yk"])[:, t, :]
                        st.did(dve.scalar_tensor_tensor(X[:, t, :], src, v["wk"][:, t, k:k + 1], X[:, t, :], ALU.mult, ALU.add))
                        st.wait()
                    if t % TPC == TPC - 1:
                        dve.sem_inc(x_out, 1)

            for p in range(NPH):
                L = p // 2
                if p:
                    dve.wait_ge(phase_over, p)
                if p % 2 == 0:
                    attention(p, L)
                elif L == 0:
                    coupling(p)
                elif L == 1:
                    quantised(p)
                else:
                    experts(p, L)

        @block.sync
        def _(sp):
            def load(p):
                if p >= 2:
                    sp.wait_ge(phase_over, p - 1)
                for i, (dst, src) in enumerate(loads[p]):
                    if p == 0 and i == len(loads[p]) - 4:
                        sp.wait_ge(zero_made, 1)
                    sp.dma_start(dst, src, allow_slow_non_contiguous=True).then_inc(w_loaded[p], 16)

            x_v = A["x"].rearrange("b (t p) d -> p (b t) d", p=P)
            sp.dma_start(X[:], x_v).then_inc(in_loaded, 16)
            for b in range(B):
                sp.dma_start(ctxN[:, b, :], A["ctx_768"][b, 0:P, :]).then_inc(in_loaded, 16)
                sp.dma_start(ctxN[0:MR, B + b, :], A["ctx_768"][b, P:M, :]).then_inc(in_loaded, 16)
            sp.dma_start(gates[:, 0:4], row(A["g_xattn"], 4)).then_inc(in_loaded, 16)
            sp.dma_start(gates[:, 4:8], row(A["g_ffn"], 4)).then_inc(in_loaded, 16)
            load(0)
            if NPH == 8:
                sp.wait_ge(zero_made, 1)
                sp.dma_start(x_slots[0:E3 * CAP, :].rearrange("(p n) d -> p n d", p=P),
                             bc(zeros[:].unsqueeze(1), (P, E3 * CAP // P, D))).then_inc(slots_clear, 16)
            for p in range(1, NPH):
                load(p)
                L = p // 2
                if p % 2 == 0 or L < 2:
                    continue
                v = ph[p]
                sp.wait_ge(phase_over, p)
                pre = f"L{L}_ffn_"
                if L == 2:
                    for e in range(E2):
                        s = e % 3
                        if e >= 3:
                            sp.wait_ge(RB.filled, RB.n(p, "dn", e - 3, NC - 1, 1))
                        sp.dma_start(v["W1"][:, s], kin(A[pre + "W1"][e])).then_inc(ew_loaded[L][s], 16)
                        sp.dma_start(v["W2"][:, s], A[pre + "W2"][e].rearrange("(m p) n -> p m n", p=P))\
                          .then_inc(ew_loaded[L][s], 16)
                    continue

                def expert_weights(i):
                    s, e = i % 3, i - 1
                    if i == 3:
                        sp.wait_ge(RB.filled, RB.n(p, "dn", E3, NC - 1, 1))
                    elif i > 3:
                        sp.wait_ge(RC.filled, RC.n(p, "dn", e - 3, 1))
                    g, u, d = (A[pre + n][e] if i else A[pre + "s" + n] for n in ("w_gate", "w_up", "w_down"))
                    for dst, src in ((v["Wg"][:, s], kin(g)), (v["Wu"][:, s], kin(u)),
                                     (v["Wd"][:, s, 0:2], d[0:2 * P, :].rearrange("(m p) n -> p m n", p=P)),
                                     (v["Wd"][0:F3 - 2 * P, s, 2], d[2 * P:F3, :])):
                        sp.dma_start(dst, src).then_inc(ew_loaded[L][s], 16)

                def expert_tokens(e):
                    if e >= 3:
                        sp.wait_ge(RA.filled, RA.n(p, "xeT", e - 3, DK - 1))
                    x = x_slots[e * CAP:(e + 1) * CAP, :]
                    sp.dma_start(v["xe"][:, e % 3, 0:2, :], x[0:2 * P, :].rearrange("(t p) d -> p t d", p=P))\
                      .then_inc(xe_loaded[e % 3], 16)
                    sp.dma_start(v["xe"][0:CAP - 2 * P, e % 3, 2, :], x[2 * P:CAP, :]).then_inc(xe_loaded[e % 3], 16)

                for i in range(3):
                    expert_weights(i)
                sp.wait_ge(scattered, 16 * 2 * NT)
                for e in range(3):
                    expert_tokens(e)
                for e in range(E3):
                    if e + 3 <= E3:
                        expert_weights(e + 3)
                    sp.wait_ge(RC.read, RC.n(p, "dn", e, 1))
                    y = y_slots[e * CAP:(e + 1) * CAP, :]
                    sp.dma_start(y[0:2 * P, :].rearrange("(t p) d -> p t d", p=P), v["ye"][:, e % 3, 0:2, :])\
                      .then_inc(ye_stored[e % 3], 16)
                    sp.dma_start(y[2 * P:CAP, :], v["ye"][0:CAP - 2 * P, e % 3, 2, :]).then_inc(ye_stored[e % 3], 16)
                    if e + 3 < E3:
                        expert_tokens(e + 3)
            o = out.rearrange("b (t p) d -> p (b t) d", p=P)
            for c in range(NC):
                ts = slice(TPC * c, TPC * (c + 1))
                if NPH < 8:
                    sp.wait_ge(phase_over, NPH)
                else:
                    sp.wait_ge(x_out, c + 1)
                sp.dma_start(o[:, ts, :], X[:, ts, :]).then_inc(stored, 16)
            sp.wait_ge(stored, 16 * NC)


def kernel(**inputs):
    import numpy as np
    import concourse.bacc as bacc
    from concourse.bass_utils import run_bass_kernel_spmd

    nc = bacc.Bacc("TRN2", target_bir_lowering=False, num_devices=1)
    arrays, aps = {}, {}
    for name, value in inputs.items():
        a = np.ascontiguousarray(value)
        arrays[f"in_{name}"] = a
        aps[name] = nc.dram_tensor(f"in_{name}", a.shape, mybir.dt.from_np(a.dtype), kind="ExternalInput").ap()
    out = nc.dram_tensor("out_x", (B, S, D), F32, kind="ExternalOutput").ap()
    build(nc, aps, out)
    r = run_bass_kernel_spmd(nc, [arrays], core_ids=[0])
    return r.results[0]["out_x"]
```

```python
import concourse.bass as bass
from concourse import mybir
from contextlib import ExitStack

F32 = mybir.dt.float32
BF16 = mybir.dt.bfloat16
U32 = mybir.dt.uint32
U8 = mybir.dt.uint8
ALU = mybir.AluOpType
ACT = mybir.ActivationFunctionType
AX = mybir.AxisListType
RMAX = bass.bass_isa.ReduceOp.max

P = 128
B, S, D = 2, 1024, 256
T = B * S
NT = T // P
CH = 512
NC = T // CH
TPC = CH // P
CPB = NC // B
DK = D // P
M, CD = 154, 192
MR = M - P
MP = P + 32
Q_PART = (0, 0, 0, 1, 1, 2)
K_PART = (0, 1, 2, 0, 1, 0)
BIG = float(2.0 ** 100)
ROUND = 12582912.0
PHASES = 8

HEADS = {0: (16, 16), 1: (8, 64), 2: (16, 16), 3: (16, 16)}
E2, H2 = 8, 512
NTL = (2 * T + E2 * (P - 1)) // P
E3, F3 = 16, 352
CAP = 320
F3T = [128, 128, 96]
F1 = 1024
FT1 = F1 // P


class Ring:

    def __init__(self, banks, filled, read):
        self.banks, self.filled, self.read, self.order, self.emptied = banks, filled, read, {}, 0

    def take(self, pe, *key):
        i = len(self.order)
        assert key not in self.order, key
        self.order[key] = i
        if i >= len(self.banks):
            pe.wait_ge(self.read, i - len(self.banks) + 1)
        return self.banks[i % len(self.banks)]

    def n(self, *key):
        return self.order[key] + 1

    def get(self, eng, *key):
        assert self.order[key] == self.emptied, (key, self.order[key], self.emptied)
        self.emptied += 1
        eng.wait_ge(self.filled, self.order[key] + 1)
        return self.banks[self.order[key] % len(self.banks)]


class Steps:

    def __init__(self, eng, sem):
        self.eng, self.sem, self.count = eng, sem, 0

    def did(self, ins):
        self.count += 1
        ins.then_inc(self.sem, 1)
        return self.count

    def wait(self, count=None):
        self.eng.wait_ge(self.sem, self.count if count is None else count)


class Arena:
    def __init__(self, tensor, words):
        self.t, self.words, self.at = tensor, words, 0

    def reset(self):
        self.at = 0

    def take(self, shape, dt=F32):
        n = 1
        for s in shape:
            n *= s
        words = n if dt in (F32, U32) else (n + 1) // 2 if dt == BF16 else (n + 3) // 4
        ap = self.t[:, self.at:self.at + words]
        self.at += (words + 7) // 8 * 8
        assert self.at <= self.words, (self.at, self.words)
        if dt != F32:
            ap = ap.bitcast(dt)[:, 0:n]
        if len(shape) > 1:
            names = "abcd"[:len(shape)]
            ap = ap.rearrange("p (" + " ".join(names) + ") -> p " + " ".join(names),
                              **{k: s for k, s in zip(names, shape)})
        return ap


def bc(ap, shape):
    return ap.broadcast_to(shape)


def build(nc, A, out):
    ctx = ExitStack()
    with ctx:
        def sb(name, shape, dt=F32):
            return ctx.enter_context(nc.sbuf_tensor(name, shape, dt))

        def sem(name):
            return ctx.enter_context(nc.semaphore(name))

        banks = [ctx.enter_context(nc.psum_tensor(f"bank{i}", [P, 512], F32)) for i in range(8)]
        RA = Ring(banks[0:2], sem("a_bank_filled"), sem("a_bank_read"))
        RB = Ring(banks[2:5], sem("b_bank_filled"), sem("b_bank_read"))
        RC = Ring(banks[5:8], sem("c_bank_filled"), sem("c_bank_read"))

        X = sb("X", [P, NT, D])
        ident = sb("ident", [P, P])
        identb = sb("identb", [P, P], BF16)
        ones = sb("ones", [P, P])
        zeros = sb("zeros", [P, D])
        before = sb("before", [P, P], BF16)
        onesb = sb("onesb", [P, P], BF16)
        hmask = sb("hmask", [P, 2])
        sel = sb("sel", [P, 16, P], BF16)
        selr = sb("selr", [P, 4, 4, 32], BF16)
        sgn = sb("sgn", [P, 1])
        nhalf = sb("nhalf", [P, NT])
        iota = sb("iota", [P, NTL])
        gates = sb("gates", [P, 8])
        tg = sb("tg", [P, 8])
        ctxT = sb("ctxT", [P, 2, B * M])
        stats = sb("stats", [P, NT, 6])
        mv = sb("mv", [P, NT, 2])
        rstd = sb("rstd", [P, NT])
        WA = 4864
        warena = [Arena(sb(f"weights{i}", [P, WA]), WA) for i in range(2)]
        SA = 35500
        scratch = Arena(sb("scratch", [P, SA]), SA)

        w_loaded = [sem(f"weights_loaded_{p}") for p in range(8)]
        in_loaded = sem("inputs_loaded")
        consts = sem("constants_made")
        tg_made = sem("gates_made")
        ln_stats = sem("ln_statistics")
        ln_rstd = sem("ln_rstd_made")
        ln_y = sem("ln_normalised")
        phase_over = sem("phase_over")
        kv_clear = sem("kv_buffers_cleared")
        kz_made = sem("keys_spread")
        kr_made = sem("last_keys_spread")
        kp_made = sem("key_parts_made")
        kp_stored = sem("key_parts_stored")
        k_stacked = sem("key_parts_stacked")
        qp0_made = sem("query_parts_of_first_chunks_made")
        krs_made = sem("key_lengths_inverted")
        qrs_made = sem("query_lengths_inverted")
        qp_made = sem("query_parts_of_later_chunks_made")
        qp_stored = [sem(f"query_parts_stored_{i}") for i in range(2)]
        q_stacked = [sem(f"query_parts_stacked_{i}") for i in range(2)]
        ones_row = sem("row_of_ones_loaded")
        v_made = sem("values_made")
        xbias = sem("bias_added_to_x")
        pool_st = sem("pool_steps")
        act_st = sem("act_steps")
        dve_st = sem("dve_steps")
        kn_made = sem("keys_normalised")
        kn_clear = sem("key_buffers_cleared")
        kss_made = sem("key_squares_summed")
        qss_made = sem("query_squares_summed")
        qn_made = sem("queries_normalised")
        qbo_made = sem("residual_query_ready")
        post_stats = sem("post_ln_statistics")
        post_z = sem("post_ln_normalised")
        mb_made = sem("mask_bias_made")
        gbo_made = sem("gated_bias_made")
        gc_ready = sem("global_net_inputs_ready")
        state_made = sem("coupled_state_made")
        wq_made = sem("weights_rounded")
        diag_made = sem("scales_on_the_diagonal")
        xmax_made = sem("largest_of_partition")
        xall_made = sem("largest_of_all")
        xi_made = sem("x_rounded")
        hscale_made = sem("hidden_scale_and_bias_made")
        hi_made = sem("hidden_rounded")
        hs_ready = sem("hidden_scale_of_second_rounding_made")
        hs_made = sem("hidden_scaled")
        rows_made = sem("output_scale_rows_made")
        oh_made = sem("one_hots_made")
        g_made = sem("gate_weights_made")
        ex_ready = sem("exponents_ready")
        ex_made = sem("exponentials_made")
        XB = {2: 1, 3: 2, 4: 3, 6: 4}
        x_out = sem("x_final")
        zero_made = sem("zeros_made")
        slots_clear = sem("slots_cleared")
        idx_made = sem("slot_indices_made")
        dumps_made = sem("spare_rows_numbered")
        scattered = sem("tokens_scattered")
        xe_loaded = [sem(f"expert_tokens_loaded_{i}") for i in range(3)]
        ye_stored = [sem(f"expert_results_stored_{i}") for i in range(3)]
        gathered = [sem(f"results_gathered_{i}") for i in range(8)]
        EWN = 4
        ew_loaded = [sem(f"expert3_loaded_{i}") for i in range(3)]
        e2_loaded = sem("experts2_loaded")
        et_made = sem("experts_of_tiles_made")
        NXT = 6
        xt_loaded = [sem(f"token_tile_loaded_{i}") for i in range(NXT)]
        yt_stored = [sem(f"result_tile_stored_{i}") for i in range(3)]
        stored = sem("output_stored")

        NIN = 2 * B + 3
        NCONST = 5

        ph = []
        loads = []

        def col(ap, n):
            return ap.rearrange("(m p) -> p m", p=P)

        def row(ap, n):
            return bc(ap.rearrange("(o n) -> o n", o=1), (P, n))

        def kin(ap):
            return ap.rearrange("(k p) n -> p k n", p=P)

        def ctxw(w, dst):
            return [(dst[:, 0, :], w[0:P, :]), (dst[0:CD - P, 1, :], w[P:CD, :])]

        for L in range(4):
            H, hd = HEADS[L]
            HD = H * hd
            MT, hpm, G = HD // P, P // hd, H // 4
            w = warena[(2 * L) % 2]
            w.reset()
            scratch.reset()
            v = dict(H=H, hd=hd, HD=HD, MT=MT, hpm=hpm, G=G)
            pre = f"L{L}_xattn_"
            nm = dict(Wq="wq", Wk="wk", Wv="wv", Wo="wo") if L == 2 else dict(Wq="Wq", Wk="Wk", Wv="Wv", Wo="Wo")
            if L == 1:
                nm["Wo"] = "Wout"
            ld = []
            v["Wq"] = w.take((DK, HD))
            v["Wk"] = w.take((2, HD))
            v["Wv"] = w.take((2, HD))
            v["vw"] = 32 if hd == 16 else hd + 1
            v["Wo"] = w.take((MT, D))
            ld += ctxw(A[pre + nm["Wk"]], v["Wk"])
            ld += ctxw(A[pre + nm["Wv"]], v["Wv"])
            ld.append((v["Wq"], kin(A[pre + nm["Wq"]])))
            if L == 2:
                v["bq"], v["bk"], v["bv"], v["bo"] = w.take((DK,)), w.take((DK,)), w.take((HD,)), w.take((D,))
                ld += [(v["bq"], col(A[pre + "bq"], DK)), (v["bk"], col(A[pre + "bk"], DK)),
                       (v["bv"], row(A[pre + "bv"], HD)), (v["bo"], row(A[pre + "bo"], D))]
            if L == 1:
                v["bo"] = w.take((D,))
                ld.append((v["bo"], row(A[pre + "bout"], D)))
            if L == 3:
                for k, s in (("bq", "bq"), ("bk", "bk"), ("bv", "bv"), ("bo", "bo"), ("lg", "ln_gamma"), ("lb", "ln_beta")):
                    v[k] = w.take((D,))
                    ld.append((v[k], row(A[pre + s], D)))
            if L == 0:
                v["m8"] = w.take((B * M,), U8)
                ld.append((v["m8"], bc(A["mask_BxS2_bf1"].rearrange("(o b) k -> o (b k)", o=1), (P, B * M))))
                v["m01"] = w.take((B * M,))
                v["mb"] = w.take((B * MP,), BF16)
            ld.append((v["Wo"], A[pre + nm["Wo"]].rearrange("(k p) n -> p k n", p=P)))
            v["Y"] = scratch.take((NT, D))
            v["yT"] = scratch.take((DK, CH))
            v["V"] = scratch.take((B, H, v["vw"]))
            v["Vr"] = scratch.take((B, G, 4, v["vw"]))
            v["PT"] = scratch.take((2, 5, CH))
            if L < 3:
                v["mx"] = scratch.take((NT, H))
                v["negm"] = scratch.take((NC, CH), BF16)
            if hd == 16:
                v["qf"] = scratch.take((2, MT, CH))
                v["qp"] = scratch.take((2, 3, MT, CH), BF16)
                v["kf"] = scratch.take((MT, B * MP))
                v["kp"] = scratch.take((3, MT, B * MP), BF16)
                v["Qs"] = scratch.take((2, H, CH), BF16)
                v["Ks"] = scratch.take((H, B * MP), BF16)
                v["av"] = scratch.take((2, CH))
                v["O"] = scratch.take((TPC, HD))
                v["oT"] = scratch.take((MT, CH))
                v["rden"] = scratch.take((2, 4 * TPC))
                v["rows"] = 16 * len(Q_PART) + (L == 0)
            else:
                v["QT"] = scratch.take((MT, T))
                v["Kz"] = scratch.take((MT * B, hpm, M))
                v["Kr"] = scratch.take((MT * B, hpm, 32))
                v["KTs"] = scratch.take((MT, B * M))
                v["O"] = scratch.take((2, TPC, HD))
                v["rden"] = scratch.take((2, 16))
            if L == 0:
                ctxN = scratch.take((2 * B, CD))
            v["gbo"] = scratch.take((D,))
            if L == 3:
                v["ss"] = scratch.take((NT + 4,))
                v["rs"] = scratch.take((NT + 4,))
                v["Kp"] = scratch.take((4, D))
                v["Qn"] = [v["Kp"], scratch.take((TPC, D))]
                v["gb"] = v["lb"]
                v["junk"] = scratch.take((D,))
            ph.append(v)
            loads.append(ld)

            w = warena[1]
            w.reset()
            scratch.reset()
            pre = f"L{L}_ffn_"
            v = dict()
            ld = []
            v["Y"] = scratch.take((NT, D))
            if L != 1:
                v["yT"] = scratch.take((DK, T))
            if L == 0:
                v["w1"], v["w2"], v["w3"], v["w4"] = w.take((DK, 256)), w.take((DK, 128)), w.take((64,)), w.take((1,))
                v["b1"], v["b2"], v["b3"], v["b4"] = w.take((DK,)), w.take((1,)), w.take((1,)), w.take((1,))
                v["g1"], v["g2"], v["g3"] = w.take((DK, 128)), w.take((64,)), w.take((1,))
                v["gb1"], v["gb2"], v["gb3"], v["ar"] = w.take((1,)), w.take((1,)), w.take((1,)), w.take((1,))
                o1 = lambda a: a.rearrange("(p o) -> p o", o=1)
                ld += [(v["g1"], kin(A[pre + "gc_w1"])), (v["g2"], A[pre + "gc_w2"]), (v["g3"][0:64], A[pre + "gc_w3"]),
                       (v["gb1"], o1(A[pre + "gc_b1"])), (v["gb2"][0:64], o1(A[pre + "gc_b2"])),
                       (v["gb3"], bc(o1(A[pre + "gc_b3"]), (P, 1))),
                       (v["w1"], kin(A[pre + "cn_w1"])), (v["w2"], kin(A[pre + "cn_w2"])),
                       (v["w3"], A[pre + "cn_w3"]), (v["w4"][0:64], A[pre + "cn_w4"]),
                       (v["b1"], col(A[pre + "cn_b1"], DK)), (v["b2"], o1(A[pre + "cn_b2"])),
                       (v["b3"][0:64], o1(A[pre + "cn_b3"])), (v["b4"], bc(o1(A[pre + "cn_b4"]), (P, 1))),
                       (v["ar"], bc(o1(A[pre + "adaptive_range"]), (P, 1)))]
                v["w4r"], v["g3r"] = scratch.take((P,)), scratch.take((P,))
                v["yS"] = scratch.take((DK, T))
                v["h1"] = scratch.take((DK, T))
                v["h2"] = scratch.take((T,))
                v["h3"] = scratch.take((T,))
                v["th"] = scratch.take((NC, CH))
                v["tmp"] = scratch.take((2, CH))
                v["msum"] = scratch.take((DK, NC))
                v["mean"] = scratch.take((DK, B))
                v["gh1"], v["gh2"], v["gt"] = scratch.take((B,)), scratch.take((B,)), scratch.take((B,))
                v["al"], v["be"] = scratch.take((1,)), scratch.take((B,))
                v["hb"] = scratch.take((2,))
            if L == 1:
                v["w1"], v["w2"] = w.take((FT1, D)), w.take((DK, F1))
                v["b1"] = w.take((FT1,))
                v["b2"] = w.take((D,))
                v["sw1"], v["iw1"] = w.take((FT1,)), w.take((FT1,))
                v["sw2"], v["iw2"] = w.take((DK,)), w.take((DK,))
                ld += [(v["w1"], A[pre + "w1"].rearrange("(f p) d -> p f d", p=P)),
                       (v["w2"], A[pre + "w2"].rearrange("(k p) f -> p k f", p=P)),
                       (v["b1"], col(A[pre + "b1"], FT1)), (v["b2"], row(A[pre + "b2"], D))]
                v["xi"] = scratch.take((NT, D), BF16)
                v["xT"] = scratch.take((DK, T), BF16)
                v["hi"] = scratch.t[:, 0:FT1 * T // 2].bitcast(BF16).rearrange("p (f t) -> p f t", f=FT1)
                assert scratch.at == FT1 * T // 2
                v["wi1"] = scratch.take((FT1, D), BF16)
                v["wi2"] = scratch.take((DK, F1), BF16)
                v["w1T"] = scratch.take((DK, F1), BF16)
                v["w2T"] = scratch.take((FT1, D), BF16)
                v["h"] = scratch.take((FT1, T))
                v["diag"] = scratch.take((DK, P))
                v["sw2r"] = scratch.take((D,))
                v["rowS"], v["rowT"], v["rowB"], v["rowI"] = (scratch.take((D,)) for _ in range(4))
                v["m"] = scratch.take((64,))
                v["sc"] = scratch.take((16,))
                v["sb1"], v["ib1"], v["bq1"] = scratch.take((FT1,)), scratch.take((FT1,)), scratch.take((FT1,))
                v["dn"] = scratch.take((2, 2, D))
                v["rnd"] = scratch.take((1,))
            if L >= 2:
                E = E2 if L == 2 else E3
                v["Wr"], v["br"] = w.take((DK, E)), w.take((E,))
                ld += [(v["Wr"], kin(A[pre + ("Wr" if L == 2 else "router_w")])),
                       (v["br"], row(A[pre + ("br" if L == 2 else "router_b")], E))]
                v["lg"], v["G"], v["oh"], v["pre"] = (scratch.take((NT, E)) for _ in range(4))
                v["oh2"] = scratch.take((NT, E))
                v["top"] = scratch.take((NT, 8))
                v["idx"] = scratch.take((NT, 8), U32)
                v["idf"] = scratch.take((NT, 8))
                v["r"] = scratch.take((12, NT))
                v["GT"] = scratch.take((T,))
            if L == 2:
                v["b1"], v["b2"] = w.take((E2 * H2,)), w.take((D,))
                ld += [(v["b1"], row(A[pre + "b1"].rearrange("e h -> (e h)"), E2 * H2)), (v["b2"][0:E2], A[pre + "b2"])]
                v["ohb"] = scratch.take((NT, E), BF16)
                v["ohs"] = scratch.take((NT + 1, E), BF16)
                v["W1"] = scratch.take((DK, E2 * H2))
                v["W2"] = scratch.take((H2 // P, E2 * D))
                v["xe"] = scratch.take((NXT, D))
                v["xeT"] = scratch.take((2, DK * P))
                v["h"] = scratch.take((2, H2))
                v["hT"] = scratch.take((2, H2 // P, P))
                v["ye"] = scratch.take((3, D))
                v["cnt"], v["til"], v["base"] = scratch.take((E,)), scratch.take((E,)), scratch.take((E,))
                v["cmp"] = scratch.take((NTL, E - 1))
                v["etf"], v["et"] = scratch.take((NTL,)), scratch.take((NTL,), U32)
                v["pk"], v["wk"] = scratch.take((NT, 2)), scratch.take((NT, 2))
                v["sidx"] = scratch.take((2 * NT,), U32)
                v["gidx"] = v["sidx"]
                v["yk"] = v["yT"].rearrange("p k (t d) -> p (k t) d", d=D)
            if L == 3:
                v["ohb"] = scratch.take((NT, E), BF16)
                v["ohs"] = scratch.take((NT + 1, E), BF16)
                v["Wg"] = scratch.take((3, DK, F3))
                v["Wu"] = scratch.take((3, DK, F3))
                v["Wd"] = scratch.take((3, 3, D))
                v["sg"] = scratch.take((4, CH))
                v["hT"] = scratch.take((2 * 3, CH))
                v["xe"] = scratch.take((3, 3, D))
                v["xeT"] = scratch.take((2 * DK, CAP))
                v["ye"] = scratch.take((3, 3, D))
                v["dump"], v["slot"], v["row"] = scratch.take((NT, 2)), scratch.take((NT, 2)), scratch.take((NT, 2))
                v["pk"], v["wk"] = scratch.take((NT, 2)), scratch.take((NT, 2))
                v["sidx"], v["gidx"] = scratch.take((2 * NT,), U32), scratch.take((2 * NT,), U32)
                v["yk"] = scratch.take((NT, D))
            ph.append(v)
            loads.append(ld)
        NPH = PHASES

        x_slots = nc.dram_tensor("x_slots", (E3 * CAP + 2 * T, D), F32, kind="Internal").ap()
        y_slots = nc.dram_tensor("y_slots", (E3 * CAP, D), F32, kind="Internal").ap()
        SHARED = ((0, 1), (2, 3))

        q_parts = nc.dram_tensor("q_parts", (NC, 3, D, CH), BF16, kind="Internal").ap()
        k_parts = nc.dram_tensor("k_parts", (3, D, B * MP), BF16, kind="Internal").ap()
        NPAIR = len(Q_PART)
        LA = {0: 0, 2: 1, 3: 2}
        FIRST = {0: 1, 2: 1, 3: 2}

        def lnorm(p, c):
            return NC * p + c + 1

        ATT = [("front", 0), ("front", 1), ("back", 0), ("front", 2), ("tail", 0), ("back", 1),
               ("front", 3), ("tail", 1), ("back", 2), ("tail", 2), ("back", 3), ("tail", 3)]

        def steps16(L):
            has_max = L < 3
            if has_max:
                o = [("keys", 0), ("proj", 0), ("turn", 0), ("proj", 1), ("rest", 0), ("turn", 1), ("values", 0)]
            else:
                o = [("keys", 0), ("proj", 0), ("unit keys", 0), ("keys turned", 0), ("proj", 1), ("unit", 0), ("turn", 0),
                     ("unit", 1), ("turn", 1), ("values", 0), ("rest", 0)]
            if has_max:
                o += [("max", 0, i) for i in range(TPC)] + [("negm", 0)]

            for c in range(NC):
                def if_next(*step):
                    return [step] if has_max and c + 1 < NC else []

                def if_last(*step):
                    return [step] if c else []

                def if_later(*step):
                    return [step] if c + 2 < NC else []
                o += [("scores", c, 0), *if_last("norm", c - 1, 3),
                      ("scores", c, 1), ("av", c, 0), *if_last("turn back", c - 1), *if_next("max", c + 1, 0),
                      ("scores", c, 2), ("av", c, 1), ("norm", c, 0), *if_last("tail", c - 1), *if_next("max", c + 1, 1),
                      *if_later("proj", c + 2),
                      ("scores", c, 3), *if_later("unit", c + 2), *if_next("max", c + 1, 2), ("av", c, 2), ("norm", c, 1), *if_next("max", c + 1, 3),
                      *if_later("turn", c + 2), ("av", c, 3), *if_next("negm", c + 1), ("norm", c, 2)]
            o += [("norm", NC - 1, 3), ("turn back", NC - 1)]
            return o + [("tail", NC - 1)]

        def stacked(L, c):
            return 16 * NPAIR * (2 * LA[L] + c // 2 + 1)

        def shared_order(half):
            a, b = SHARED[half]
            return [("up", a), ("up", b), ("down", a), ("down", b)]

        def tile_steps():
            o = [("in", 0), ("in", 1)]
            for i in range(NTL + 2):
                o += [("up", i), ("in", i + 2), ("turn", i - 1), ("down", i - 2)]
            return [x for n, x in enumerate(o) if 0 <= x[1] < NTL and x not in o[:n]]

        def split(eng, st, p, v, c, made):
            s = c % 2
            q, parts = v["qf"][:, s], v["qp"][:, s]
            eng.wait_ge(RA.read, RA.n(p, "q", c, v["MT"] - 1))
            st.did(eng.tensor_tensor(q, q, parts[:, 0], ALU.subtract))
            st.wait()
            st.did(eng.tensor_copy(parts[:, 1], q))
            st.wait()
            eng.tensor_tensor(parts[:, 2], q, parts[:, 1], ALU.subtract).then_inc(made, 1)

        block = ctx.enter_context(nc.Block())

        @block.tensor
        def _(pe):
            def transpose_y(p, v, c):
                pe.wait_ge(ln_y, lnorm(p, c))
                for d in range(DK):
                    bk = RA.take(pe, p, "yT", c, d)
                    for i in range(TPC):
                        last = pe.transpose(bk[:, i * P:(i + 1) * P], v["Y"][:, TPC * c + i, d * P:(d + 1) * P], ident[:])
                    last.then_inc(RA.filled, 1)

            def context_transposed(p):
                pe.wait_ge(consts, NCONST)
                pe.wait_ge(in_loaded, 16 * NIN)
                for b in range(B):
                    bk = RA.take(pe, p, "ctx", b)
                    pe.transpose(bk[:, 0:P], ctxN[:, b, 0:P], ident[:])
                    pe.transpose(bk[:, P:M], ctxN[0:MR, B + b, 0:P], ident[0:MR, 0:MR])
                    pe.transpose(bk[0:CD - P, 160:160 + P], ctxN[:, b, P:CD], ident[:])
                    pe.transpose(bk[0:CD - P, 160 + P:160 + M], ctxN[0:MR, B + b, P:CD],
                                 ident[0:MR, 0:MR]).then_inc(RA.filled, 1)
                pe.wait_ge(RA.read, RA.n(p, "ctx", B - 1))

            def keys(p, v):
                for m in range(v["MT"]):
                    bk = RB.take(pe, p, "k", m)
                    pe.matmul(bk[:, 0:B * M], v["Wk"][:, 0, m * P:(m + 1) * P], ctxT[:, 0, :], start=True, stop=False)
                    pe.matmul(bk[:, 0:B * M], v["Wk"][0:CD - P, 1, m * P:(m + 1) * P], ctxT[0:CD - P, 1, :],
                              start=False, stop=True).then_inc(RB.filled, 1)

            def ctx_rows(p, v, kind, w):
                HD = v["HD"]
                for b in range(B):
                    for s, (k0, kn) in enumerate(((0, P), (P, MR))):
                        bk = RB.take(pe, p, kind, b, s)
                        o = b * M + k0
                        pe.matmul(bk[0:kn, 0:HD], ctxT[:, 0, o:o + kn], w[:, 0, :], start=True, stop=False)
                        pe.matmul(bk[0:kn, 0:HD], ctxT[0:CD - P, 1, o:o + kn], w[0:CD - P, 1, :],
                                  start=False, stop=True).then_inc(RB.filled, 1)

            def project(p, v, c):
                for m in range(v["MT"]):
                    bk = RA.take(pe, p, "q", c, m)
                    for k in range(DK):
                        last = pe.matmul(bk[:], v["Wq"][:, k, m * P:(m + 1) * P], v["yT"][:, k, :],
                                         start=k == 0, stop=k == DK - 1)
                    last.then_inc(RA.filled, 1)

            def maxima_transposed(p, v, c, key):
                H = v["H"]
                pe.wait_ge(RB.read, RB.n(p, "mxs", c, *key))
                bk = RB.take(pe, p, "mx", c)
                for i in range(TPC):
                    last = pe.transpose(bk[0:H, i * P:(i + 1) * P], v["mx"][:, TPC * c + i, :], ident[:])
                last.then_inc(RB.filled, 1)

            def output(p, v, c, rows):
                for q in range(2):
                    bk = RB.take(pe, p, "out", c, q)
                    for i in range(2):
                        tt = 2 * q + i
                        for m, o in enumerate(rows):
                            last = pe.matmul(bk[:, i * D:(i + 1) * D], o[:, tt * P:(tt + 1) * P],
                                             v["Wo"][:, m, :], start=m == 0, stop=m == len(rows) - 1)
                    last.then_inc(RB.filled, 1)

            def attention16(p, L):
                v = ph[p]
                H, MT, G, R = v["H"], v["MT"], v["G"], v["rows"]
                pe.wait_ge(w_loaded[p], 16 * len(loads[p]))
                if L == 0:
                    context_transposed(p)
                for what, c, *i in steps16(L):
                    b, s = c // CPB, c % 2
                    i = i[0] if i else None
                    if what == "keys":
                        keys(p, v) if L < 3 else ctx_rows(p, v, "kp", v["Wk"])
                    elif what == "values":
                        ctx_rows(p, v, "v", v["Wv"])
                    elif what == "keys turned":
                        pe.wait_ge(kn_made, 1)
                        for m in range(MT):
                            bk = RB.take(pe, p, "k", m)
                            for n in range(B):
                                pe.transpose(bk[:, n * M:n * M + P], v["Kp"][:, 2 * n, m * P:(m + 1) * P], ident[:])
                                last = pe.transpose(bk[:, n * M + P:(n + 1) * M], v["Kp"][0:MR, 2 * n + 1, m * P:(m + 1) * P],
                                                    ident[0:MR, 0:MR])
                            last.then_inc(RB.filled, 1)
                    elif what == "proj":
                        transpose_y(p, v, c)
                        pe.wait_ge(RA.read, RA.n(p, "yT", c, DK - 1))
                        if L < 3:
                            project(p, v, c)
                            continue
                        for q in range(2):
                            bk = RB.take(pe, p, "qp", c, q)
                            for j in range(2):
                                tt = 2 * q + j
                                for k in range(DK):
                                    last = pe.matmul(bk[:, j * D:(j + 1) * D], v["yT"][:, k, tt * P:(tt + 1) * P],
                                                     v["Wq"][:, k, :], start=k == 0, stop=k == DK - 1)
                            last.then_inc(RB.filled, 1)
                    elif what == "turn" and L == 3:
                        pe.wait_ge(qn_made, c + 1)
                        for m in range(MT):
                            bk = RA.take(pe, p, "q", c, m)
                            for j in range(TPC):
                                last = pe.transpose(bk[:, j * P:(j + 1) * P], v["Qn"][s][:, j, m * P:(m + 1) * P], ident[:])
                            last.then_inc(RA.filled, 1)
                    elif what == "max":
                        if i == 0:
                            pe.wait_ge(q_stacked[s], stacked(L, c))
                            if c == 0:
                                pe.wait_ge(k_stacked, 16 * NPAIR * (LA[L] + 1))
                                if L == 0:
                                    pe.wait_ge(ones_row, 32)
                                    pe.wait_ge(mb_made, 1)
                        for h0 in range(0, H, 3):
                            hn = min(3, H - h0)
                            bk = RB.take(pe, p, "mxs", c, i, h0)
                            for j in range(hn):
                                last = pe.matmul(bk[:, j * M:(j + 1) * M], v["Qs"][0:R, s, h0 + j, i * P:(i + 1) * P],
                                                 v["Ks"][0:R, h0 + j, b * MP:b * MP + M], start=True, stop=True)
                            last.then_inc(RB.filled, 1)
                    elif what == "negm":
                        maxima_transposed(p, v, c, (TPC - 1, (H - 1) // 3 * 3))
                    elif what == "scores":
                        if i == 0:
                            pe.wait_ge(q_stacked[s], stacked(L, c))
                            if c == 0:
                                pe.wait_ge(k_stacked, 16 * NPAIR * (LA[L] + 1))
                            if L < 3:
                                pe.wait_ge(RB.read, RB.n(p, "mx", c))
                        for j in range(4):
                            h = 4 * i + j
                            bk = RC.take(pe, p, "s", c, i, j)
                            last = pe.matmul(bk[:], v["Ks"][0:R, h, b * MP:b * MP + P], v["Qs"][0:R, s, h, :],
                                             start=True, stop=L == 3)
                            if L < 3:
                                last = pe.matmul(bk[:], sel[:, h, :], v["negm"][:, c, :], start=False, stop=True)
                            last.then_inc(RC.filled, 1)
                        bk = RC.take(pe, p, "s", c, i, 4)
                        if L < 3:
                            pe.matmul(bk[:], selr[:, i, :, :].rearrange("p j k -> p (j k)"), v["negm"][:, c, :],
                                      start=True, stop=False)
                        for j in range(4):
                            h = 4 * i + j
                            last = pe.matmul(bk[32 * j:32 * (j + 1), :], v["Ks"][0:R, h, b * MP + P:(b + 1) * MP],
                                             v["Qs"][0:R, s, h, :], start=L == 3, stop=True)
                        last.then_inc(RC.filled, 1)
                    elif what == "av":
                        if c == 0 and i == 0:
                            pe.wait_ge(v_made, 4 * (L + 1))
                        slot = (c * G + i) % 2
                        pe.wait_ge(RC.read, RC.n(p, "s", c, i, 4))
                        bk = RC.take(pe, p, "av", c, i)
                        for j in range(4):
                            pe.matmul(bk[32 * j:32 * (j + 1), :], v["V"][:, b, 4 * i + j, :],
                                      v["PT"][:, slot, j, :], start=True, stop=False)
                        for j in range(4):
                            last = pe.matmul(bk[32 * j:32 * (j + 1), :], v["Vr"][:, b, i, j, :],
                                             v["PT"][:, slot, 4, :], start=False, stop=True)
                        last.then_inc(RC.filled, 1)
                    elif what == "norm":
                        pe.wait_ge(RC.read, RC.n(p, "av", c, i))
                        bk = RB.take(pe, p, "norm", c, i)
                        for j in range(TPC):
                            last = pe.transpose(bk[:, j * P:(j + 1) * P], v["av"][:, i % 2, j * P:(j + 1) * P], ident[:])
                        last.then_inc(RB.filled, 1)
                    elif what == "turn back":
                        pe.wait_ge(RB.read, RB.n(p, "norm", c, G - 1))
                        for m in range(MT):
                            bk = RA.take(pe, p, "oT", c, m)
                            for j in range(TPC):
                                last = pe.transpose(bk[:, j * P:(j + 1) * P], v["O"][:, j, m * P:(m + 1) * P], ident[:])
                            last.then_inc(RA.filled, 1)
                    elif what == "tail":
                        pe.wait_ge(RA.read, RA.n(p, "oT", c, MT - 1))
                        output(p, v, c, [v["oT"][:, m, :] for m in range(MT)])

            def attention(p, L):
                v = ph[p]
                H, hd, MT, hpm, G = (v[k] for k in ("H", "hd", "MT", "hpm", "G"))
                pe.wait_ge(w_loaded[p], 16 * len(loads[p]))

                def queries(c):
                    transpose_y(p, v, c)
                    pe.wait_ge(RA.read, RA.n(p, "yT", c, DK - 1))
                    project(p, v, c)

                queries(0)
                keys(p, v)
                ctx_rows(p, v, "v", v["Wv"])
                for what, c in ATT:
                    b = c // CPB
                    cs = slice(c * CH, (c + 1) * CH)
                    if what == "front":
                        if c:
                            queries(c)
                        pe.wait_ge(RA.read, RA.n(p, "q", c, MT - 1))
                        pe.wait_ge(kz_made, B * MT)
                        for i in range(TPC):
                            q0 = c * CH + i * P
                            for m in range(MT):
                                bk = RB.take(pe, p, "mxs", c, i, m)
                                pe.matmul(bk[:, 0:hpm * M], v["QT"][:, m, q0:q0 + P],
                                          v["Kz"][:, m * B + b, :, :].rearrange("p h k -> p (h k)"),
                                          start=True, stop=True).then_inc(RB.filled, 1)
                    elif what == "back":
                        pe.wait_ge(kr_made, B * MT)
                        pe.wait_ge(v_made, 4 * (L + 1))
                        maxima_transposed(p, v, c, (TPC - 1, MT - 1))
                        for g in range(G + 1):
                            if g < G:
                                for j in range(4):
                                    h = 4 * g + j
                                    bk = RC.take(pe, p, "s", c, g, j)
                                    pe.matmul(bk[:], v["Kz"][:, (h // hpm) * B + b, h % hpm, 0:P], v["QT"][:, h // hpm, cs],
                                              start=True, stop=False)
                                    if g == 0 and j == 0:
                                        pe.wait_ge(RB.read, RB.n(p, "mx", c))
                                    pe.matmul(bk[:], sel[:, h, :], v["negm"][:, c, :], start=False, stop=True)\
                                      .then_inc(RC.filled, 1)
                                bk = RC.take(pe, p, "s", c, g, 4)
                                pe.matmul(bk[:], selr[:, g, :, :].rearrange("p j k -> p (j k)"), v["negm"][:, c, :],
                                          start=True, stop=False)
                                for n in range(2):
                                    m = 2 * g + n
                                    last = pe.matmul(bk[64 * n:64 * (n + 1), :],
                                                     v["Kr"][:, m * B + b, :, :].rearrange("p h k -> p (h k)"),
                                                     v["QT"][:, m, cs], start=False, stop=True)
                                last.then_inc(RC.filled, 1)
                            if g > 0:
                                gg = g - 1
                                slot = (c * G + gg) % 2
                                pe.wait_ge(RC.read, RC.n(p, "s", c, gg, 4))
                                w = hd + 1
                                for i in range(TPC):
                                    bk = RB.take(pe, p, "av", c, gg, i)
                                    qs = slice(i * P, (i + 1) * P)
                                    pe.matmul(bk[:, 0:4 * w], v["PT"][:, slot, 4, qs],
                                              v["Vr"][:, b, gg, :, :].rearrange("p j d -> p (j d)"), start=True, stop=False)
                                    for j in range(4):
                                        last = pe.matmul(bk[:, j * w:(j + 1) * w], v["PT"][:, slot, j, qs],
                                                         v["V"][:, b, 4 * gg + j, :], start=False, stop=j == 3)
                                    last.then_inc(RB.filled, 1)
                    else:
                        pe.wait_ge(RB.read, RB.n(p, "av", c, G - 1, TPC - 1))
                        for m in range(MT):
                            bk = RA.take(pe, p, "oT", c, m)
                            for i in range(TPC):
                                last = pe.transpose(bk[:, i * P:(i + 1) * P], v["O"][:, c % 2, i, m * P:(m + 1) * P], ident[:])
                            last.then_inc(RA.filled, 1)
                        pe.wait_ge(RA.read, RA.n(p, "oT", c, MT - 1))
                        output(p, v, c, [v["QT"][:, m, cs] for m in range(MT)])

            def coupling(p):
                v = ph[p]
                pe.wait_ge(w_loaded[p], 16 * len(loads[p]))
                for c in range(NC):
                    transpose_y(p, v, c)

                def global_net(layer):
                    if layer == 1:
                        pe.wait_ge(gc_ready, 1)
                        bk = RA.take(pe, p, "g1")
                        for k in range(DK):
                            last = pe.matmul(bk[:, 0:B], v["g1"][:, k, :], v["mean"][:, k, :], start=k == 0, stop=k == DK - 1)
                        last.then_inc(RA.filled, 1)
                    elif layer == 2:
                        pe.wait_ge(RA.read, RA.n(p, "g1"))
                        bk = RA.take(pe, p, "g2")
                        pe.matmul(bk[0:64, 0:B], v["g2"][:], v["gh1"][:], start=True, stop=True).then_inc(RA.filled, 1)
                    else:
                        pe.wait_ge(RA.read, RA.n(p, "g2"))
                        bk = RA.take(pe, p, "g3")
                        pe.matmul(bk[:, 0:B], v["g3r"][0:64], v["gh2"][0:64], start=True, stop=True).then_inc(RA.filled, 1)

                st = [v["yT"], v["yS"]]
                for r in range(3):
                    for c in range(NC):
                        cs = slice(c * CH, (c + 1) * CH)
                        if r:
                            pe.wait_ge(state_made, NC * (r - 1) + c + 1)
                        for m in range(DK):
                            bk = RC.take(pe, p, r, "l1", c, m)
                            for k in range(DK):
                                last = pe.matmul(bk[:], v["w1"][:, k, m * P:(m + 1) * P], st[r % 2][:, k, cs],
                                                 start=k == 0, stop=k == DK - 1)
                            last.then_inc(RC.filled, 1)
                    if r == 0:
                        global_net(1)
                    for c in range(NC):
                        cs = slice(c * CH, (c + 1) * CH)
                        pe.wait_ge(RC.read, RC.n(p, r, "l1", c, DK - 1))
                        bk = RC.take(pe, p, r, "l2", c)
                        for k in range(DK):
                            last = pe.matmul(bk[:], v["w2"][:, k, :], v["h1"][:, k, cs], start=k == 0, stop=k == DK - 1)
                        last.then_inc(RC.filled, 1)
                    if r == 0:
                        global_net(2)
                    for c in range(NC):
                        cs = slice(c * CH, (c + 1) * CH)
                        pe.wait_ge(RC.read, RC.n(p, r, "l2", c))
                        bk = RC.take(pe, p, r, "l3", c)
                        pe.matmul(bk[0:64, :], v["w3"][:], v["h2"][:, cs], start=True, stop=True).then_inc(RC.filled, 1)
                    if r == 0:
                        global_net(3)
                    for c in range(NC):
                        cs = slice(c * CH, (c + 1) * CH)
                        pe.wait_ge(RC.read, RC.n(p, r, "l3", c))
                        bk = RC.take(pe, p, r, "l4", c)
                        pe.matmul(bk[:], v["w4r"][:], v["h3"][:, cs], start=True, stop=True).then_inc(RC.filled, 1)
                for c in range(NC):
                    pe.wait_ge(state_made, NC * 2 + c + 1)
                    for q in range(2):
                        bk = RB.take(pe, p, "fin", c, q)
                        for i in range(2):
                            t = (2 * c + q) * 2 + i
                            for k in range(DK):
                                last = pe.transpose(bk[:, i * D + k * P:i * D + (k + 1) * P], st[1][:, k, t * P:(t + 1) * P], ident[:])
                        last.then_inc(RB.filled, 1)

            def quantised(p):
                v = ph[p]
                pe.wait_ge(wq_made, 1)
                for d in range(DK):
                    bk = RA.take(pe, p, "w1T", d)
                    o = bk[:].bitcast(BF16)
                    for f in range(FT1):
                        last = pe.transpose(o[:, f * P:(f + 1) * P], v["wi1"][:, f, d * P:(d + 1) * P], identb[:])
                    last.then_inc(RA.filled, 1)
                for d in range(DK):
                    bk = RA.take(pe, p, "w2T", d)
                    o = bk[:].bitcast(BF16)
                    for f in range(FT1):
                        last = pe.transpose(o[:, f * P:(f + 1) * P], v["wi2"][:, d, f * P:(f + 1) * P], identb[:])
                    last.then_inc(RA.filled, 1)
                pe.wait_ge(diag_made, 1)
                bk = RB.take(pe, p, "sw2r")
                for d in range(DK):
                    last = pe.matmul(bk[:, d * P:(d + 1) * P], ones[:], v["diag"][:, d, :], start=True, stop=True)
                last.then_inc(RB.filled, 1)
                for n in range(NC + 1):
                    if n < NC:
                        c = n
                        pe.wait_ge(xi_made, c + 1)
                        bk = RA.take(pe, p, "xT", c)
                        o = bk[:].bitcast(BF16)
                        for d in range(DK):
                            for i in range(TPC):
                                last = pe.transpose(o[:, d * CH + i * P:d * CH + (i + 1) * P],
                                                    v["xi"][:, TPC * c + i, d * P:(d + 1) * P], identb[:])
                        last.then_inc(RA.filled, 1)
                    if n:
                        c = n - 1
                        cs = slice(c * CH, (c + 1) * CH)
                        pe.wait_ge(RA.read, RA.n(p, "xT", c))
                        for f in range(FT1):
                            bk = RC.take(pe, p, "up", c, f)
                            for k in range(DK):
                                last = pe.matmul(bk[:], v["w1T"][:, k, f * P:(f + 1) * P], v["xT"][:, k, cs],
                                                 start=k == 0, stop=k == DK - 1)
                            last.then_inc(RC.filled, 1)
                for c in range(NC):
                    pe.wait_ge(hi_made, c + 1)
                    for q in range(2):
                        bk = RB.take(pe, p, "dn", c, q)
                        for i in range(2):
                            t = (2 * c + q) * 2 + i
                            for f in range(FT1):
                                last = pe.matmul(bk[:, i * D:(i + 1) * D], v["hi"][:, f, t * P:(t + 1) * P], v["w2T"][:, f, :],
                                                 start=f == 0, stop=f == FT1 - 1)
                        last.then_inc(RB.filled, 1)

            def route(p, L):
                v = ph[p]
                E = E2 if L == 2 else E3
                pe.wait_ge(w_loaded[p], 16 * len(loads[p]))
                for c in range(NC + 1):
                    if c < NC:
                        transpose_y(p, v, c)
                        pe.wait_ge(RA.read, RA.n(p, "yT", c, DK - 1))
                        bk = RA.take(pe, p, "lgT", c)
                        for k in range(DK):
                            last = pe.matmul(bk[0:E, :], v["Wr"][:, k, :], v["yT"][:, k, c * CH:(c + 1) * CH],
                                             start=k == 0, stop=k == DK - 1)
                        last.then_inc(RA.filled, 1)
                    if c:
                        pe.wait_ge(RA.read, RA.n(p, "lgT", c - 1))
                        bk = RB.take(pe, p, "lg", c - 1)
                        for i in range(TPC):
                            t = TPC * (c - 1) + i
                            last = pe.transpose(bk[:, i * E:(i + 1) * E], v["GT"][0:E, t * P:(t + 1) * P], ident[0:E, 0:E])
                        last.then_inc(RB.filled, 1)

            def places(p, v, E, layer):
                pe.wait_ge(oh_made, layer - 1)
                bk = RB.take(pe, p, "pos")
                for t in range(NT):
                    last = pe.matmul(bk[:, t * E:(t + 1) * E], before[:], v["ohb"][:, t, :], start=True, stop=t == 0)
                    if t:
                        last = pe.matmul(bk[:, t * E:(t + 1) * E], onesb[:], v["ohs"][:, t, :], start=False, stop=True)
                if layer == 2:
                    last = pe.matmul(bk[:, NT * E:(NT + 1) * E], onesb[:], v["ohs"][:, NT, :], start=True, stop=True)
                last.then_inc(RB.filled, 1)

            def tiled_experts(p):
                v = ph[p]
                E = E2
                route(p, 2)
                places(p, v, E, 2)
                pe.wait_ge(g_made, 1)
                for c in range(NC):
                    bk = RA.take(pe, p, "gT", c)
                    for i in range(TPC):
                        last = pe.transpose(bk[0:E, i * P:(i + 1) * P], v["G"][:, TPC * c + i, :], ident[:])
                    last.then_inc(RA.filled, 1)
                for c in range(NC):
                    pe.wait_ge(RA.read, RA.n(p, "gT", c))
                    for q in range(2):
                        bk = RB.take(pe, p, "b2", c, q)
                        for i in range(2):
                            t = (2 * c + q) * 2 + i
                            last = pe.matmul(bk[:, i * D:(i + 1) * D], v["GT"][0:E, t * P:(t + 1) * P], v["b2"][0:E, :],
                                             start=True, stop=True)
                        last.then_inc(RB.filled, 1)
                pe.wait_ge(e2_loaded, 16 * 2 * E2)
                pe.wait_ge(et_made, 1)
                expert = {}
                for what, i in tile_steps():
                    if what == "in":
                        pe.wait_ge(xt_loaded[i % NXT], 16 * (i // NXT + 1))
                        bk = RA.take(pe, p, "in", i)
                        for d in range(DK):
                            last = pe.transpose(bk[:, d * P:(d + 1) * P], v["xe"][:, i % NXT, d * P:(d + 1) * P], ident[:])
                        last.then_inc(RA.filled, 1)
                    elif what == "up":
                        expert[i] = pe.value_load(v["et"][0:1, i:i + 1], min_val=0, max_val=E2 - 1)
                        pe.wait_ge(RA.read, RA.n(p, "in", i))
                        bk = RB.take(pe, p, "up", i)
                        for k in range(DK):
                            last = pe.matmul(bk[:], v["xeT"][:, i % 2, k * P:(k + 1) * P],
                                             v["W1"][:, k, bass.ds(expert[i] * H2, H2)], start=k == 0, stop=k == DK - 1)
                        last.then_inc(RB.filled, 1)
                    elif what == "turn":
                        pe.wait_ge(RB.read, RB.n(p, "up", i))
                        bk = RA.take(pe, p, "turn", i)
                        for m in range(H2 // P):
                            last = pe.transpose(bk[:, m * P:(m + 1) * P], v["h"][:, i % 2, m * P:(m + 1) * P], ident[:])
                        last.then_inc(RA.filled, 1)
                    else:
                        pe.wait_ge(RA.read, RA.n(p, "turn", i))
                        bk = RC.take(pe, p, "down", i)
                        for m in range(H2 // P):
                            last = pe.matmul(bk[:, 0:D], v["hT"][:, i % 2, m, :], v["W2"][:, m, bass.ds(expert[i] * D, D)],
                                             start=m == 0, stop=m == H2 // P - 1)
                        last.then_inc(RC.filled, 1)

            def routed_experts(p):
                v = ph[p]
                route(p, 3)
                places(p, v, E3, 3)

                def gate_up(s, key, moving, n):
                    for m in range(3):
                        fn = F3T[m]
                        for ring, w, name in ((RA, v["Wg"], "gate"), (RB, v["Wu"], "up")):
                            bk = ring.take(pe, p, name, *key, m)
                            for k in range(DK):
                                last = pe.matmul(bk[0:fn, 0:n], w[:, s, k, m * P:m * P + fn], moving(k),
                                                 start=k == 0, stop=k == DK - 1)
                            last.then_inc(ring.filled, 1)

                def shared(half, s, n):
                    pe.wait_ge(ew_loaded[s], 16 * EWN * n)
                    for what, c in shared_order(half):
                        if what == "up":
                            gate_up(s, (E3, c), lambda k: v["yT"][:, k, c * CH:(c + 1) * CH], CH)
                            continue
                        pe.wait_ge(RB.read, RB.n(p, "up", E3, c, 2))
                        for q in range(2):
                            bk = RB.take(pe, p, "dn", E3, c, q)
                            for i in range(2):
                                tt = q * 2 + i
                                for m in range(3):
                                    fn = F3T[m]
                                    last = pe.matmul(bk[:, i * D:(i + 1) * D],
                                                     v["hT"][0:fn, c % 2 * 3 + m, tt * P:(tt + 1) * P],
                                                     v["Wd"][0:fn, s, m, :], start=m == 0, stop=m == 2)
                            last.then_inc(RB.filled, 1)

                def tokens_of(e):
                    pe.wait_ge(xe_loaded[e % 3], 16 * 2 * (e // 3 + 1))
                    for d in range(DK):
                        bk = RA.take(pe, p, "xeT", e, d)
                        for i, n in enumerate((P, P, CAP - 2 * P)):
                            last = pe.transpose(bk[:, i * P:i * P + n], v["xe"][0:n, e % 3, i, d * P:(d + 1) * P], ident[0:n, 0:n])
                        last.then_inc(RA.filled, 1)

                shared(0, 0, 1)
                tokens_of(0)
                for e in range(E3):
                    s = (e + 1) % 3
                    pe.wait_ge(ew_loaded[s], 16 * EWN * ((e + 1) // 3 + 1))
                    pe.wait_ge(RA.read, RA.n(p, "xeT", e, DK - 1))
                    gate_up(s, (e, 0), lambda k: v["xeT"][:, e % 2 * DK + k, :], CAP)
                    if e + 1 < E3:
                        tokens_of(e + 1)
                    pe.wait_ge(RB.read, RB.n(p, "up", e, 0, 2))
                    for q, tiles in enumerate(((0, 1), (2,))):
                        bk = RC.take(pe, p, "dn", e, q)
                        for i in tiles:
                            n = min(P, CAP - i * P)
                            for m in range(3):
                                fn = F3T[m]
                                last = pe.matmul(bk[0:n, i % 2 * D:(i % 2 + 1) * D], v["hT"][0:fn, e % 2 * 3 + m, i * P:i * P + n],
                                                 v["Wd"][0:fn, s, m, :], start=m == 0, stop=m == 2)
                        last.then_inc(RC.filled, 1)

                shared(1, (E3 + 1) % 3, (E3 + 1) // 3 + 1)

            for p in range(NPH):
                L = p // 2
                if p:
                    pe.wait_ge(phase_over, p)
                if p % 2 == 0:
                    (attention if L == 1 else attention16)(p, L)
                elif L == 0:
                    coupling(p)
                elif L == 1:
                    quantised(p)
                elif L == 2:
                    tiled_experts(p)
                else:
                    routed_experts(p)

        @block.scalar
        def _(act):
            st = Steps(act, act_st)
            act.wait_ge(in_loaded, 16 * NIN)
            act.activation(tg[:], gates[:], ACT.Tanh).then_inc(tg_made, 1)

            def yT(p, v, c):
                for d in range(DK):
                    bk = RA.get(act, p, "yT", c, d)
                    o = v["yT"][:, d, :] if p % 2 == 0 else v["yT"][:, d, c * CH:(c + 1) * CH]
                    act.activation(o, bk[:], ACT.Copy).then_inc(RA.read, 1)

            def probabilities(p, v, c, g):
                n = c * v["G"] + g
                if n >= 2:
                    pc, pg = divmod(n - 2, v["G"])
                    if v["hd"] == 16:
                        act.wait_ge(RC.filled, RC.n(p, "av", pc, pg))
                    else:
                        act.wait_ge(RB.filled, RB.n(p, "av", pc, pg, TPC - 1))
                for j in range(5):
                    bk = RC.get(act, p, "s", c, g, j)
                    act.activation(v["PT"][:, n % 2, j, :], bk[:], ACT.Exp, scale=float(v["hd"]) ** -0.5).then_inc(RC.read, 1)

            def attention16(p, L):
                v = ph[p]
                MT, G = v["MT"], v["G"]
                if L == 0:
                    for b in range(B):
                        bk = RA.get(act, p, "ctx", b)
                        act.activation(ctxT[:, 0, b * M:(b + 1) * M], bk[:, 0:M], ACT.Copy)
                        act.activation(ctxT[0:CD - P, 1, b * M:(b + 1) * M], bk[0:CD - P, 160:160 + M], ACT.Copy)\
                           .then_inc(RA.read, 1)
                if L == 2:
                    act.wait_ge(w_loaded[p], 16 * len(loads[p]))
                for what, c, *i in steps16(L):
                    s = c % 2
                    if what == "keys" and L == 3:
                        act.wait_ge(kn_clear, 1)
                        for n in range(4):
                            rows = P if n % 2 == 0 else MR
                            act.wait_ge(RB.read, RB.n(p, "kp", n // 2, n % 2))
                            if n:
                                st.wait()
                            st.did(act.activation(v["junk"][0:rows], v["Kp"][0:rows, n, :], ACT.Square,
                                                  accum_out=v["ss"][0:rows, NT + n:NT + n + 1]))
                        st.wait()
                        act.sem_inc(kss_made, 1)
                    if what == "proj":
                        yT(p, v, c)
                        if L == 3:
                            act.wait_ge(RB.read, RB.n(p, "qp", c, 1))
                            for i in range(TPC):
                                t = TPC * c + i
                                st.wait()
                                st.did(act.activation(v["junk"][:], v["Y"][:, t, :], ACT.Square, accum_out=v["ss"][:, t:t + 1]))
                            st.wait()
                            act.sem_inc(qss_made, 1)
                    if what == ("turn" if L == 3 else "proj"):
                        if c >= 2:
                            act.wait_ge(qp_stored[s], 16 * (2 * LA[L] + 1))
                        for m in range(MT):
                            bk = RA.get(act, p, "q", c, m)
                            for o in (v["qp"][:, s, 0, m, :], v["qf"][:, s, m, :]):
                                if L == 2:
                                    ins = act.activation(o, bk[:], ACT.Identity, bias=v["bq"][:, m:m + 1])
                                else:
                                    ins = act.activation(o, bk[:], ACT.Copy)
                            ins.then_inc(RA.read, 1)
                    if what == "scores":
                        probabilities(p, v, c, i[0])
                    if what == "av":
                        n = c * G + i[0]
                        if n >= 2:
                            act.wait_ge(RB.filled, RB.n(p, "norm", *divmod(n - 2, G)))
                        bk = RC.get(act, p, "av", c, i[0])
                        act.activation(v["av"][:, i[0] % 2, :], bk[:], ACT.Copy).then_inc(RC.read, 1)
                    if what == "turn back":
                        for m in range(MT):
                            bk = RA.get(act, p, "oT", c, m)
                            act.activation(v["oT"][:, m, :], bk[:], ACT.Copy).then_inc(RA.read, 1)

            def attention(p, L):
                v = ph[p]
                MT = v["MT"]
                for what, c in ATT:
                    cs = slice(c * CH, (c + 1) * CH)
                    if what == "front":
                        yT(p, v, c)
                    if what == "back":
                        for g in range(v["G"]):
                            probabilities(p, v, c, g)
                        continue
                    for m in range(MT):
                        bk = RA.get(act, p, "q" if what == "front" else "oT", c, m)
                        act.activation(v["QT"][:, m, cs], bk[:], ACT.Copy).then_inc(RA.read, 1)

            def coupling(p):
                v = ph[p]
                act.wait_ge(w_loaded[p], 16 * len(loads[p]))
                for c in range(NC):
                    yT(p, v, c)
                for r in range(3):
                    for c in range(NC):
                        for m in range(DK):
                            bk = RC.get(act, p, r, "l1", c, m)
                            act.activation(v["h1"][:, m, c * CH:(c + 1) * CH], bk[:], ACT.Gelu, bias=v["b1"][:, m:m + 1])\
                               .then_inc(RC.read, 1)
                    if r == 0:
                        bk = RA.get(act, p, "g1")
                        act.activation(v["gh1"][:], bk[:, 0:B], ACT.Gelu, bias=v["gb1"][:]).then_inc(RA.read, 1)
                    for c in range(NC):
                        bk = RC.get(act, p, r, "l2", c)
                        act.activation(v["h2"][:, c * CH:(c + 1) * CH], bk[:], ACT.Gelu, bias=v["b2"][:]).then_inc(RC.read, 1)
                    if r == 0:
                        bk = RA.get(act, p, "g2")
                        act.activation(v["gh2"][0:64], bk[0:64, 0:B], ACT.Gelu, bias=v["gb2"][0:64]).then_inc(RA.read, 1)
                    for c in range(NC):
                        bk = RC.get(act, p, r, "l3", c)
                        act.activation(v["h3"][0:64, c * CH:(c + 1) * CH], bk[0:64, :], ACT.Gelu, bias=v["b3"][0:64])\
                           .then_inc(RC.read, 1)
                    if r == 0:
                        bk = RA.get(act, p, "g3")
                        act.activation(v["gt"][:], bk[:, 0:B], ACT.Tanh, bias=v["hb"][:, 1:2], scale=0.5).then_inc(RA.read, 1)
                    for c in range(NC):
                        bk = RC.get(act, p, r, "l4", c)
                        act.activation(v["th"][:, c, :], bk[:], ACT.Tanh, bias=v["hb"][:, 0:1], scale=0.5).then_inc(RC.read, 1)

            def quantised(p):
                v = ph[p]
                for d in range(DK):
                    bk = RA.get(act, p, "w1T", d)
                    act.activation(v["w1T"][:, d, :], bk[:].bitcast(BF16), ACT.Copy).then_inc(RA.read, 1)
                for d in range(DK):
                    bk = RA.get(act, p, "w2T", d)
                    act.activation(v["w2T"][:, :, d * P:(d + 1) * P],
                                   bk[:].bitcast(BF16).rearrange("p (f j) -> p f j", j=P), ACT.Copy).then_inc(RA.read, 1)
                for n in range(NC + 1):
                    if n < NC:
                        bk = RA.get(act, p, "xT", n)
                        act.activation(v["xT"][:, :, n * CH:(n + 1) * CH],
                                       bk[:].bitcast(BF16).rearrange("p (d j) -> p d j", d=DK), ACT.Copy).then_inc(RA.read, 1)
                    if n == 1:
                        act.wait_ge(hscale_made, 1)
                    for f in range(FT1 if n else 0):
                        c = n - 1
                        bk = RC.get(act, p, "up", c, f)
                        act.activation(v["h"][:, f, c * CH:(c + 1) * CH], bk[:], ACT.Relu,
                                       bias=v["bq1"][:, f:f + 1], scale=v["sb1"][:, f:f + 1]).then_inc(RC.read, 1)
                act.wait_ge(hs_ready, 1)
                for c in range(1, NC):
                    a = v["h"][:, :, c * CH:(c + 1) * CH]
                    act.activation(a, a, ACT.Identity, bias=v["rnd"][:], scale=v["sc"][:, 7:8]).then_inc(hs_made, 1)

            def logits(p, v, c, E):
                bk = RA.get(act, p, "lgT", c)
                act.activation(v["GT"][0:E, c * CH:(c + 1) * CH], bk[0:E, :], ACT.Copy).then_inc(RA.read, 1)

            def tiled_experts(p):
                v = ph[p]
                act.wait_ge(w_loaded[p], 16 * len(loads[p]))
                for c in range(NC):
                    yT(p, v, c)
                    logits(p, v, c, E2)
                act.wait_ge(ex_ready, 1)
                act.activation(v["r"][:, 1, :], v["r"][:, 0, :], ACT.Exp).then_inc(ex_made, 1)
                for c in range(NC):
                    bk = RA.get(act, p, "gT", c)
                    act.activation(v["GT"][0:E2, c * CH:(c + 1) * CH], bk[0:E2, :], ACT.Copy).then_inc(RA.read, 1)
                for what, i in tile_steps():
                    if what == "in":
                        bk = RA.get(act, p, "in", i)
                        act.activation(v["xeT"][:, i % 2, :], bk[:, 0:D], ACT.Copy).then_inc(RA.read, 1)
                    elif what == "turn":
                        bk = RA.get(act, p, "turn", i)
                        act.activation(v["hT"][:, i % 2], bk[:].rearrange("p (m t) -> p m t", t=P), ACT.Relu).then_inc(RA.read, 1)
                    elif what == "down":
                        if i >= 3:
                            act.wait_ge(yt_stored[i % 3], 16 * (i // 3))
                        bk = RC.get(act, p, "down", i)
                        act.activation(v["ye"][:, i % 3, :], bk[:, 0:D], ACT.Copy).then_inc(RC.read, 1)

            def routed_experts(p):
                v = ph[p]
                for c in range(NC + 1):
                    if c < NC:
                        yT(p, v, c)
                        logits(p, v, c, E3)
                    if c:
                        ts = slice(TPC * (c - 1), TPC * c)
                        act.wait_ge(ex_ready, 1 + c)
                        act.activation(v["pre"][:, ts, :], v["lg"][:, ts, :], ACT.Exp).then_inc(ex_made, 1)
                items = [(E3, c, m) for c in SHARED[0] for m in range(3)] + \
                    [(e, 0, m) for e in range(E3) for m in range(3)] + [(E3, c, m) for c in SHARED[1] for m in range(3)]

                def silu(n, width):
                    e, c, m = items[n]
                    fn = F3T[m]
                    if n >= 4:
                        act.wait_ge(RB.read, RB.n(p, "up", *items[n - 4]))
                    bk = RA.get(act, p, "gate", e, c, m)
                    act.activation(v["sg"][0:fn, n % 4, 0:width], bk[0:fn, 0:width], ACT.Silu).then_inc(RA.read, 1)

                for n in range(3 * 2):
                    silu(n, CH)

                def tokens_of(e):
                    for d in range(DK):
                        bk = RA.get(act, p, "xeT", e, d)
                        act.activation(v["xeT"][:, e % 2 * DK + d, :], bk[:, 0:CAP], ACT.Copy).then_inc(RA.read, 1)

                tokens_of(0)
                for e in range(E3):
                    for m in range(3):
                        silu(3 * 2 + 3 * e + m, CAP)
                    if e + 1 < E3:
                        tokens_of(e + 1)
                    if e >= 3:
                        act.wait_ge(ye_stored[e % 3], 16 * 2 * (e // 3))
                    bk = RC.get(act, p, "dn", e, 0)
                    act.activation(v["ye"][:, e % 3, 0:2, :], bk[:].rearrange("p (t d) -> p t d", t=2), ACT.Copy)\
                       .then_inc(RC.read, 1)
                    n = CAP - 2 * P
                    bk = RC.get(act, p, "dn", e, 1)
                    act.activation(v["ye"][0:n, e % 3, 2, :], bk[0:n, 0:D], ACT.Copy).then_inc(RC.read, 1)
                for n in range(3 * 2 + 3 * E3, len(items)):
                    silu(n, CH)

            for p in range(NPH):
                L = p // 2
                if p:
                    act.wait_ge(phase_over, p)
                if p % 2 == 0:
                    (attention if L == 1 else attention16)(p, L)
                elif L == 0:
                    coupling(p)
                elif L == 1:
                    quantised(p)
                elif L == 2:
                    tiled_experts(p)
                else:
                    routed_experts(p)

        @block.gpsimd
        def _(pool):
            st = Steps(pool, pool_st)
            for a in (ident, identb, sel, selr):
                st.did(pool.memset(a[:], 0.0))
            for a in (hmask, before, ones, sgn):
                st.did(pool.memset(a[:], 1.0))
            st.did(pool.memset(nhalf[:], -0.5))
            pool.memset(zeros[:], 0.0).then_inc(zero_made, 1)
            st.did(pool.memset(onesb[:], 1.0))
            st.wait()
            for a in (ident, identb):
                st.did(pool.affine_select(out=a[:], in_=a[:], compare_op=ALU.not_equal, fill=1.0, base=0,
                                          pattern=[[-1, P]], channel_multiplier=1))
            st.did(pool.affine_select(out=before[:], in_=before[:], compare_op=ALU.is_gt, fill=0.0, base=0,
                                      pattern=[[1, P]], channel_multiplier=-1))
            st.did(pool.affine_select(out=sgn[:], in_=sgn[:], compare_op=ALU.is_gt, fill=-1.0, base=64,
                                      pattern=[[0, 1]], channel_multiplier=-1))
            st.wait()
            st.did(pool.affine_select(out=hmask[:], in_=hmask[:], compare_op=ALU.is_ge, fill=0.0, base=0,
                                      pattern=[[-64, 2]], channel_multiplier=1))
            st.wait()
            st.did(pool.affine_select(out=hmask[:], in_=hmask[:], compare_op=ALU.is_ge, fill=0.0, base=63,
                                      pattern=[[64, 2]], channel_multiplier=-1))
            for base in (0, -32):
                st.wait()
                st.did(pool.affine_select(out=sel[:], in_=sel[:], compare_op=ALU.not_equal, fill=1.0, base=base,
                                          pattern=[[-1, 16], [0, P]], channel_multiplier=1))
                a = selr[:, :, :, 0:MR]
                st.did(pool.affine_select(out=a, in_=a, compare_op=ALU.not_equal, fill=1.0, base=base,
                                          pattern=[[-4, 4], [-1, 4], [0, MR]], channel_multiplier=1))
            st.did(pool.iota(iota[:], [[1, NTL]], base=0, channel_multiplier=0, allow_small_or_imprecise_dtypes=True))
            st.wait()
            pool.sem_inc(consts, NCONST)

            def norm(p, chunks=range(NC)):
                for c in chunks:
                    ts = slice(TPC * c, TPC * (c + 1))
                    pool.wait_ge(ln_stats, lnorm(p, c))
                    rsqrt(rstd[:, ts], mv[:, ts, 1], True)
                    pool.sem_inc(ln_rstd, 1)

            def add_row(row, made, n, p):
                pool.wait_ge(ln_y, lnorm(p, NC - 1))
                pool.wait_ge(made, n)
                for c in range(NC):
                    a = X[:, TPC * c:TPC * (c + 1), :]
                    last = pool.tensor_tensor(a, a, bc(row.unsqueeze(1), (P, TPC, D)), ALU.add)
                last.then_inc(xbias, 1)

            def clear(p, L):
                v = ph[p]
                hd, vw = v["hd"], v["vw"]
                if hd == 64:
                    st.did(pool.memset(v["Kr"][:], 0.0))
                st.did(pool.memset(v["V"][:], 1.0))
                st.did(pool.memset(v["Vr"][:], 0.0))
                if L < 3:
                    st.did(pool.memset(v["negm"][:], 0.0))
                for j in range(4):
                    st.wait()
                    st.did(pool.memset(v["Vr"][32 * j:32 * j + MR, :, :, j, hd:vw], 1.0))
                st.wait()
                pool.sem_inc(kv_clear, 1)

            def rsqrt(o, a, add):
                n = o.shape[-1]
                st.did(pool.tensor_scalar(o, a, 1e-5, None, ALU.add) if add else pool.tensor_scalar(o, a, 1e-24, None, ALU.max))
                st.wait()
                st.did(pool.tensor_tensor(o, o, nhalf[:, 0:n], ALU.pow))
                st.wait()

            def attention16(p, L):
                v = ph[p]
                MT = v["MT"]
                if L == 3:
                    pool.memset(v["ss"][:], 1.0).then_inc(kn_clear, 1)
                norm(p, range(0, 2))
                if L < 3:
                    clear(p, L)
                for what, c, *i in steps16(L):
                    ts = slice(TPC * c, TPC * (c + 1))
                    if what == "keys" and L == 3:
                        pool.wait_ge(kss_made, 1)
                        rsqrt(v["rs"][:, NT:NT + 4], v["ss"][:, NT:NT + 4], False)
                        pool.sem_inc(krs_made, 1)
                        clear(p, L)
                    elif what == "proj" and L == 3:
                        pool.wait_ge(qss_made, c + 1)
                        rsqrt(v["rs"][:, ts], v["ss"][:, ts], False)
                        pool.sem_inc(qrs_made, 1)
                    elif what == "unit" and L == 3:
                        pool.wait_ge(qn_made, c + 1)
                        a = v["Y"][:, ts, :]
                        pool.tensor_tensor(a, a, bc(v["bo"][:].unsqueeze(1), (P, TPC, D)), ALU.add).then_inc(qbo_made, 1)
                    elif what == "rest":
                        norm(p, range(2, NC))
                    elif what == "turn" and c >= FIRST[L]:
                        split(pool, st, p, v, c, qp_made)
                    elif what == "scores" and L and (c, i[0]) == (0, 0):
                        add_row((v["gb"] if L == 3 else v["gbo"])[:], gbo_made, L, p)
                    elif what == "tail" and L == 3:
                        pool.wait_ge(post_stats, c + 1)
                        rsqrt(rstd[:, ts], mv[:, ts, 1], True)
                        pool.sem_inc(post_z, 1)

            def attention(p, L):
                v = ph[p]
                norm(p)
                clear(p, L)
                for n in range(v["MT"] * B):
                    pool.wait_ge(kz_made, n + 1)
                    pool.tensor_copy(v["Kr"][:, n, :, 0:MR], v["Kz"][:, n, :, P:M]).then_inc(kr_made, 1)
                add_row(v["gbo"][:], gbo_made, L, p)

            for p in range(NPH):
                L = p // 2
                v = ph[p]
                if p:
                    pool.wait_ge(phase_over, p)
                if p % 2 == 0:
                    (attention if L == 1 else attention16)(p, L)
                    continue
                norm(p)
                if L == 1:
                    for n in range(2):
                        pool.wait_ge(xmax_made, n + 1)
                        pool.partition_all_reduce(v["sc"][:, n:n + 1], v["m"][:, 60 + n:61 + n], P, RMAX).then_inc(xall_made, 1)
                    add_row(v["rowB"][:], rows_made, 1, p)
                if L < 2:
                    continue
                if L == 3:
                    pool.iota(v["dump"][:], [[2 * P, NT], [1, 2]], base=E3 * CAP, channel_multiplier=2,
                              allow_small_or_imprecise_dtypes=True).then_inc(dumps_made, 1)
                pool.wait_ge(idx_made, L - 1)
                pool.wait_ge(slots_clear, 16)
                pool.wait_ge(ln_y, lnorm(p, NC - 1))
                for t in range(NT):
                    for k in range(2):
                        i = 2 * t + k
                        pool.indirect_dma_start(x_slots, bass.IndirectOffsetOnAxis(ap=v["sidx"][:, i:i + 1], axis=0),
                                                v["Y"][:, t, :], None).then_inc(scattered, 16)
                for i in range(3):
                    if L == 2:
                        pool.wait_ge(yt_stored[i], 16 * len(range(i, NTL, 3)))
                    else:
                        pool.wait_ge(ye_stored[i], 16 * 2 * len(range(i, E3, 3)))
                pool.wait_ge(scattered, 16 * 2 * NT * (L - 1))
                for t in range(NT):
                    for k in range(2):
                        i = 2 * t + k
                        dst = (v["Y"] if k == 0 else v["yk"])[:, t, :]
                        pool.indirect_dma_start(dst, None, y_slots[0:NTL * P if L == 2 else E3 * CAP, :],
                                                bass.IndirectOffsetOnAxis(ap=v["gidx"][:, i:i + 1], axis=0))\
                            .then_inc(gathered[t // 2], 16)

        @block.vector
        def _(dve):
            st = Steps(dve, dve_st)
            dve.wait_ge(in_loaded, 16 * NIN)
            dve.wait_ge(tg_made, 1)
            dve.wait_ge(consts, NCONST)

            def x_norm(p, chunks=range(NC)):
                for c in range(chunks.start, chunks.stop + 1):
                    if c < chunks.stop:
                        for t in range(TPC * c, TPC * (c + 1)):
                            st.did(dve.bn_stats(stats[:, t, :], X[:, t, :]))
                        st.wait()
                        for t in range(TPC * c, TPC * (c + 1)):
                            last = dve.bn_aggr(mv[:, t, :], stats[:, t, :])
                        last.then_inc(ln_stats, 1)
                    if c > chunks.start:
                        dve.wait_ge(ln_rstd, lnorm(p, c - 1))
                        for t in range(TPC * (c - 1), TPC * c):
                            last = dve.tensor_scalar(ph[p]["Y"][:, t, :], X[:, t, :], mv[:, t, 0:1], rstd[:, t:t + 1],
                                                     ALU.subtract, ALU.mult)
                        last.then_inc(ln_y, 1)

            def add_out(bk, q, scalar):
                a = X[:, 2 * q:2 * q + 2, :]
                return dve.scalar_tensor_tensor(a, bk[:].rearrange("p (t d) -> p t d", t=2), scalar, a, ALU.mult, ALU.add)

            def over(p):
                dve.wait_ge(RB.read, RB.emptied)
                dve.sem_inc(phase_over, 1)

            def prepare(p, L, v):
                dve.wait_ge(w_loaded[p], 16 * len(loads[p]))
                if L in (1, 2):
                    dve.tensor_scalar(v["gbo"][:], v["bo"][:], tg[:, L:L + 1], None, ALU.mult).then_inc(gbo_made, 1)
                if L == 3:
                    st.did(dve.tensor_scalar(v["lg"][:], v["lg"][:], tg[:, L:L + 1], None, ALU.mult))
                    dve.tensor_scalar(v["gb"][:], v["lb"][:], tg[:, L:L + 1], None, ALU.mult).then_inc(gbo_made, 1)
                x_norm(p, range(0, 2) if L != 1 else range(NC))

            def values(p, L, v):
                hd, HD = v["hd"], v["HD"]
                dve.wait_ge(kv_clear, L + 1)
                for b in range(B):
                    bk = RB.get(dve, p, "v", b, 0)
                    a = bk[:, 0:HD].rearrange("p (h d) -> p h d", d=hd)
                    o = v["V"][:, b, :, 0:hd]
                    if L >= 2:
                        ins = dve.tensor_tensor(o, a, v["bv"][:].rearrange("p (h d) -> p h d", d=hd), ALU.add)
                    else:
                        ins = dve.tensor_copy(o, a)
                    st.did(ins)
                    st.wait()
                    dve.sem_inc(RB.read, 1)
                    dve.sem_inc(v_made, 1)
                    bk = RB.get(dve, p, "v", b, 1)
                    a = bk[0:MR, 0:HD].rearrange("p (g j d) -> p g j d", j=4, d=hd)
                    for j in range(4):
                        o = v["Vr"][32 * j:32 * j + MR, b, :, j, 0:hd]
                        if L >= 2:
                            bv = v["bv"][0:MR].rearrange("p (g j d) -> p g j d", j=4, d=hd)[:, :, j, :]
                            ins = dve.tensor_tensor(o, a[:, :, j, :], bv, ALU.add)
                        else:
                            ins = dve.tensor_copy(o, a[:, :, j, :])
                        st.did(ins)
                    st.wait()
                    dve.sem_inc(RB.read, 1)
                    dve.sem_inc(v_made, 1)

            def negated_maxima(p, v, c):
                H = v["H"]
                bk = RB.get(dve, p, "mx", c)
                st.did(dve.tensor_scalar(v["negm"][0:H, c, :], bk[0:H, :], -1.0, None, ALU.mult))
                st.wait()
                dve.scalar_tensor_tensor(v["negm"][32:32 + H, c, :], bk[0:H, :], -1.0, v["negm"][0:H, c, :],
                                         ALU.mult, ALU.subtract).then_inc(RB.read, 1)

            def attention16(p, L):
                v = ph[p]
                H, MT, G, HD = (v[k] for k in ("H", "MT", "G", "HD"))
                prepare(p, L, v)
                if L == 0:
                    st.did(dve.tensor_copy(v["m01"][:], v["m8"][:]))
                st.did(dve.memset(v["kf"][:], 0.0))
                st.wait()

                def mask_row():
                    r0 = 16 * NPAIR
                    st.did(dve.memset(v["mb"][r0:r0 + 1], 0.0))
                    st.wait()
                    st.did(dve.tensor_scalar(v["mb"][r0:r0 + 1].rearrange("p (b k) -> p b k", k=MP)[:, :, 0:M],
                                             v["m8"][r0:r0 + 1].rearrange("p (b k) -> p b k", k=M), -1.0, BIG,
                                             ALU.add, ALU.mult))
                    st.wait()
                    dve.tensor_copy(v["Ks"][r0:r0 + 1, :, :], bc(v["mb"][r0:r0 + 1].unsqueeze(1), (1, H, B * MP)))\
                       .then_inc(mb_made, 1)

                def key_parts():
                    for m in range(MT):
                        bk = RB.get(dve, p, "k", m)
                        o = v["kf"][:, m, :].rearrange("p (b k) -> p b k", k=MP)[:, :, 0:M]
                        a = bk[:, 0:B * M].rearrange("p (b k) -> p b k", k=M)
                        if L == 2:
                            ins = dve.tensor_scalar(o, a, v["bk"][:, m:m + 1], None, ALU.add)
                        elif L == 0:
                            ins = dve.tensor_tensor(o, a, v["m01"][:].rearrange("p (b k) -> p b k", k=M), ALU.mult)
                        else:
                            ins = dve.tensor_copy(o, a)
                        ins.then_inc(RB.read, 1)
                    dve.wait_ge(RB.read, RB.emptied)
                    k, parts = v["kf"][:], v["kp"]
                    st.did(dve.tensor_copy(parts[:, 0], k))
                    st.wait()
                    st.did(dve.tensor_tensor(k, k, parts[:, 0], ALU.subtract))
                    st.wait()
                    st.did(dve.tensor_copy(parts[:, 1], k))
                    st.wait()
                    dve.tensor_tensor(parts[:, 2], k, parts[:, 1], ALU.subtract).then_inc(kp_made, 1)

                for what, c, *i in steps16(L):
                    i = i[0] if i else None
                    if what == "keys":
                        if L < 3:
                            key_parts()
                        else:
                            for b in range(B):
                                for s in range(2):
                                    n = P if s == 0 else MR
                                    bk = RB.get(dve, p, "kp", b, s)
                                    dve.tensor_tensor(v["Kp"][0:n, 2 * b + s, :], bk[0:n, 0:HD], v["bk"][0:n], ALU.add)\
                                       .then_inc(RB.read, 1)
                    elif what == "keys turned":
                        key_parts()
                    elif what == "rest":
                        x_norm(p, range(2, NC))
                        if L == 0:
                            mask_row()
                    elif what == "values":
                        values(p, L, v)
                    elif what == "proj" and L == 3:
                        for q in range(2):
                            bk = RB.get(dve, p, "qp", c, q)
                            t = (2 * c + q) * 2
                            dve.tensor_tensor(v["Y"][:, t:t + 2, :], bk[:].rearrange("p (t d) -> p t d", t=2),
                                              bc(v["bq"][:].unsqueeze(1), (P, 2, D)), ALU.add).then_inc(RB.read, 1)
                    elif what == "unit keys":
                        dve.wait_ge(krs_made, 1)
                        for n in range(4):
                            rows = P if n % 2 == 0 else MR
                            a = v["Kp"][0:rows, n, :]
                            st.did(dve.tensor_scalar(a, a, v["rs"][0:rows, NT + n:NT + n + 1], None, ALU.mult))
                        st.wait()
                        dve.sem_inc(kn_made, 1)
                    elif what == "unit" and L == 3:
                        dve.wait_ge(qrs_made, c + 1)
                        if c == 0:
                            dve.wait_ge(RB.filled, RB.n(p, "k", MT - 1))
                        if c >= 2:
                            dve.wait_ge(RA.filled, RA.n(p, "q", c - 2, MT - 1))
                        for j in range(TPC):
                            t = TPC * c + j
                            last = dve.tensor_scalar(v["Qn"][c % 2][:, j, :], v["Y"][:, t, :], v["rs"][:, t:t + 1], None, ALU.mult)
                        last.then_inc(qn_made, 1)
                    elif what == "turn" and c < FIRST[L]:
                        split(dve, st, p, v, c, qp0_made)
                    elif what == "max":
                        for h0 in range(0, H, 3):
                            hn = min(3, H - h0)
                            bk = RB.get(dve, p, "mxs", c, i, h0)
                            dve.tensor_reduce(v["mx"][:, TPC * c + i, h0:h0 + hn],
                                              bk[:, 0:hn * M].rearrange("p (h k) -> p h k", k=M), AX.X, ALU.max)\
                               .then_inc(RB.read, 1)
                    elif what == "negm":
                        negated_maxima(p, v, c)
                    elif what == "norm":
                        bk = RB.get(dve, p, "norm", c, i)
                        a = bk[:].rearrange("p (q j d) -> p q j d", j=4, d=32)
                        w = v["rden"][:, i % 2, :].rearrange("p (q j) -> p q j", j=4)
                        st.did(dve.reciprocal(w, a[:, :, :, 16]))
                        st.wait()
                        o = v["O"][:, :, 64 * i:64 * (i + 1)].rearrange("p q (j d) -> p q j d", j=4)
                        dve.tensor_tensor(o, a[:, :, :, 0:16], bc(w.unsqueeze(3), (P, TPC, 4, 16)), ALU.mult)\
                           .then_inc(RB.read, 1)
                    elif what == "tail":
                        if L and c == 0:
                            dve.wait_ge(xbias, XB[p])
                        if L < 3:
                            for q in range(2):
                                bk = RB.get(dve, p, "out", c, q)
                                add_out(bk, 2 * c + q, tg[:, L:L + 1]).then_inc(RB.read, 1)
                            continue
                        dve.wait_ge(qbo_made, c + 1)
                        for q in range(2):
                            bk = RB.get(dve, p, "out", c, q)
                            a = v["Y"][:, (2 * c + q) * 2:(2 * c + q) * 2 + 2, :]
                            dve.tensor_tensor(a, bk[:].rearrange("p (t d) -> p t d", t=2), a, ALU.add).then_inc(RB.read, 1)
                        dve.wait_ge(RB.read, RB.emptied)
                        for t in range(TPC * c, TPC * (c + 1)):
                            st.did(dve.bn_stats(stats[:, t, :], v["Y"][:, t, :]))
                        st.wait()
                        for t in range(TPC * c, TPC * (c + 1)):
                            last = dve.bn_aggr(mv[:, t, :], stats[:, t, :])
                        last.then_inc(post_stats, 1)
                        dve.wait_ge(post_z, c + 1)
                        for t in range(TPC * c, TPC * (c + 1)):
                            st.did(dve.tensor_scalar(v["Y"][:, t, :], v["Y"][:, t, :], mv[:, t, 0:1], rstd[:, t:t + 1],
                                                     ALU.subtract, ALU.mult))
                        st.wait()
                        z = v["Y"][:, TPC * c:TPC * (c + 1), :]
                        xx = X[:, TPC * c:TPC * (c + 1), :]
                        st.did(dve.tensor_tensor(z, z, bc(v["lg"][:].unsqueeze(1), (P, TPC, D)), ALU.mult))
                        st.wait()
                        st.did(dve.tensor_tensor(xx, xx, z, ALU.add))
                if L == 3:
                    st.wait()
                over(p)

            def attention(p, L):
                v = ph[p]
                hd, MT, hpm, G = (v[k] for k in ("hd", "MT", "hpm", "G"))
                prepare(p, L, v)
                for m in range(MT):
                    bk = RB.get(dve, p, "k", m)
                    dve.tensor_copy(v["KTs"][:, m, :], bk[:, 0:B * M]).then_inc(RB.read, 1)
                    dve.wait_ge(RB.read, RB.emptied)
                    for b in range(B):
                        dve.tensor_tensor(v["Kz"][:, m * B + b, :, :],
                                          bc(v["KTs"][:, m, b * M:(b + 1) * M].unsqueeze(1), (P, hpm, M)),
                                          bc(hmask[:].unsqueeze(2), (P, hpm, M)), ALU.mult).then_inc(kz_made, 1)
                values(p, L, v)
                for what, c in ATT:
                    if what == "front":
                        for i in range(TPC):
                            for m in range(MT):
                                bk = RB.get(dve, p, "mxs", c, i, m)
                                dve.tensor_reduce(v["mx"][:, TPC * c + i, m * hpm:(m + 1) * hpm],
                                                  bk[:, 0:hpm * M].rearrange("p (h k) -> p h k", k=M), AX.X, ALU.max)\
                                   .then_inc(RB.read, 1)
                    elif what == "back":
                        negated_maxima(p, v, c)
                        for g in range(G):
                            for i in range(TPC):
                                bk = RB.get(dve, p, "av", c, g, i)
                                a = bk[:, 0:4 * (hd + 1)].rearrange("p (j d) -> p j d", j=4)
                                r = v["rden"][:, i % 2, 0:4]
                                st.did(dve.reciprocal(r, a[:, :, hd]))
                                st.wait()
                                o = v["O"][:, c % 2, i, g * 4 * hd:(g + 1) * 4 * hd].rearrange("p (j d) -> p j d", j=4)
                                dve.tensor_tensor(o, a[:, :, 0:hd], bc(r.unsqueeze(2), (P, 4, hd)), ALU.mult)\
                                   .then_inc(RB.read, 1)
                    else:
                        if c == 0:
                            dve.wait_ge(xbias, XB[p])
                        for q in range(2):
                            bk = RB.get(dve, p, "out", c, q)
                            add_out(bk, 2 * c + q, tg[:, L:L + 1]).then_inc(RB.read, 1)
                        if c == 1 and p + 1 < NPH:
                            round_weights(p + 1)
                over(p)

            def coupling(p):
                v = ph[p]
                x_norm(p)
                dve.wait_ge(w_loaded[p], 16 * len(loads[p]))
                st.did(dve.memset(v["w4r"][64:P], 0.0))
                st.did(dve.memset(v["h3"][64:P], 0.0))
                st.did(dve.tensor_copy(v["w4r"][0:64], bc(v["w4"][0:64], (64, P))))
                st.did(dve.tensor_copy(v["g3r"][0:64], bc(v["g3"][0:64], (64, P))))
                st.did(dve.tensor_scalar(v["hb"][:, 0:1], v["b4"][:], 0.5, None, ALU.mult))
                st.did(dve.tensor_scalar(v["hb"][:, 1:2], v["gb3"][:], 0.5, None, ALU.mult))
                for c in range(NC):
                    for d in range(DK):
                        dve.wait_ge(RA.read, RA.n(p, "yT", c, d))
                        st.did(dve.tensor_reduce(v["msum"][:, d, c:c + 1], v["yT"][:, d, c * CH:(c + 1) * CH], AX.X, ALU.add))
                st.wait()
                for b in range(B):
                    st.did(dve.tensor_tensor(v["mean"][:, :, b], v["msum"][:, :, CPB * b], v["msum"][:, :, CPB * b + 1], ALU.add))
                st.wait()
                a = v["mean"][:].rearrange("p k b -> p (k b)")
                dve.tensor_scalar(a, a, 1.0 / S, None, ALU.mult).then_inc(gc_ready, 1)
                dve.wait_ge(RA.read, RA.n(p, "g3"))
                st.did(dve.tensor_scalar(v["al"][:], v["ar"][:], 0.3, sgn[:, 0:1], ALU.mult, ALU.mult))
                st.did(dve.tensor_scalar(v["be"][:], v["gt"][:], v["ar"][:, 0:1], 0.7, ALU.mult, ALU.mult))
                st.wait()
                st.did(dve.tensor_scalar(v["be"][:], v["be"][:], 0.1, sgn[:, 0:1], ALU.add, ALU.mult))
                st.wait()
                s2 = [v["yT"], v["yS"]]
                for r in range(3):
                    old, new = s2[r % 2], s2[(r + 1) % 2]
                    for c in range(NC):
                        cs = slice(c * CH, (c + 1) * CH)
                        b = c // CPB
                        dve.wait_ge(RC.read, RC.n(p, r, "l4", c))
                        k, w = v["tmp"][:, 0, :], v["tmp"][:, 1, :]
                        st.did(dve.tensor_scalar(k, v["th"][:, c, :], v["al"][:, 0:1], v["be"][:, b:b + 1], ALU.mult, ALU.add))
                        st.wait()
                        st.did(dve.tensor_tensor(w, k, old[:, 1, cs], ALU.mult))
                        st.wait()
                        st.did(dve.tensor_tensor(new[:, 0, cs], w, old[:, 0, cs], ALU.add))
                        st.wait()
                        st.did(dve.tensor_tensor(w, k, old[:, 0, cs], ALU.mult))
                        st.wait()
                        dve.tensor_tensor(new[:, 1, cs], old[:, 1, cs], w, ALU.subtract).then_inc(state_made, 1)
                        dve.wait_ge(state_made, NC * r + c + 1)
                for c in range(NC):
                    for q in range(2):
                        bk = RB.get(dve, p, "fin", c, q)
                        add_out(bk, 2 * c + q, tg[:, 4:5]).then_inc(RB.read, 1)
                over(p)

            def round_weights(p):
                v = ph[p]
                dve.wait_ge(w_loaded[p], 16 * len(loads[p]))
                for w, n, sw, iw in (("w1", FT1, "sw1", "iw1"), ("w2", DK, "sw2", "iw2")):
                    st.did(dve.tensor_reduce(v[sw][:], v[w][:], AX.X, ALU.max, apply_absolute_value=True))
                    st.wait()
                    st.did(dve.tensor_scalar(v[sw][:], v[sw][:], 1e-8, 1.0 / 127.0, ALU.max, ALU.mult))
                    st.wait()
                    st.did(dve.reciprocal(v[iw][:], v[sw][:]))
                    st.wait()
                    for i in range(n):
                        st.did(dve.tensor_scalar(v[w][:, i, :], v[w][:, i, :], v[iw][:, i:i + 1], 127.0, ALU.mult, ALU.min))
                    st.wait()
                    st.did(dve.tensor_scalar(v[w][:], v[w][:], -128.0, ROUND, ALU.max, ALU.add))
                    st.wait()

            def quantised(p):
                v = ph[p]
                x_norm(p)
                for w, wi in (("w1", "wi1"), ("w2", "wi2")):
                    st.did(dve.tensor_scalar(v[wi][:], v[w][:], ROUND, None, ALU.subtract))
                st.wait()
                dve.sem_inc(wq_made, 1)
                for d in range(DK):
                    last = st.did(dve.tensor_scalar(v["diag"][:, d, :], ident[:], v["sw2"][:, d:d + 1], None, ALU.mult))
                st.wait()
                dve.sem_inc(diag_made, 1)
                bk = RB.get(dve, p, "sw2r")
                dve.tensor_copy(v["sw2r"][:], bk[:, 0:D]).then_inc(RB.read, 1)

                def scale(n):
                    st.wait()
                    dve.sem_inc(xmax_made, 1)
                    dve.wait_ge(xall_made, n + 1)
                    st.did(dve.tensor_scalar(v["sc"][:, 4 + n:5 + n], v["sc"][:, n:n + 1], 1e-8, 1.0 / 255.0, ALU.max, ALU.mult))
                    st.wait()
                    st.did(dve.reciprocal(v["sc"][:, 6 + n:7 + n], v["sc"][:, 4 + n:5 + n]))
                    st.wait()

                for c in range(NC):
                    dve.wait_ge(ln_y, lnorm(p, c))
                    st.did(dve.tensor_reduce(v["m"][:, c:c + 1], v["Y"][:, TPC * c:TPC * (c + 1), :], AX.XY, ALU.max))
                st.wait()
                st.did(dve.tensor_reduce(v["m"][:, 60:61], v["m"][:, 0:NC], AX.X, ALU.max))
                scale(0)
                st.did(dve.memset(v["rnd"][:], ROUND))
                st.did(dve.tensor_scalar(v["sb1"][:], v["sw1"][:], v["sc"][:, 4:5], None, ALU.mult))
                st.wait()
                st.did(dve.reciprocal(v["ib1"][:], v["sb1"][:]))
                st.wait()
                st.did(dve.tensor_tensor(v["bq1"][:], v["b1"][:], v["ib1"][:], ALU.mult))
                st.wait()
                st.did(dve.tensor_scalar(v["bq1"][:], v["bq1"][:], ROUND, ROUND, ALU.add, ALU.subtract))
                st.wait()
                dve.tensor_tensor(v["bq1"][:], v["bq1"][:], v["sb1"][:], ALU.mult).then_inc(hscale_made, 1)
                for c in range(NC):
                    a = v["Y"][:, TPC * c:TPC * (c + 1), :]
                    st.did(dve.tensor_scalar(a, a, v["sc"][:, 6:7], 255.0, ALU.mult, ALU.min))
                    st.wait()
                    st.did(dve.tensor_scalar(a, a, 0.0, ROUND, ALU.max, ALU.add))
                    st.wait()
                    dve.tensor_scalar(v["xi"][:, TPC * c:TPC * (c + 1), :], a, ROUND, None, ALU.subtract).then_inc(xi_made, 1)
                for c in range(NC):
                    for f in range(FT1):
                        dve.wait_ge(RC.read, RC.n(p, "up", c, f))
                        n = 8 + c * FT1 + f
                        st.did(dve.tensor_reduce(v["m"][:, n:n + 1], v["h"][:, f, c * CH:(c + 1) * CH], AX.X, ALU.max))
                st.wait()
                st.did(dve.tensor_reduce(v["m"][:, 61:62], v["m"][:, 8:8 + NC * FT1], AX.X, ALU.max))
                scale(1)
                dve.sem_inc(hs_ready, 1)
                dve.wait_ge(RB.read, RB.n(p, "sw2r"))
                st.did(dve.tensor_scalar(v["rowS"][:], v["sw2r"][:], v["sc"][:, 5:6], None, ALU.mult))
                st.wait()
                st.did(dve.reciprocal(v["rowI"][:], v["rowS"][:]))
                st.wait()
                st.did(dve.tensor_tensor(v["rowB"][:], v["b2"][:], v["rowI"][:], ALU.mult))
                st.wait()
                st.did(dve.tensor_scalar(v["rowB"][:], v["rowB"][:], ROUND, ROUND, ALU.add, ALU.subtract))
                st.wait()
                st.did(dve.tensor_tensor(v["rowB"][:], v["rowB"][:], v["rowS"][:], ALU.mult))
                st.wait()
                st.did(dve.tensor_scalar(v["rowB"][:], v["rowB"][:], tg[:, 5:6], None, ALU.mult))
                st.did(dve.tensor_scalar(v["rowT"][:], v["rowS"][:], tg[:, 5:6], None, ALU.mult))
                st.wait()
                dve.sem_inc(rows_made, 1)
                for c in range(NC):
                    a = v["h"][:, :, c * CH:(c + 1) * CH]
                    if c == 0:
                        st.did(dve.tensor_scalar(a, a, v["sc"][:, 7:8], ROUND, ALU.mult, ALU.add))
                        st.wait()
                    else:
                        dve.wait_ge(hs_made, c)
                    dve.tensor_scalar(v["hi"][:, :, c * CH:(c + 1) * CH], a, ROUND, 255.0, ALU.subtract, ALU.min)\
                       .then_inc(hi_made, 1)
                dve.wait_ge(xbias, XB[p])
                for c in range(NC):
                    for q in range(2):
                        bk = RB.get(dve, p, "dn", c, q)
                        o = v["dn"][:, q, :, :]
                        dve.tensor_tensor(o, bk[:].rearrange("p (t d) -> p t d", t=2),
                                          bc(v["rowT"][:].unsqueeze(1), (P, 2, D)), ALU.mult).then_inc(RB.read, 1)
                        dve.wait_ge(RB.read, RB.emptied)
                        a = X[:, (2 * c + q) * 2:(2 * c + q) * 2 + 2, :]
                        st.did(dve.tensor_tensor(a, a, o, ALU.add))
                st.wait()
                over(p)

            def experts(p, L):
                v = ph[p]
                E = E2 if L == 2 else E3
                r = v["r"]
                gate = tg[:, 4 + L:5 + L]
                x_norm(p)
                dve.wait_ge(w_loaded[p], 16 * len(loads[p]))
                st.did(dve.memset(v["ohs"][:, 0, :], 0.0))
                for c in range(NC):
                    ts = slice(TPC * c, TPC * (c + 1))
                    bk = RB.get(dve, p, "lg", c)
                    dve.tensor_tensor(v["lg"][:, ts, :], bk[:, 0:TPC * E].rearrange("p (t e) -> p t e", e=E),
                                      bc(v["br"][:].unsqueeze(1), (P, TPC, E)), ALU.add).then_inc(RB.read, 1)
                    dve.wait_ge(RB.read, RB.emptied)
                    if L == 3:
                        st.did(dve.tensor_reduce(r[:, 0, ts], v["lg"][:, ts, :], AX.X, ALU.max))
                        st.wait()
                        st.did(dve.tensor_tensor(v["lg"][:, ts, :], v["lg"][:, ts, :], bc(r[:, 0, ts].unsqueeze(2), (P, TPC, E)),
                                                 ALU.subtract))
                        st.wait()
                        dve.sem_inc(ex_ready, 1)
                        dve.wait_ge(ex_made, 2 + c)
                        st.did(dve.tensor_reduce(r[:, 0, ts], v["pre"][:, ts, :], AX.X, ALU.add))
                        st.wait()
                        st.did(dve.reciprocal(r[:, 1, ts], r[:, 0, ts]))
                        st.wait()
                        st.did(dve.tensor_tensor(v["lg"][:, ts, :], v["pre"][:, ts, :], bc(r[:, 1, ts].unsqueeze(2), (P, TPC, E)),
                                                 ALU.mult))
                        st.wait()
                    for t in range(TPC * c, TPC * (c + 1)):
                        st.did(dve.max(v["top"][:, t, :], v["lg"][:, t, :]))
                    st.wait()
                    for t in range(TPC * c, TPC * (c + 1)):
                        st.did(dve.max_index(v["idx"][:, t, :], v["top"][:, t, :], v["lg"][:, t, :]))
                    st.wait()
                    st.did(dve.tensor_copy(v["idf"][:, ts, 0:2], v["idx"][:, ts, 0:2]))
                    st.wait()
                    io = bc(iota[:, 0:E].unsqueeze(1), (P, TPC, E))
                    st.did(dve.tensor_tensor(v["oh"][:, ts, :], io, bc(v["idf"][:, ts, 0:1], (P, TPC, E)), ALU.is_equal))
                    st.did(dve.tensor_tensor(v["oh2"][:, ts, :], io, bc(v["idf"][:, ts, 1:2], (P, TPC, E)), ALU.is_equal))
                    st.wait()
                    st.did(dve.tensor_tensor(v["ohb"][:, ts, :], v["oh"][:, ts, :], v["oh2"][:, ts, :], ALU.add))
                    for t in range(TPC * c, TPC * (c + 1)):
                        st.wait()
                        st.did(dve.tensor_tensor(v["ohs"][:, t + 1, :], v["ohs"][:, t, :], v["ohb"][:, t, :], ALU.add))
                st.wait()
                dve.sem_inc(oh_made, 1)
                if L == 2:
                    tile_slots(p, v)
                if L == 2:
                    st.did(dve.tensor_tensor(r[:, 0, :], v["top"][:, :, 1], v["top"][:, :, 0], ALU.subtract))
                    st.wait()
                    dve.sem_inc(ex_ready, 1)
                    dve.wait_ge(ex_made, 1)
                    st.did(dve.tensor_scalar(r[:, 2, :], r[:, 1, :], 1.0, None, ALU.add))
                    st.wait()
                    st.did(dve.reciprocal(r[:, 3, :], r[:, 2, :]))
                    st.wait()
                    st.did(dve.tensor_tensor(r[:, 4, :], r[:, 1, :], r[:, 3, :], ALU.mult))
                    g0, g1 = r[:, 3, :], r[:, 4, :]
                else:
                    st.did(dve.tensor_tensor(r[:, 2, :], v["top"][:, :, 0], v["top"][:, :, 1], ALU.add))
                    st.wait()
                    st.did(dve.tensor_scalar(r[:, 3, :], r[:, 2, :], 1e-9, None, ALU.add))
                    st.wait()
                    st.did(dve.reciprocal(r[:, 4, :], r[:, 3, :]))
                    st.wait()
                    st.did(dve.tensor_tensor(r[:, 5, :], v["top"][:, :, 0], r[:, 4, :], ALU.mult))
                    st.did(dve.tensor_tensor(r[:, 6, :], v["top"][:, :, 1], r[:, 4, :], ALU.mult))
                    g0, g1 = r[:, 5, :], r[:, 6, :]
                st.wait()
                if L == 3:
                    routed(p, v, gate, g0, g1)
                    return
                for k, g in enumerate((g0, g1)):
                    st.did(dve.tensor_scalar(v["wk"][:, :, k], g, gate, None, ALU.mult))
                st.did(dve.tensor_tensor(v["oh"][:], v["oh"][:], bc(g0.unsqueeze(2), (P, NT, E)), ALU.mult))
                st.did(dve.tensor_tensor(v["oh2"][:], v["oh2"][:], bc(g1.unsqueeze(2), (P, NT, E)), ALU.mult))
                st.wait()
                st.did(dve.tensor_tensor(v["G"][:], v["oh"][:], v["oh2"][:], ALU.add))
                st.wait()
                st.did(dve.tensor_scalar(v["G"][:], v["G"][:], gate, None, ALU.mult))
                st.wait()
                dve.sem_inc(g_made, 1)
                dve.wait_ge(ln_y, lnorm(p, NC - 1))
                for c in range(NC):
                    for q in range(2):
                        bk = RB.get(dve, p, "b2", c, q)
                        a = X[:, (2 * c + q) * 2:(2 * c + q) * 2 + 2, :]
                        dve.tensor_tensor(a, a, bk[:].rearrange("p (t d) -> p t d", t=2), ALU.add).then_inc(RB.read, 1)
                dve.wait_ge(RB.read, RB.emptied)
                for i in range(NTL):
                    e = dve.value_load(v["et"][0:1, i:i + 1], min_val=0, max_val=E2 - 1)
                    bk = RB.get(dve, p, "up", i)
                    dve.tensor_tensor(v["h"][:, i % 2, :], bk[:], v["b1"][:, bass.ds(e * H2, H2)], ALU.add).then_inc(RB.read, 1)
                for c in range(NC):
                    combine(v, 1, c)
                st.wait()
                over(p)

            def tile_slots(p, v):
                E = E2
                bk = RB.get(dve, p, "pos")
                st.did(dve.tensor_scalar(v["til"][:], bk[:, NT * E:(NT + 1) * E], P / 2 - 0.5, 1.0 / P, ALU.add, ALU.mult))
                st.did(dve.memset(v["base"][:, 0:1], 0.0))
                st.wait()
                st.did(dve.tensor_scalar(v["til"][:], v["til"][:], ROUND, ROUND, ALU.add, ALU.subtract))
                for e in range(1, E):
                    st.wait()
                    st.did(dve.tensor_tensor(v["base"][:, e:e + 1], v["base"][:, e - 1:e], v["til"][:, e - 1:e], ALU.add))
                st.wait()
                st.did(dve.tensor_scalar(v["cnt"][:], v["base"][:], float(P), None, ALU.mult))
                st.did(dve.tensor_tensor(v["cmp"][:], bc(iota[:].unsqueeze(2), (P, NTL, E - 1)),
                                         bc(v["base"][:, 1:E].unsqueeze(1), (P, NTL, E - 1)), ALU.is_ge))
                st.wait()
                st.did(dve.tensor_tensor(v["pre"][:], bk[:, 0:NT * E].rearrange("p (t e) -> p t e", e=E),
                                         bc(v["cnt"][:].unsqueeze(1), (P, NT, E)), ALU.add))
                st.wait()
                dve.sem_inc(RB.read, 1)
                for k, oh in enumerate(("oh", "oh2")):
                    st.did(dve.tensor_tensor(v["G"][:] if k == 0 else v["lg"][:], v[oh][:], v["pre"][:], ALU.mult))
                st.wait()
                for k, a in enumerate(("G", "lg")):
                    st.did(dve.tensor_reduce(v["pk"][:, :, k], v[a][:], AX.X, ALU.add))
                st.wait()
                st.did(dve.tensor_copy(v["sidx"][:], v["pk"][:].rearrange("p t k -> p (t k)")))
                st.wait()
                dve.sem_inc(idx_made, 1)
                st.did(dve.tensor_reduce(v["etf"][:], v["cmp"][:], AX.X, ALU.add))
                st.wait()
                st.did(dve.tensor_copy(v["et"][:], v["etf"][:]))
                st.wait()
                dve.sem_inc(et_made, 1)

            def combine(v, n, c):
                for t in range(TPC * c, TPC * (c + 1)):
                    if t % 2 == 0:
                        dve.wait_ge(gathered[t // 2], 16 * 4 * n)
                    for k in range(2):
                        src = (v["Y"] if k == 0 else v["yk"])[:, t, :]
                        st.did(dve.scalar_tensor_tensor(X[:, t, :], src, v["wk"][:, t, k:k + 1], X[:, t, :], ALU.mult, ALU.add))
                        st.wait()
                if n == 2:
                    dve.sem_inc(x_out, 1)

            def expert_out(p, e, c, gate_of):
                for q in range(2):
                    bk = RB.get(dve, p, "dn", e, c, q)
                    for i in range(2):
                        t = (2 * c + q) * 2 + i
                        ins = dve.scalar_tensor_tensor(X[:, t, :], bk[:, i * D:(i + 1) * D], gate_of(t), X[:, t, :],
                                                       ALU.mult, ALU.add)
                    ins.then_inc(RB.read, 1)

            def routed(p, v, gate, g0, g1):
                bk = RB.get(dve, p, "pos")
                st.did(dve.tensor_copy(v["pre"][:], bk[:, 0:NT * E3].rearrange("p (t e) -> p t e", e=E3)))
                st.wait()
                dve.sem_inc(RB.read, 1)
                for k, (oh, g) in enumerate((("oh", g0), ("oh2", g1))):
                    st.did(dve.tensor_tensor(v[oh][:], v[oh][:], v["pre"][:], ALU.mult))
                    st.wait()
                    st.did(dve.tensor_reduce(v["pk"][:, :, k], v[oh][:], AX.X, ALU.add))
                    st.wait()
                    st.did(dve.tensor_scalar(v["wk"][:, :, k], v["pk"][:, :, k], float(CAP), gate, ALU.is_lt, ALU.mult))
                    st.wait()
                    st.did(dve.tensor_tensor(v["wk"][:, :, k], v["wk"][:, :, k], g, ALU.mult))
                st.did(dve.tensor_scalar(v["slot"][:], v["pk"][:], float(CAP), None, ALU.is_lt))
                st.did(dve.tensor_scalar(v["row"][:], v["pk"][:], float(CAP - 1), None, ALU.min))
                st.wait()
                st.did(dve.scalar_tensor_tensor(v["row"][:], v["idf"][:, :, 0:2], float(CAP), v["row"][:], ALU.mult, ALU.add))
                st.wait()
                dve.wait_ge(dumps_made, 1)
                st.did(dve.tensor_tensor(v["pk"][:], v["row"][:], v["dump"][:], ALU.subtract))
                st.wait()
                st.did(dve.tensor_tensor(v["pk"][:], v["pk"][:], v["slot"][:], ALU.mult))
                st.wait()
                st.did(dve.tensor_tensor(v["pk"][:], v["pk"][:], v["dump"][:], ALU.add))
                st.wait()
                st.did(dve.tensor_copy(v["sidx"][:], v["pk"][:].rearrange("p t k -> p (t k)")))
                st.did(dve.tensor_copy(v["gidx"][:], v["row"][:].rearrange("p t k -> p (t k)")))
                st.wait()
                dve.sem_inc(idx_made, 1)
                dve.wait_ge(ln_y, lnorm(p, NC - 1))
                st.did(dve.scalar_tensor_tensor(X[:], v["Y"][:], gate, X[:], ALU.mult, ALU.add))
                st.wait()
                n = 0

                def product(e, c, slot, width):
                    nonlocal n
                    for m in range(3):
                        fn = F3T[m]
                        dve.wait_ge(RA.read, RA.n(p, "gate", e, c, m))
                        bk = RB.get(dve, p, "up", e, c, m)
                        dve.tensor_tensor(v["hT"][0:fn, slot * 3 + m, 0:width], v["sg"][0:fn, n % 4, 0:width],
                                          bk[0:fn, 0:width], ALU.mult).then_inc(RB.read, 1)
                        n += 1

                def shared(half):
                    for what, c in shared_order(half):
                        if what == "down":
                            if half:
                                combine(v, 2, SHARED[0][c % 2])
                            expert_out(p, E3, c, lambda t: gate)
                            continue
                        if half:
                            dve.wait_ge(RC.filled, RC.n(p, "dn", E3 - 2 + c % 2, 1))
                        product(E3, c, c % 2, CH)

                shared(0)
                for e in range(E3):
                    if e >= 2:
                        dve.wait_ge(RC.filled, RC.n(p, "dn", e - 2, 1))
                    product(e, 0, e % 2, CAP)
                shared(1)
                dve.wait_ge(RB.read, RB.emptied)
                for c in SHARED[1]:
                    combine(v, 2, c)

            for p in range(NPH):
                L = p // 2
                if p:
                    dve.wait_ge(phase_over, p)
                if p % 2 == 0:
                    (attention if L == 1 else attention16)(p, L)
                elif L == 0:
                    coupling(p)
                elif L == 1:
                    quantised(p)
                else:
                    experts(p, L)

        @block.sync
        def _(sp):
            def load(p):
                if p >= 2:
                    sp.wait_ge(phase_over, p - 1)
                for dst, src in loads[p]:
                    sp.dma_start(dst, src, allow_slow_non_contiguous=True).then_inc(w_loaded[p], 16)

            x_v = A["x"].rearrange("b (t p) d -> p (b t) d", p=P)
            sp.dma_start(X[:], x_v).then_inc(in_loaded, 16)
            for b in range(B):
                sp.dma_start(ctxN[:, b, :], A["ctx_768"][b, 0:P, :]).then_inc(in_loaded, 16)
                sp.dma_start(ctxN[0:MR, B + b, :], A["ctx_768"][b, P:M, :]).then_inc(in_loaded, 16)
            sp.dma_start(gates[:, 0:4], row(A["g_xattn"], 4)).then_inc(in_loaded, 16)
            sp.dma_start(gates[:, 4:8], row(A["g_ffn"], 4)).then_inc(in_loaded, 16)
            load(0)
            r0 = 16 * NPAIR
            sp.wait_ge(consts, NCONST)
            for i in range(2):
                sp.dma_start(ph[0]["Qs"][r0:r0 + 1, i].rearrange("p h (a n) -> p (h a) n", n=P),
                             bc(onesb[r0:r0 + 1, :].unsqueeze(1), (1, ph[0]["H"] * TPC, P))).then_inc(ones_row, 16)

            def stack_keys(p, L):
                v = ph[p]
                sp.wait_ge(kp_made, LA[L] + 1)
                sp.dma_start(k_parts.rearrange("s (m p) k -> p (s m) k", p=P),
                             v["kp"][:].rearrange("p s m k -> p (s m) k")).then_inc(kp_stored, 16)
                sp.wait_ge(kp_stored, 16 * (LA[L] + 1))
                for i, part in enumerate(K_PART):
                    sp.dma_start(v["Ks"][16 * i:16 * (i + 1), :, :], k_parts[part].rearrange("(h d) k -> d h k", d=16))\
                      .then_inc(k_stacked, 16)

            def stack_queries(p, L, c):
                v = ph[p]
                s = c % 2
                past = [n for n in LA if n < L]
                if c < FIRST[L]:
                    sp.wait_ge(qp0_made, sum(FIRST[n] for n in past) + c + 1)
                else:
                    sp.wait_ge(qp_made, sum(NC - FIRST[n] for n in past) + c + 1 - FIRST[L])
                sp.dma_start(q_parts[c].rearrange("s (m p) q -> p (s m) q", p=P),
                             v["qp"][:, s].rearrange("p s m q -> p (s m) q")).then_inc(qp_stored[s], 16)
                sp.wait_ge(qp_stored[s], 16 * (2 * LA[L] + c // 2 + 1))
                if c >= 2:
                    sp.wait_ge(RC.filled, RC.n(p, "s", c - 2, v["G"] - 1, 4))
                for i, part in enumerate(Q_PART):
                    sp.dma_start(v["Qs"][16 * i:16 * (i + 1), s], q_parts[c, part].rearrange("(h d) q -> d h q", d=16))\
                      .then_inc(q_stacked[s], 16)

            if NPH >= 6:
                sp.wait_ge(zero_made, 1)
                sp.dma_start(x_slots[0:E3 * CAP, :].rearrange("(p n) d -> p n d", p=P),
                             bc(zeros[:].unsqueeze(1), (P, E3 * CAP // P, D))).then_inc(slots_clear, 16)
            for p in range(NPH):
                L = p // 2
                if p % 2 == 0:
                    if L != 1:
                        stack_keys(p, L)
                        for c in range(2):
                            stack_queries(p, L, c)
                    if p + 1 < NPH:
                        load(p + 1)
                    if L != 1:
                        for c in range(2, NC):
                            stack_queries(p, L, c)
                    continue
                if p + 1 < NPH:
                    load(p + 1)
                if L < 2:
                    continue
                v = ph[p]
                sp.wait_ge(phase_over, p)
                pre = f"L{L}_ffn_"
                if L == 2:
                    for e in range(E2):
                        sp.dma_start(v["W1"][:, :, e * H2:(e + 1) * H2], kin(A[pre + "W1"][e])).then_inc(e2_loaded, 16)
                        sp.dma_start(v["W2"][:, :, e * D:(e + 1) * D], A[pre + "W2"][e].rearrange("(m p) n -> p m n", p=P))\
                          .then_inc(e2_loaded, 16)

                    def tile_tokens(i):
                        if i >= NXT:
                            sp.wait_ge(RA.filled, RA.n(p, "in", i - NXT))
                        sp.dma_start(v["xe"][:, i % NXT, :], x_slots[i * P:(i + 1) * P, :]).then_inc(xt_loaded[i % NXT], 16)

                    sp.wait_ge(scattered, 16 * 2 * NT)
                    for i in range(NXT):
                        tile_tokens(i)
                    for i in range(NTL):
                        if i + NXT < NTL:
                            tile_tokens(i + NXT)
                        sp.wait_ge(RC.read, RC.n(p, "down", i))
                        sp.dma_start(y_slots[i * P:(i + 1) * P, :], v["ye"][:, i % 3, :]).then_inc(yt_stored[i % 3], 16)
                    continue

                def expert_weights(i):
                    s, e = i % 3, i - 1
                    if i == 3:
                        sp.wait_ge(RB.filled, RB.n(p, "dn", E3, SHARED[0][1], 1))
                    elif i > 3:
                        sp.wait_ge(RC.filled, RC.n(p, "dn", e - 3, 1))
                    g, u, d = (A[pre + n][e] if 0 <= e < E3 else A[pre + "s" + n] for n in ("w_gate", "w_up", "w_down"))
                    for dst, src in ((v["Wg"][:, s], kin(g)), (v["Wu"][:, s], kin(u)),
                                     (v["Wd"][:, s, 0:2], d[0:2 * P, :].rearrange("(m p) n -> p m n", p=P)),
                                     (v["Wd"][0:F3 - 2 * P, s, 2], d[2 * P:F3, :])):
                        sp.dma_start(dst, src).then_inc(ew_loaded[s], 16)

                def expert_tokens(e):
                    if e >= 3:
                        sp.wait_ge(RA.filled, RA.n(p, "xeT", e - 3, DK - 1))
                    x = x_slots[e * CAP:(e + 1) * CAP, :]
                    sp.dma_start(v["xe"][:, e % 3, 0:2, :], x[0:2 * P, :].rearrange("(t p) d -> p t d", p=P))\
                      .then_inc(xe_loaded[e % 3], 16)
                    sp.dma_start(v["xe"][0:CAP - 2 * P, e % 3, 2, :], x[2 * P:CAP, :]).then_inc(xe_loaded[e % 3], 16)

                for i in range(3):
                    expert_weights(i)
                sp.wait_ge(scattered, 16 * 2 * NT * 2)
                for e in range(3):
                    expert_tokens(e)
                for e in range(E3):
                    if e + 3 <= E3 + 1:
                        expert_weights(e + 3)
                    sp.wait_ge(RC.read, RC.n(p, "dn", e, 1))
                    y = y_slots[e * CAP:(e + 1) * CAP, :]
                    sp.dma_start(y[0:2 * P, :].rearrange("(t p) d -> p t d", p=P), v["ye"][:, e % 3, 0:2, :])\
                      .then_inc(ye_stored[e % 3], 16)
                    sp.dma_start(y[2 * P:CAP, :], v["ye"][0:CAP - 2 * P, e % 3, 2, :]).then_inc(ye_stored[e % 3], 16)
                    if e + 3 < E3:
                        expert_tokens(e + 3)
            o = out.rearrange("b (t p) d -> p (b t) d", p=P)
            for c in range(NC):
                ts = slice(TPC * c, TPC * (c + 1))
                if NPH < 8:
                    sp.wait_ge(phase_over, NPH)
                else:
                    sp.wait_ge(x_out, c + 1)
                sp.dma_start(o[:, ts, :], X[:, ts, :]).then_inc(stored, 16)
            sp.wait_ge(stored, 16 * NC)


def kernel(**inputs):
    import numpy as np
    import concourse.bacc as bacc
    from concourse.bass_utils import run_bass_kernel_spmd

    nc = bacc.Bacc("TRN2", target_bir_lowering=False, num_devices=1)
    arrays, aps = {}, {}
    for name, value in inputs.items():
        a = np.ascontiguousarray(value)
        arrays[f"in_{name}"] = a
        aps[name] = nc.dram_tensor(f"in_{name}", a.shape, mybir.dt.from_np(a.dtype), kind="ExternalInput").ap()
    out = nc.dram_tensor("out_x", (B, S, D), F32, kind="ExternalOutput").ap()
    build(nc, aps, out)
    r = run_bass_kernel_spmd(nc, [arrays], core_ids=[0])
    return r.results[0]["out_x"]
```
